# Optimizing a Trainium2 kernel written in Bass

```python
import numpy as np
import jax
import jax.numpy as jnp

def _softmax(x, axis=-1):
    return jax.nn.softmax(x, axis=axis)

def _gelu(x):
    return jax.nn.gelu(x, approximate=True)

def _silu(x):
    return jax.nn.silu(x)

def _sigmoid(x):
    return jax.nn.sigmoid(x)

def _layernorm(x, axis=-1, eps=1e-05):
    m = jnp.mean(x, axis=axis, keepdims=True)
    v = jnp.var(x, axis=axis, keepdims=True)
    return (x - m) / jnp.sqrt(v + eps)

def _scatter_add(tgt, idx, src, axis=0):
    return tgt.at[idx].add(src)

def _segment_sum(src, seg, n):
    return jax.ops.segment_sum(src, seg, n)
kernel_name = 'mk_vit_tower_d1_tok_img768_r4_3ce28e'

def setup_inputs(seed: int=0):
    np.random.seed(seed)
    _w = jnp.asarray

    def _rec_inputs():
        import jax
        import jax.numpy as jnp
        _rk = jax.random.key(seed)
        x = -0.000348323 + 0.999952 * jax.random.normal(jax.random.fold_in(_rk, 1), (64, 3, 64, 64), jnp.float32)
        return x
    x = _rec_inputs()

    def _L0_tok_setup():
        import jax, jax.numpy as jnp
        import numpy as np
        PATCH = 16

        def _shifted_concat(x):
            B, C, H, W = x.shape
            xp = jnp.pad(x, ((0, 0), (0, 0), (1, 1), (1, 1)))
            right = xp[:, :, 1:1 + H, 0:W]
            left = xp[:, :, 1:1 + H, 2:2 + W]
            down = xp[:, :, 0:H, 1:1 + W]
            up = xp[:, :, 2:2 + H, 1:1 + W]
            return jnp.concatenate([x, right, left, down, up], axis=1)

        def _patchify(x, p):
            B, C, H, W = x.shape
            h, w = (H // p, W // p)
            x = x.reshape(B, C, h, p, w, p)
            x = x.transpose(0, 2, 4, 3, 5, 1)
            return x.reshape(B, h * w, p * p * C)

        def _layernorm(x, gamma, beta, eps=1e-05):
            mu = jnp.mean(x, axis=-1, keepdims=True)
            var = jnp.var(x, axis=-1, keepdims=True)
            return (x - mu) * jax.lax.rsqrt(var + eps) * gamma + beta
        key = jax.random.key(seed)
        k1, k2 = jax.random.split(key)
        B, H, W = (32, 96, 96)
        patch_dim = PATCH * PATCH * 15
        d_hidn = 192
        x = jax.random.normal(k1, (B, 3, H, W), dtype=jnp.float32)
        gamma = jnp.ones((patch_dim,), dtype=jnp.float32)
        beta = jnp.zeros((patch_dim,), dtype=jnp.float32)
        W_ = jax.random.normal(k2, (patch_dim, d_hidn), dtype=jnp.float32) * patch_dim ** (-0.5)
        b = jnp.zeros((d_hidn,), dtype=jnp.float32)
        return {'x': x, 'gamma': gamma, 'beta': beta, 'W': W_, 'b': b}
    _L0_tok_all = _L0_tok_setup()
    _L0_tok_in = {k: v for k, v in _L0_tok_all.items() if k in ('gamma', 'beta', 'W', 'b')}
    del _L0_tok_all

    def _L0_attn_setup():
        import jax, jax.numpy as jnp
        import numpy as np
        DIM = 192
        GP_NUM = 49
        key = jax.random.key(seed)
        ks = jax.random.split(key, 7)
        b, n, d = (8, 512, DIM)
        s = d ** (-0.5)
        x = jax.random.normal(ks[0], (b, n, d), dtype=jnp.float32)
        W_qkv = jax.random.normal(ks[1], (d, 3 * d), dtype=jnp.float32) * s
        b_qkv = jnp.zeros((3 * d,), dtype=jnp.float32)
        W_proj = jax.random.normal(ks[2], (d, d), dtype=jnp.float32) * s
        b_proj = jnp.zeros((d,), dtype=jnp.float32)
        W_gp = jax.random.normal(ks[3], (d, GP_NUM), dtype=jnp.float32) * s
        alpha = jax.random.normal(ks[4], (), dtype=jnp.float32)
        return {'x': x, 'W_qkv': W_qkv, 'b_qkv': b_qkv, 'W_proj': W_proj, 'b_proj': b_proj, 'W_gp': W_gp, 'alpha': alpha}
    _L0_attn_all = _L0_attn_setup()
    _L0_attn_in = {k: v for k, v in _L0_attn_all.items() if k in ('W_qkv', 'b_qkv', 'W_proj', 'b_proj', 'W_gp', 'alpha')}
    del _L0_attn_all

    def _L0_ffn_setup():
        import jax, jax.numpy as jnp
        import numpy as np
        B, N, D, E, F, K = (2, 512, 192, 8, 768, 2)
        V_MAX = 3.0
        FEAT_CLAMP = 10.0

        def bk_green_diag(a):
            aT = jnp.swapaxes(a, 0, 1)

            def step(c, ai):
                d = ai - 1.0 / c
                return (d, d)
            d0 = aT[0]
            _, d_rest = jax.lax.scan(step, d0, aT[1:])
            d = jnp.concatenate([d0[None], d_rest], axis=0)
            eN = aT[-1]
            _, e_rest = jax.lax.scan(step, eN, aT[:-1], reverse=True)
            e = jnp.concatenate([e_rest, eN[None]], axis=0)
            G = 1.0 / (d + e - aT)
            return jnp.swapaxes(G, 0, 1)
        key = jax.random.key(seed)
        ks = jax.random.split(key, 8)
        s = lambda k, shape, sc: jax.random.normal(k, shape, jnp.float32) * sc
        return {'x': s(ks[0], (B, N, D), 1.0), 'v_w': s(ks[1], (D,), 0.02), 'v_b': jnp.zeros((), jnp.float32), 'gate_w': s(ks[2], (D, E), 0.02), 'gate_b': jnp.zeros((E,), jnp.float32), 'w1': s(ks[3], (E, D, F), 0.02), 'b1': jnp.zeros((E, F), jnp.float32), 'w2': s(ks[4], (E, F, D), 0.02), 'b2': jnp.zeros((E, D), jnp.float32), 'out_w': s(ks[5], (2, D), 0.02), 'out_b': jnp.zeros((D,), jnp.float32), 'bk_scale': jnp.ones((D,), jnp.float32)}
    _L0_ffn_all = _L0_ffn_setup()
    _L0_ffn_in = {k: v for k, v in _L0_ffn_all.items() if k in ('v_w', 'v_b', 'gate_w', 'gate_b', 'w1', 'b1', 'w2', 'b2', 'out_w', 'out_b', 'bk_scale')}
    del _L0_ffn_all
    return {'x': x, 'L0_tok_gamma': _L0_tok_in['gamma'], 'L0_tok_beta': _L0_tok_in['beta'], 'L0_tok_W': _L0_tok_in['W'], 'L0_tok_b': _L0_tok_in['b'], 'L0_attn_W_qkv': _L0_attn_in['W_qkv'], 'L0_attn_b_qkv': _L0_attn_in['b_qkv'], 'L0_attn_W_proj': _L0_attn_in['W_proj'], 'L0_attn_b_proj': _L0_attn_in['b_proj'], 'L0_attn_W_gp': _L0_attn_in['W_gp'], 'L0_attn_alpha': _L0_attn_in['alpha'], 'L0_ffn_v_w': _L0_ffn_in['v_w'], 'L0_ffn_v_b': _L0_ffn_in['v_b'], 'L0_ffn_gate_w': _L0_ffn_in['gate_w'], 'L0_ffn_gate_b': _L0_ffn_in['gate_b'], 'L0_ffn_w1': _L0_ffn_in['w1'], 'L0_ffn_b1': _L0_ffn_in['b1'], 'L0_ffn_w2': _L0_ffn_in['w2'], 'L0_ffn_b2': _L0_ffn_in['b2'], 'L0_ffn_out_w': _L0_ffn_in['out_w'], 'L0_ffn_out_b': _L0_ffn_in['out_b'], 'L0_ffn_bk_scale': _L0_ffn_in['bk_scale']}

def reference(x, L0_tok_gamma, L0_tok_beta, L0_tok_W, L0_tok_b, L0_attn_W_qkv, L0_attn_b_qkv, L0_attn_W_proj, L0_attn_b_proj, L0_attn_W_gp, L0_attn_alpha, L0_ffn_v_w, L0_ffn_v_b, L0_ffn_gate_w, L0_ffn_gate_b, L0_ffn_w1, L0_ffn_b1, L0_ffn_w2, L0_ffn_b2, L0_ffn_out_w, L0_ffn_out_b, L0_ffn_bk_scale):
    import jax
    import jax.numpy as jnp

    def _L0_tok_ref(x, gamma, beta, W, b):
        import jax, jax.numpy as jnp
        import numpy as np
        PATCH = 16

        def _shifted_concat(x):
            B, C, H, W = x.shape
            xp = jnp.pad(x, ((0, 0), (0, 0), (1, 1), (1, 1)))
            right = xp[:, :, 1:1 + H, 0:W]
            left = xp[:, :, 1:1 + H, 2:2 + W]
            down = xp[:, :, 0:H, 1:1 + W]
            up = xp[:, :, 2:2 + H, 1:1 + W]
            return jnp.concatenate([x, right, left, down, up], axis=1)

        def _patchify(x, p):
            B, C, H, W = x.shape
            h, w = (H // p, W // p)
            x = x.reshape(B, C, h, p, w, p)
            x = x.transpose(0, 2, 4, 3, 5, 1)
            return x.reshape(B, h * w, p * p * C)

        def _layernorm(x, gamma, beta, eps=1e-05):
            mu = jnp.mean(x, axis=-1, keepdims=True)
            var = jnp.var(x, axis=-1, keepdims=True)
            return (x - mu) * jax.lax.rsqrt(var + eps) * gamma + beta
        xs = _shifted_concat(x)
        tokens = _patchify(xs, PATCH)
        normed = _layernorm(tokens, gamma, beta)
        return jnp.einsum('bnd,de->bne', normed, W) + b

    def _L0_attn_ref(x, W_qkv, b_qkv, W_proj, b_proj, W_gp, alpha):
        import jax, jax.numpy as jnp
        import numpy as np
        DIM = 192
        GP_NUM = 49
        d = x.shape[-1]
        scale = d ** (-0.5)
        qkv = x @ W_qkv + b_qkv
        q, k, v = jnp.split(qkv, 3, axis=-1)
        attn_scores = jnp.einsum('bnd,bmd->bnm', q, k) * scale
        gw = jax.nn.softmax(jax.nn.gelu(v @ W_gp, approximate=False), axis=-1)
        group_weight = jnp.einsum('bng,bmg->bnm', gw, gw)
        attn_scores = jax.nn.softmax(attn_scores * group_weight, axis=-1)
        a = jax.nn.sigmoid(alpha)
        attn_weights = (1.0 - a) * attn_scores + a * group_weight
        out = jnp.einsum('bnm,bmd->bnd', attn_weights, v)
        return out @ W_proj + b_proj

    def _L0_ffn_ref(x, v_w, v_b, gate_w, gate_b, w1, b1, w2, b2, out_w, out_b, bk_scale):
        import jax, jax.numpy as jnp
        import numpy as np
        B, N, D, E, F, K = (2, 512, 192, 8, 768, 2)
        V_MAX = 3.0
        FEAT_CLAMP = 10.0

        def bk_green_diag(a):
            aT = jnp.swapaxes(a, 0, 1)

            def step(c, ai):
                d = ai - 1.0 / c
                return (d, d)
            d0 = aT[0]
            _, d_rest = jax.lax.scan(step, d0, aT[1:])
            d = jnp.concatenate([d0[None], d_rest], axis=0)
            eN = aT[-1]
            _, e_rest = jax.lax.scan(step, eN, aT[:-1], reverse=True)
            e = jnp.concatenate([e_rest, eN[None]], axis=0)
            G = 1.0 / (d + e - aT)
            return jnp.swapaxes(G, 0, 1)
        v = jnp.clip(x @ v_w + v_b, -V_MAX, V_MAX)
        a = (-2.0 + v).astype(jnp.complex64) - 1j
        G = bk_green_diag(a)
        feats = jnp.stack([G.real, G.imag], axis=-1)
        logits = x @ gate_w + gate_b
        probs = jax.nn.softmax(logits, axis=-1)
        topv, topi = jax.lax.top_k(probs, K)
        topv = topv / jnp.sum(topv, axis=-1, keepdims=True)
        comb = jnp.sum(topv[..., None] * jax.nn.one_hot(topi, E, dtype=x.dtype), axis=2)
        h = jax.nn.gelu(jnp.einsum('bnd,edf->bnef', x, w1) + b1)
        y = jnp.einsum('bnef,efd->bned', h, w2) + b2
        ffn_out = jnp.einsum('bne,bned->bnd', comb, y)
        feats_c = jnp.clip(feats, -FEAT_CLAMP, FEAT_CLAMP)
        spec_out = feats_c @ out_w + out_b
        return ffn_out + bk_scale * spec_out
    h = _L0_tok_ref(x, L0_tok_gamma, L0_tok_beta, L0_tok_W, L0_tok_b)
    h = h + _L0_attn_ref(_layernorm(h, axis=-1), L0_attn_W_qkv, L0_attn_b_qkv, L0_attn_W_proj, L0_attn_b_proj, L0_attn_W_gp, L0_attn_alpha)
    h = h + _L0_ffn_ref(_layernorm(h, axis=-1), L0_ffn_v_w, L0_ffn_v_b, L0_ffn_gate_w, L0_ffn_gate_b, L0_ffn_w1, L0_ffn_b1, L0_ffn_w2, L0_ffn_b2, L0_ffn_out_w, L0_ffn_out_b, L0_ffn_bk_scale)
    return h

_drawn_inputs = setup_inputs


def setup_inputs(seed=0):
    import zlib

    import numpy as np

    out = dict(_drawn_inputs(seed))
    spreads = {'L0_tok_gamma': (1.0, 0.2),
     'L0_tok_beta': (0.0, 0.1),
     'L0_tok_b': (0.0, 0.1),
     'L0_attn_b_qkv': (0.0, 0.1),
     'L0_attn_b_proj': (0.0, 0.1),
     'L0_ffn_gate_b': (0.0, 0.1),
     'L0_ffn_b1': (0.0, 0.364),
     'L0_ffn_b2': (0.0, 0.1),
     'L0_ffn_out_b': (0.0, 0.1),
     'L0_ffn_bk_scale': (1.0, 0.6)}
    factors = {'L0_attn_W_gp': 7.787, 'L0_ffn_v_w': 8.0, 'L0_ffn_out_w': 5.126}
    for name, (base, spread) in spreads.items():
        noise = np.random.default_rng([zlib.crc32(name.encode()), seed]).standard_normal(out[name].shape)
        drawn = base * np.exp(spread * noise) if base else spread * noise
        out[name] = jnp.asarray(drawn.astype(out[name].dtype))
    for name, factor in factors.items():
        out[name] = (out[name] * factor).astype(out[name].dtype)
    return out
```

```python
from contextlib import ExitStack

import concourse.bass as bass
from concourse import mybir

F32 = mybir.dt.float32
BF16 = mybir.dt.bfloat16
I32 = mybir.dt.int32
U32 = mybir.dt.uint32
ACT = mybir.ActivationFunctionType
ALU = mybir.AluOpType
AX = mybir.AxisListType

P = 128
IMAGES, PLACES, D = 64, 16, 192
TOKENS = IMAGES * PLACES
TILES = TOKENS // P
HALF = TILES // 2
HT = HALF * P
LO = 128
HI = D - LO
SHIFTS = 5
FEATURES = 3840
CHUNKS = 8
INNER = 6
EDGE = 96
CROWS = [P] * INNER + [EDGE] * 2
GROUPS = 49
VG = D + GROUPS
E, F = 8, 768
FC = F // P
FH = F // 2
TOP = 2
BLOCKS = (TOP * TOKENS - E) // P + E
BCOLS = BLOCKS + 1
FAR = 2 * TOP * TOKENS
EPS = 1e-5
SCALE = float(D) ** -0.5

C_ID, C_DIAG, C_TRI, C_ONE = 0, 128, 256, 384
C_MULT = 512
C_EXP = C_MULT + CHUNKS
C_THR = C_EXP + E
C_RESET = C_THR + E
C_BLK = C_RESET + E * TILES
C_BLK128 = C_BLK + BCOLS
C_TILE = C_BLK128 + BCOLS
C_PART = C_TILE + TOP * TILES
C_OFF = C_PART + 1
C_ALL = C_OFF + P


def tower(nc, pixels, mult_w, edge_w, gammas_betas, tok_b, wqkv, wpg, b_proj, alpha, gate, w1, w2, b2, spec_w, bk,
          consts, out):
    hn2_rows = nc.dram_tensor("hn2_rows", (TOKENS, D), F32, kind="Internal").ap()
    y_rows = nc.dram_tensor("y_rows", (TOP * TOKENS, D), F32, kind="Internal").ap()

    with ExitStack() as ctx:
        def sb(name, shape, dt=F32):
            return ctx.enter_context(nc.sbuf_tensor(name, shape, dt))

        def sem(name):
            return ctx.enter_context(nc.semaphore(name))

        bank = [ctx.enter_context(nc.psum_tensor(f"bank{i}", [P, 512], F32)) for i in range(5, 8)]
        psT = ctx.enter_context(nc.psum_tensor("psT", [P, 4, 512], F32))
        psE = ctx.enter_context(nc.psum_tensor("psE", [P, 512], F32))
        b0, b1, b2k, b3 = (psT[:, i, :] for i in range(4))
        b4 = psE[:, :]
        b5, b6, b7 = (t[:, :] for t in bank)

        cst = sb("cst", [P, C_ALL])
        X = sb("X", [P, CHUNKS, TOKENS])
        sizes = [2 * TOKENS, 2 * SHIFTS * D, 2 * D, CHUNKS * (D + 1), SHIFTS * D, SHIFTS * D, TILES * D]
        early = sb("early", [P, max(sum(sizes), E * FC * D)])
        starts = [sum(sizes[:i]) for i in range(len(sizes) + 1)]
        part = [early[:, starts[i]:starts[i + 1]] for i in range(len(sizes))]
        Xsq = part[0].rearrange("p (a n) -> p a n", a=2)
        Wt = part[1].rearrange("p (a s n) -> p a s n", a=2, s=SHIFTS)
        We = part[2].rearrange("p (a n) -> p a n", a=2)[0:EDGE]
        weff = part[3].rearrange("p (a n) -> p a n", a=CHUNKS)
        bprod = part[4].rearrange("p (a n) -> p a n", a=SHIFTS)
        bacc = part[5].rearrange("p (a n) -> p a n", a=SHIFTS)
        ttmp = part[6].rearrange("p (a n) -> p a n", a=TILES)
        w2s = early[:, 0:E * FC * D].rearrange("p (a n) -> p a n", n=D)
        gb = sb("gb", [P, 2, CHUNKS, SHIFTS])
        gam, bet = gb[:, 0], gb[:, 1]
        tokb = sb("tokb", [P, D])
        g_sb = sb("g_sb", [P, D])
        bw_sb = sb("bw_sb", [P, D])
        st = sb("st", [P, 12, TILES])
        h = sb("h", [P, TILES, D])
        hb = sb("hb", [P, TILES, D])
        hn = sb("hn", [P, TILES, D])
        bn6 = sb("bn6", [P, TILES, 6])
        mv = sb("mv", [P, TILES, 2])
        rstd = sb("rstd", [P, TILES])
        var = sb("var", [P, TILES])
        sd = sb("sd", [P, TILES])
        hnTa = sb("hnTa", [P, TOKENS])
        hnTb = sb("hnTb", [HI + 1, TOKENS])
        wqa = sb("wqa", [P, 3 * D])
        wqb = sb("wqb", [HI + 1, 3 * D])
        wpa = sb("wpa", [P, VG])
        wpb = sb("wpb", [HI, VG])
        wvTa = sb("wvTa", [P, D + 1])
        wvTb = sb("wvTb", [HI, D + 1])
        wga = sb("wga", [P, VG])
        wgb = sb("wgb", [HI + 1, VG])
        bpr = sb("bpr", [P, D])
        qk = sb("qk", [P, 4, TOKENS])
        q0, k0, q1, k1 = qk[:, 0], qk[:, 1], qk[0:HI, 2], qk[0:HI, 3]
        hg = qk[:, 0, 0:F]
        hT = qk[:, 1, 0:F].rearrange("p (c n) -> p c n", n=P)
        combT = qk[0:E, 2]
        vp = sb("vp", [P, TILES, D])
        gw = sb("gw", [P, TILES, GROUPS])
        gred = sb("gred", [P, 3, TILES])
        gwT = sb("gwT", [GROUPS, TOKENS])
        maps = sb("maps", [P, 4, TILES, P])
        gwm, tt, Aw, AT = (maps[:, i] for i in range(4))
        ct = sb("ct", [P, TILES, PLACES])
        cred = sb("cred", [P, 3, TILES])
        sig = sb("sig", [P, 5])
        wgate = sb("wgate", [P, E + 1])
        wgateb = sb("wgateb", [HI + 1, E + 1])
        vcl = sb("vcl", [P, TILES])
        vT = sb("vT", [TILES, P])
        lg = sb("lg", [P, TILES, E])
        gate_st = sb("gate_st", [P, 3, TILES])
        pr = sb("pr", [P, TILES, E])
        m8 = sb("m8", [P, TILES, 8])
        i8 = sb("i8", [P, TILES, 8], U32)
        cw = sb("cw", [P, TOP, TILES])
        idxf = sb("idxf", [P, TOP, TILES])
        oh = sb("oh", [P, TOP, TILES, E])
        ohp = sb("ohp", [P, TOP, TILES, E])
        M = sb("M", [P, TILES, E])
        incl = sb("incl", [P, E, TILES])
        rank = sb("rank", [P, E, TILES])
        gt = sb("gt", [P, E, E])
        blk = sb("blk", [P, 3, E])
        slot = sb("slot", [P, E, TILES])
        slots = sb("slots", [P, 3, TOP * TILES])
        sloti = sb("sloti", [P, 2, TOP * TILES], I32)
        gidr = sb("gidr", [P, BCOLS], I32)
        offb = sb("offb", [P, P], BF16)
        offs = sb("offs", [P, TOP * TILES], BF16)
        ohoff = sb("ohoff", [P, TOP * TILES, P], BF16)
        ohblk = sb("ohblk", [P, TOP * TILES, BCOLS])
        tabr = sb("tabr", [P, TOP * TILES, 2, BCOLS], BF16)
        tab = sb("tab", [P, 5, BCOLS])
        gid = sb("gid", [P, BCOLS], I32)
        sid = sb("sid", [P, BCOLS], I32)
        cur = sb("cur", [P, 2], I32)
        emt = sb("emt", [1, BCOLS, E])
        emtf = sb("emtf", [1, BCOLS])
        emap = sb("emap", [1, BCOLS], I32)
        nblk = sb("nblk", [1, 2], I32)
        comb = sb("comb", [P, TILES, E])
        combt = sb("combt", [P, TOP, TILES, E])
        b2s = sb("b2s", [E, D])
        sw = sb("sw", [3, D])
        bks = sb("bks", [3, D])
        feat = sb("feat", [3, TOKENS])
        v2 = sb("v2", [P, PLACES])
        v2r = sb("v2r", [P, PLACES])
        add = sb("add", [P, PLACES, 2])
        ch = sb("ch", [P, PLACES, 2])
        chj = sb("chj", [P, PLACES, 2])
        chd = sb("chd", [P, 2, PLACES])
        back = sb("back", [IMAGES, PLACES, 2])
        z = sb("z", [IMAGES, 2, PLACES])
        zz = sb("zz", [IMAGES, 4, PLACES])
        w1a = sb("w1a", [P, E, F])
        w1b = X[0:HI + 1, 0:E * F // TOKENS, :].rearrange("p a b -> p (a b)").rearrange("p (e f) -> p e f", e=E)
        xg = sb("xg", [P, D])
        xgTa = sb("xgTa", [P, P])
        xgTb = sb("xgTb", [HI + 1, P])
        ysb = sb("ysb", [P, D])
        yb = maps[:, :, :, :].rearrange("p a t n -> p (a t n)")[:, 0:TOP * TILES * D].rearrange(
            "p (j t d) -> p j t d", j=TOP, t=TILES)

        vg = psT[:, 2:4, :].rearrange("p a (b n) -> p a b n", b=2)
        ident = cst[:, C_ID:C_ID + P]
        diag = cst[:, C_DIAG:C_DIAG + P]
        ones = cst[:, C_ONE:C_ONE + P]
        half = [slice(0, HALF), slice(HALF, TILES)]
        cols = [slice(0, HT), slice(HT, TOKENS)]

        names = """s_cst s_gb s_tokb s_qkv s_wp s_bpr s_alpha s_gate s_b2 s_sw s_w1a s_w1b s_w2 s_bk
            v_weff a_sq v_chain p_chain p_prod p_acc pe_w t_sum t_bias v_bias v_h v_hn p_hb pe_hT a_hT pe_qk av_qk a_q v_qk pe_vg a_vp a_gelu
            v_gsub a_gexp v_gw pe_gwT a_gwT pe_wvT a_wvT pe_wg a_wg
            pe_s pe_gw v_csub a_cexp v_A pe_AT a_AT pe_o v_h1 v_hn2 d_hn2 pe_h2T a_h2T pe_gate v_v pe_vT a_vT d_v
            v_lsub a_lexp v_M pe_rank v_tabr pe_tab v_tab v_emap p_ones a_sig v_sig v_comb pe_combT v_feat d_feat v_sw
            a_combT d_gather pe_xT a_xgT pe_up0 pe_up1 a_ge pe_hgT v_hgT pe_y v_y d_scatter pe_base v_base
            d_yb0 d_yb1 d_yb2 d_yb3 v_out d_out p_gidx p_sidx p_pass v_var a_sd""".split()
        S = {n: sem(n) for n in dict.fromkeys(names)}
        d_x = [sem(f"d_x{c}") for c in range(CHUNKS)]
        d_w = [sem(f"d_w{c}") for c in range(CHUNKS)]
        block = ctx.enter_context(nc.Block())

        @block.sync
        def _(sp):
            sp.dma_start(cst[:, :], consts).then_inc(S["s_cst"], 16)
            sp.dma_start(gb[:, :, :, :], gammas_betas).then_inc(S["s_gb"], 16)
            for c in range(CHUNKS):
                k = CROWS[c]
                if c < INNER:
                    if c >= 2:
                        sp.wait_ge(S["v_weff"], c - 1)
                        sp.wait_ge(S["p_prod"], c - 1)
                    sp.dma_start(Wt[:, c % 2, :, :], mult_w[c]).then_inc(d_w[c], 16)
                else:
                    sp.dma_start(We[:, c - INNER, :], edge_w[c - INNER]).then_inc(d_w[c], 16)
                sp.dma_start(X[0:k, c, :], pixels[c, 0:k, :]).then_inc(d_x[c], 16)
            sp.dma_start(tokb[:, :], tok_b.partition_broadcast(P)).then_inc(S["s_tokb"], 16)
            sp.dma_start(wqa[:, :], wqkv[0:LO]).then_inc(S["s_qkv"], 16)
            sp.dma_start(wqb[:, :], wqkv[LO:]).then_inc(S["s_qkv"], 16)
            sp.dma_start(wpa[:, :], wpg[0:LO]).then_inc(S["s_wp"], 16)
            sp.dma_start(wpb[:, :], wpg[LO:]).then_inc(S["s_wp"], 16)
            sp.dma_start(bpr[:, :], b_proj.partition_broadcast(P)).then_inc(S["s_bpr"], 16)
            sp.dma_start(sig[:, 0:1], alpha.partition_broadcast(P)).then_inc(S["s_alpha"], 16)
            sp.dma_start(wgate[:, :], gate[0:LO]).then_inc(S["s_gate"], 16)
            sp.dma_start(wgateb[:, :], gate[LO:]).then_inc(S["s_gate"], 16)
            sp.dma_start(b2s[:, :], b2).then_inc(S["s_b2"], 16)
            sp.dma_start(sw[:, :], spec_w).then_inc(S["s_sw"], 16)
            sp.dma_start(bks[:, :], bk.partition_broadcast(3)).then_inc(S["s_bk"], 16)
            sp.dma_start(w1a[:, :, :], w1[:, 0:LO, :].rearrange("e p f -> p e f")).then_inc(S["s_w1a"], 16)
            sp.wait_ge(S["pe_w"], CHUNKS)
            sp.dma_start(w1b, w1[:, LO:, :].rearrange("e p f -> p e f")).then_inc(S["s_w1b"], 16)
            sp.wait_ge(S["v_h"], 2)
            sp.wait_ge(S["t_bias"], 1)
            sp.dma_start(w2s[:, :, :], w2.rearrange("e (c p) d -> p (e c) d", p=P)).then_inc(S["s_w2"], 16)
            for f in range(2):
                sp.wait_ge(S["v_hn2"], f + 1)
                sp.dma_start(hn2_rows[f * HT:(f + 1) * HT].rearrange("(t p) d -> p t d", p=P),
                             hn[:, half[f], :]).then_inc(S["d_hn2"], 16)
            sp.wait_ge(S["a_vT"], 1)
            for d in range(2):
                sp.dma_start(v2[d * IMAGES:(d + 1) * IMAGES, :],
                             vT[:, :].rearrange("t (b n) -> t b n", n=PLACES)).then_inc(S["d_v"], 16)
            sp.wait_ge(S["v_feat"], 1)
            for r in range(2):
                sp.dma_start(feat[r:r + 1, :].rearrange("r (b n) -> r b n", n=PLACES),
                             z[:, r, :]).then_inc(S["d_feat"], 16)
            sp.wait_ge(S["p_acc"], CHUNKS + 1)
            for q in range(4):
                sp.dma_start(yb[:, 0, 2 * q:2 * q + 2, :],
                             y_rows[2 * q * P:(2 * q + 2) * P].rearrange("(t p) d -> p t d", p=P)
                             ).then_inc(S[f"d_yb{q}"], 16)
                sp.dma_start(yb[:, 1, 2 * q:2 * q + 2, :],
                             y_rows[TOKENS + 2 * q * P:TOKENS + (2 * q + 2) * P].rearrange("(t p) d -> p t d", p=P)
                             ).then_inc(S[f"d_yb{q}"], 16)
            for q in range(4):
                sp.wait_ge(S["v_out"], 2 * q + 2)
                sp.dma_start(out[2 * q * P:(2 * q + 2) * P].rearrange("(t p) d -> p t d", p=P),
                             hb[:, 2 * q:2 * q + 2, :]).then_inc(S["d_out"], 16)
            sp.wait_ge(S["d_out"], 64)

        @block.gpsimd
        def _(pool):
            pool.memset(hnTb[HI:HI + 1, :], 1.0).then_inc(S["p_ones"], 1)
            pool.memset(xgTb[HI:HI + 1, :], 1.0).then_inc(S["p_ones"], 1)
            pool.memset(feat[:, :], 1.0).then_inc(S["p_ones"], 1)
            pool.wait_ge(S["p_ones"], 3)
            pool.wait_ge(S["s_gb"], 16)
            for c in range(CHUNKS):
                pool.wait_ge(d_w[c], 16)
                if c < INNER:
                    dst = bacc if c == 0 else bprod
                    if c >= 2:
                        pool.wait_ge(S["p_acc"], c)
                    pool.tensor_tensor(dst[:, :, :], Wt[:, c % 2, :, :],
                                       bet[:, c, :].unsqueeze(2).broadcast_to([P, SHIFTS, D]),
                                       ALU.mult).then_inc(S["p_prod"], 1)
                    pool.wait_ge(S["p_prod"], c + 1)
                    if c > 0:
                        pool.tensor_tensor(bacc[:, :, :], bacc[:, :, :], bprod[:, :, :],
                                           ALU.add).then_inc(S["p_acc"], 1)
                    else:
                        pool.sem_inc(S["p_acc"], 1)
                else:
                    pool.wait_ge(S["p_acc"], c)
                    pool.tensor_tensor(bprod[0:EDGE, 0, :], We[:, c - INNER, :],
                                       bet[0:EDGE, c, 0:1].broadcast_to([EDGE, D]),
                                       ALU.mult).then_inc(S["p_prod"], 1)
                    pool.wait_ge(S["p_prod"], c + 1)
                    pool.tensor_tensor(bacc[0:EDGE, 0, :], bacc[0:EDGE, 0, :], bprod[0:EDGE, 0, :],
                                       ALU.add).then_inc(S["p_acc"], 1)
            pool.wait_ge(S["s_bpr"], 16)
            for f in range(2):
                pool.wait_ge(S["v_h"], f + 1)
                pool.tensor_tensor(hb[:, half[f], :], h[:, half[f], :],
                                   bpr[:, :].unsqueeze(1).broadcast_to([P, HALF, D]),
                                   ALU.add).then_inc(S["p_hb"], 1)
            pool.wait_ge(S["v_tab"], 1)
            pool.wait_ge(S["v_emap"], 1)
            pool.wait_ge(S["d_hn2"], 32)
            m = pool.value_load(nblk[0:1, 1:2], min_val=TOP * TOKENS // P - 2, max_val=BLOCKS - 2)

            last_row = pool.to_reg(TOP * TOKENS - 1)

            def gather(b):
                pool.tensor_copy(cur[:, 0:1], gid[:, bass.ds(b, 1)]).then_inc(S["p_gidx"], 1)
                pool.wait_ge(S["p_gidx"], b + 1)
                pool.sem_inc(S["p_pass"], 1)
                pool.indirect_dma_start(xg[:, :], None, hn2_rows,
                                        bass.IndirectOffsetOnAxis(cur[:, 0:1], 0)
                                        ).then_inc(S["d_gather"], 16)

            def scatter(b):
                pool.wait_ge(S["v_y"], b + 1)
                pool.sem_inc(S["p_pass"], 1)
                pool.tensor_copy(cur[:, 1:2], sid[:, bass.ds(b, 1)]).then_inc(S["p_sidx"], 1)
                pool.wait_ge(S["p_sidx"], b + 1)
                pool.sem_inc(S["p_pass"], 1)
                pool.indirect_dma_start(y_rows, bass.IndirectOffsetOnAxis(cur[:, 1:2], 0), ysb[:, :], None,
                                        bounds_check=last_row, oob_is_err=False
                                        ).then_inc(S["d_scatter"], 16)

            gather(0)
            for b in range(1, 3):
                pool.wait_ge(S["pe_xT"], b)
                gather(b)
            with pool.Fori(0, m) as i:
                pool.wait_ge(S["pe_xT"], i + 3)
                pool.sem_inc(S["p_pass"], 1)
                gather(i + 3)
                scatter(i)
            scatter(m)
            scatter(m + 1)
            pool.wait_ge(S["d_scatter"], m * 16 + 32)
            pool.sem_inc(S["p_acc"], 1)

        @block.scalar
        def _(act):
            for c in range(CHUNKS):
                act.wait_ge(d_x[c], 16)
                if c >= 2:
                    act.wait_ge(S["pe_w"], c - 1)
                k = CROWS[c]
                act.activation(Xsq[0:k, c % 2, :], X[0:k, c, :], ACT.Square).then_inc(S["a_sq"], 1)
            act.wait_ge(S["v_var"], 1)
            act.activation(st[:, 6, :], st[:, 5, :], ACT.Sqrt).then_inc(S["a_sd"], 1)

            def deviation(f, turn):
                act.wait_ge(S["v_var"], turn)
                act.activation(sd[:, half[f]], var[:, half[f]], ACT.Sqrt).then_inc(S["a_sd"], 1)

            act.wait_ge(S["pe_wvT"], 1)
            act.activation(wvTa[:, :], b7[:, 0:D + 1], ACT.Copy).then_inc(S["a_wvT"], 1)
            act.activation(wvTb[:, :], b7[0:HI, 256:256 + D + 1], ACT.Copy).then_inc(S["a_wvT"], 1)
            act.wait_ge(S["pe_wg"], 1)
            act.activation(wga[:, :], b7[:, 0:VG], ACT.Copy).then_inc(S["a_wg"], 1)
            act.activation(wgb[:, :], b7[0:HI + 1, 256:256 + VG], ACT.Copy).then_inc(S["a_wg"], 1)
            deviation(0, 2)
            deviation(1, 3)
            for f in range(2):
                act.wait_ge(S["pe_hT"], f + 1)
                act.activation(hnTa[:, cols[f]], b7, ACT.Copy).then_inc(S["a_hT"], 1)
                act.activation(hnTb[0:HI, cols[f]], b6[0:HI, :], ACT.Copy).then_inc(S["a_hT"], 1)
                act.wait_ge(S["pe_qk"], 3 * f + 1)
                act.activation(q0[:, cols[f]], b0, ACT.Copy).then_inc(S["a_q"], 1)
                act.wait_ge(S["pe_qk"], 3 * f + 2)
                act.activation(k0[:, cols[f]], b1, ACT.Copy).then_inc(S["a_q"], 1)
                act.wait_ge(S["pe_vg"], f + 1)
                act.activation(gw[:, half[f], :].rearrange("p (a b) g -> p a b g", b=2), vg[:, :, :, D:VG],
                               ACT.Gelu).then_inc(S["a_gelu"], 1)
                act.activation(vp[:, half[f], :].rearrange("p (a b) g -> p a b g", b=2), vg[:, :, :, 0:D],
                               ACT.Copy).then_inc(S["a_vp"], 1)
                act.wait_ge(S["v_gsub"], f + 1)
                act.activation(gw[:, half[f], :], gw[:, half[f], :], ACT.Exp).then_inc(S["a_gexp"], 1)
            act.wait_ge(S["s_alpha"], 16)
            act.activation(sig[:, 1:2], sig[:, 0:1], ACT.Exp, scale=-1.0).then_inc(S["a_sig"], 1)
            for f in range(2):
                act.wait_ge(S["pe_gwT"], f + 1)
                act.activation(gwT[:, cols[f]], b5[0:GROUPS, :], ACT.Copy).then_inc(S["a_gwT"], 1)
                act.wait_ge(S["v_csub"], f + 1)
                act.activation(ct[:, half[f], :], ct[:, half[f], :], ACT.Exp).then_inc(S["a_cexp"], 1)
                act.wait_ge(S["pe_AT"], f + 1)
                act.activation(AT[:, half[f], :].rearrange("p t n -> p (t n)"), b0, ACT.Copy).then_inc(S["a_AT"], 1)
            deviation(0, 4)
            deviation(1, 5)
            for f in range(2):
                act.wait_ge(S["pe_h2T"], f + 1)
                act.activation(hnTa[:, cols[f]], b7, ACT.Copy).then_inc(S["a_h2T"], 1)
                act.activation(hnTb[0:HI, cols[f]], b6[0:HI, :], ACT.Copy).then_inc(S["a_h2T"], 1)
            act.wait_ge(S["v_lsub"], 1)
            act.activation(pr[:, :, :], lg[:, :, :], ACT.Exp).then_inc(S["a_lexp"], 1)
            act.wait_ge(S["pe_vT"], 1)
            act.activation(vT[:, :], b4[0:TILES, 0:P], ACT.Copy).then_inc(S["a_vT"], 1)
            for f in range(2):
                act.wait_ge(S["pe_combT"], f + 1)
                act.activation(combT[:, cols[f]], (b5, b6)[f][0:E, :], ACT.Copy).then_inc(S["a_combT"], 1)
            act.wait_ge(S["v_emap"], 1)
            n = act.value_load(nblk[0:1, 0:1], min_val=TOP * TOKENS // P, max_val=BLOCKS)

            def take_x():
                act.activation(xgTa[:, :], b7[:, 0:P], ACT.Copy).then_inc(S["a_xgT"], 1)
                act.activation(xgTb[0:HI, :], b7[0:HI, P:2 * P], ACT.Copy).then_inc(S["a_xgT"], 1)

            def gelu(part):
                act.activation(hg[:, part * FH:(part + 1) * FH], (b0, b1)[part][:, 0:FH],
                               ACT.Gelu_apprx_tanh).then_inc(S["a_ge"], 1)

            act.wait_ge(S["pe_xT"], 1)
            act.wait_ge(S["p_ones"], 3)
            take_x()
            act.wait_ge(S["pe_up0"], 1)
            gelu(0)
            act.wait_ge(S["pe_up1"], 1)
            gelu(1)
            act.wait_ge(S["pe_xT"], 2)
            take_x()
            with act.Fori(1, n) as i:
                act.wait_ge(S["pe_up0"], i + 1)
                act.wait_ge(S["pe_hgT"], i * 2)
                gelu(0)
                act.wait_ge(S["pe_up1"], i + 1)
                gelu(1)
                act.wait_ge(S["pe_xT"], i + 2)
                take_x()

        @block.vector
        def _(dve):
            count = [0]

            def link(ins):
                count[0] += 1
                ins.then_inc(S["v_chain"], 1)
                dve.wait_ge(S["v_chain"], count[0])

            dve.wait_ge(S["s_cst"], 16)
            dve.tensor_copy(weff[:, :, D:D + 1], cst[:, C_MULT:C_MULT + CHUNKS].unsqueeze(2))
            dve.tensor_copy(offb[:, :], cst[:, C_OFF:C_OFF + P])
            dve.wait_ge(S["s_gb"], 16)
            for c in range(CHUNKS):
                dve.wait_ge(d_w[c], 16)
                if c < INNER:
                    link(dve.tensor_scalar(weff[:, c, 0:D], Wt[:, c % 2, 0, :], gam[:, c, 0:1], None, ALU.mult))
                    for s in range(1, SHIFTS):
                        ins = dve.scalar_tensor_tensor(weff[:, c, 0:D], Wt[:, c % 2, s, :], gam[:, c, s:s + 1],
                                                       weff[:, c, 0:D], ALU.mult, ALU.add)
                        if s < SHIFTS - 1:
                            link(ins)
                    ins.then_inc(S["v_weff"], 1)
                else:
                    dve.tensor_scalar(weff[0:EDGE, c, 0:D], We[:, c - INNER, :], gam[0:EDGE, c, 0:1], None,
                                      ALU.mult).then_inc(S["v_weff"], 1)
            dve.wait_ge(S["s_sw"], 16)
            dve.wait_ge(S["s_bk"], 16)
            dve.tensor_tensor(sw[:, :], sw[:, :], bks[:, :], ALU.mult).then_inc(S["v_sw"], 1)
            dve.wait_ge(S["t_sum"], 1)
            tview = psT[:, :, :].rearrange("p a (b n) -> p a b n", b=2)
            tv = [tview[:, t // 2, t % 2, :] for t in range(TILES)]
            link(dve.tensor_scalar(st[:, 0, :].rearrange("p (a b) -> p a b", b=2), tview[:, :, :, D], -1.0 / FEATURES,
                                   None, ALU.mult))
            link(dve.tensor_tensor(st[:, 1, :], st[:, 0, :], st[:, 0, :], ALU.mult))
            link(dve.scalar_tensor_tensor(st[:, 2, :], b4[:, 0:TILES], 1.0 / FEATURES, st[:, 1, :],
                                          ALU.mult, ALU.subtract))
            dve.tensor_scalar(st[:, 5, :], st[:, 2, :], EPS, None, ALU.add).then_inc(S["v_var"], 1)
            dve.wait_ge(S["a_sd"], 1)
            link(dve.reciprocal(st[:, 3, :], st[:, 6, :]))
            link(dve.tensor_tensor(st[:, 4, :], st[:, 0, :], st[:, 3, :], ALU.mult))
            dve.wait_ge(S["t_bias"], 1)
            dve.wait_ge(S["s_tokb"], 16)
            dve.tensor_copy(g_sb[:, :], b5[:, 0:D])
            link(dve.tensor_tensor(bw_sb[:, :], b6[:, 0:D], tokb[:, :], ALU.add))
            for t in range(TILES):
                ins = dve.scalar_tensor_tensor(ttmp[:, t, :], g_sb[:, :], st[:, 4, t:t + 1], bw_sb[:, :],
                                               ALU.mult, ALU.add)
            link(ins)
            for t in range(TILES):
                ins = dve.scalar_tensor_tensor(h[:, t, :], tv[t][:, 0:D], st[:, 3, t:t + 1], ttmp[:, t, :],
                                               ALU.mult, ALU.add)
                if t % HALF == HALF - 1:
                    ins.then_inc(S["v_h"], 1)

            def norm(src, f, done, turn):
                for t in range(f * HALF, (f + 1) * HALF):
                    ins = dve.bn_stats(bn6[:, t, :], src[:, t, :])
                link(ins)
                for t in range(f * HALF, (f + 1) * HALF):
                    ins = dve.bn_aggr(mv[:, t, :], bn6[:, t, :])
                link(ins)
                dve.tensor_scalar(var[:, half[f]], mv[:, half[f], 1], EPS, None, ALU.add).then_inc(S["v_var"], 1)
                dve.wait_ge(S["a_sd"], turn)
                link(dve.reciprocal(rstd[:, half[f]], sd[:, half[f]]))
                for t in range(f * HALF, (f + 1) * HALF):
                    ins = dve.tensor_scalar(hn[:, t, :], src[:, t, :], mv[:, t, 0:1], rstd[:, t:t + 1],
                                            ALU.subtract, ALU.mult)
                ins.then_inc(S[done], 1)

            for f in range(2):
                dve.wait_ge(S["v_h"], f + 1)
                norm(h, f, "v_hn", f + 2)
            for f in range(2):
                dve.wait_ge(S["pe_qk"], 3 * f + 3)
                dve.tensor_copy(q1[:, cols[f]], b5[0:HI, :])
                dve.tensor_copy(k1[:, cols[f]], b5[HI:P, :]).then_inc(S["v_qk"], 1)
                dve.wait_ge(S["a_gelu"], f + 1)
                g = gw[:, half[f], :]
                link(dve.tensor_reduce(gred[:, 0, half[f]], g, AX.X, ALU.max))
                dve.tensor_tensor(g, g, gred[:, 0, half[f]].unsqueeze(2).broadcast_to([P, HALF, GROUPS]),
                                  ALU.subtract).then_inc(S["v_gsub"], 1)
                dve.wait_ge(S["a_gexp"], f + 1)
                link(dve.tensor_reduce(gred[:, 1, half[f]], g, AX.X, ALU.add))
                link(dve.reciprocal(gred[:, 2, half[f]], gred[:, 1, half[f]]))
                dve.tensor_tensor(g, g, gred[:, 2, half[f]].unsqueeze(2).broadcast_to([P, HALF, GROUPS]),
                                  ALU.mult).then_inc(S["v_gw"], 1)
            dve.wait_ge(S["a_sig"], 1)
            link(dve.tensor_scalar(sig[:, 2:3], sig[:, 1:2], 1.0, None, ALU.add))
            link(dve.reciprocal(sig[:, 3:4], sig[:, 2:3]))
            link(dve.tensor_tensor(sig[:, 4:5], sig[:, 1:2], sig[:, 3:4], ALU.mult))
            for f in range(2):
                dg = diag.unsqueeze(1).broadcast_to([P, HALF, P])
                dve.wait_ge(S["pe_gw"], f + 1)
                link(dve.tensor_tensor(gwm[:, half[f], :], b6.rearrange("p (t n) -> p t n", n=P), dg, ALU.mult))
                link(dve.scalar_tensor_tensor(tt[:, half[f], :], b7.rearrange("p (t n) -> p t n", n=P), SCALE,
                                              gwm[:, half[f], :], ALU.mult, ALU.mult))
                c = ct[:, half[f], :]
                link(dve.tensor_reduce(c, tt[:, half[f], :].rearrange("p t (b n) -> p t n b", n=PLACES), AX.X,
                                       ALU.add))
                link(dve.tensor_reduce(cred[:, 0, half[f]], c, AX.X, ALU.max))
                dve.tensor_tensor(c, c, cred[:, 0, half[f]].unsqueeze(2).broadcast_to([P, HALF, PLACES]),
                                  ALU.subtract).then_inc(S["v_csub"], 1)
                dve.wait_ge(S["a_cexp"], f + 1)
                link(dve.tensor_reduce(cred[:, 1, half[f]], c, AX.X, ALU.add))
                link(dve.reciprocal(cred[:, 2, half[f]], cred[:, 1, half[f]]))
                link(dve.tensor_scalar(cred[:, 2, half[f]], cred[:, 2, half[f]], sig[:, 4:5], None, ALU.mult))
                link(dve.tensor_tensor(c, c, cred[:, 2, half[f]].unsqueeze(2).broadcast_to([P, HALF, PLACES]),
                                       ALU.mult))
                for t in range(f * HALF, (f + 1) * HALF):
                    ins = dve.tensor_tensor(Aw[:, t, :].rearrange("p (b n) -> p b n", n=PLACES),
                                            ct[:, t, :].unsqueeze(1).broadcast_to([P, P // PLACES, PLACES]),
                                            diag.rearrange("p (b n) -> p b n", n=PLACES), ALU.mult)
                link(ins)
                dve.scalar_tensor_tensor(Aw[:, half[f], :], gwm[:, half[f], :], sig[:, 3:4], Aw[:, half[f], :],
                                         ALU.mult, ALU.add).then_inc(S["v_A"], 1)
            for f in range(2):
                dve.wait_ge(S["pe_o"], f + 1)
                dve.wait_ge(S["p_hb"], f + 1)
                hv = hb[:, half[f], :].rearrange("p (a b) d -> p a b d", b=2)
                ov = psT[:, 1:3, :].rearrange("p a (b n) -> p a b n", b=2)[:, :, :, 0:D]
                link(dve.tensor_tensor(hv, ov, hv, ALU.add))
                dve.sem_inc(S["v_h1"], 1)
                norm(hb, f, "v_hn2", f + 4)
            dve.wait_ge(S["pe_gate"], 2)
            gv = b5[:, 0:TILES * 16].rearrange("p (t n) -> p t n", n=16)
            dve.tensor_scalar(vcl[:, :], gv[:, :, E], -3.0, 3.0, ALU.max, ALU.min).then_inc(S["v_v"], 1)
            link(dve.tensor_reduce(gate_st[:, 0, :], gv[:, :, 0:E], AX.X, ALU.max))
            dve.tensor_tensor(lg[:, :, :], gv[:, :, 0:E], gate_st[:, 0, :].unsqueeze(2).broadcast_to([P, TILES, E]),
                              ALU.subtract).then_inc(S["v_lsub"], 1)
            dve.wait_ge(S["a_lexp"], 1)
            link(dve.tensor_reduce(gate_st[:, 1, :], pr[:, :, :], AX.X, ALU.add))
            link(dve.reciprocal(gate_st[:, 2, :], gate_st[:, 1, :]))
            link(dve.tensor_tensor(pr[:, :, :], pr[:, :, :],
                                   gate_st[:, 2, :].unsqueeze(2).broadcast_to([P, TILES, E]), ALU.mult))
            for t in range(TILES):
                ins = dve.max(m8[:, t, :], pr[:, t, :])
            link(ins)
            for t in range(TILES):
                ins = dve.max_index(i8[:, t, :], m8[:, t, :], pr[:, t, :])
            link(ins)
            link(dve.tensor_copy(idxf[:, :, :], i8[:, :, 0:TOP].rearrange("p t j -> p j t")))
            link(dve.tensor_tensor(oh[:, :, :, :].rearrange("p j t e -> p (j t) e"),
                                   idxf[:, :, :].rearrange("p j t -> p (j t)").unsqueeze(2).broadcast_to(
                                       [P, TOP * TILES, E]),
                                   cst[:, C_EXP:C_EXP + E].unsqueeze(1).broadcast_to([P, TOP * TILES, E]),
                                   ALU.is_equal))
            dve.tensor_tensor(M[:, :, :], oh[:, 0], oh[:, 1], ALU.add).then_inc(S["v_M"], 1)
            link(dve.tensor_tensor(gate_st[:, 0, :], m8[:, :, 0], m8[:, :, 1], ALU.add))
            link(dve.reciprocal(gate_st[:, 1, :], gate_st[:, 0, :]))
            link(dve.tensor_tensor(cw[:, :, :], m8[:, :, 0:TOP].rearrange("p t j -> p j t"),
                                   gate_st[:, 1, :].unsqueeze(1).broadcast_to([P, TOP, TILES]), ALU.mult))
            dve.wait_ge(S["pe_rank"], 1)
            tot = b3[:, 0:E * TILES]
            pre = b3[:, 256:256 + E * TILES]
            fl = lambda a: a.rearrange("p e t -> p (e t)")
            link(dve.tensor_tensor_scan(fl(incl[:, :, :]), cst[:, C_RESET:C_RESET + E * TILES], tot, 0.0,
                                        ALU.mult, ALU.add))
            link(dve.tensor_tensor(fl(rank[:, :, :]), fl(incl[:, :, :]), tot, ALU.subtract))
            dve.tensor_tensor(fl(rank[:, :, :]), fl(rank[:, :, :]), pre, ALU.add)
            link(dve.tensor_tensor(gt[:, :, :], incl[:, :, TILES - 1:TILES].broadcast_to([P, E, E]),
                                   cst[:, C_THR:C_THR + E].unsqueeze(1).broadcast_to([P, E, E]), ALU.is_gt))
            link(dve.tensor_reduce(blk[:, 0, :], gt[:, :, :], AX.X, ALU.add))
            link(dve.tensor_tensor_scan(blk[:, 1, :], ones[:, 0:E], blk[:, 0, :], 0.0, ALU.mult, ALU.add))
            link(dve.tensor_tensor(blk[:, 2, :], blk[:, 1, :], blk[:, 0, :], ALU.subtract))
            link(dve.scalar_tensor_tensor(slot[:, :, :], blk[:, 2, :].unsqueeze(2).broadcast_to([P, E, TILES]),
                                          float(P), rank[:, :, :], ALU.mult, ALU.add))
            for j in range(TOP):
                ins = dve.tensor_tensor(ohp[:, j], oh[:, j], slot[:, :, :].rearrange("p e t -> p t e"), ALU.mult)
            link(ins)
            link(dve.tensor_reduce(slots[:, 0, :], ohp[:, :, :, :].rearrange("p j t e -> p (j t) e"), AX.X, ALU.add))
            link(dve.tensor_copy(sloti[:, 0, :], slots[:, 0, :]))
            link(dve.tensor_scalar(sloti[:, 1, :], sloti[:, 0, :], P - 1, None, ALU.bitwise_and))
            link(dve.tensor_copy(slots[:, 1, :], sloti[:, 1, :]))
            dve.tensor_copy(offs[:, :], slots[:, 1, :])
            link(dve.tensor_tensor(slots[:, 2, :], slots[:, 0, :], slots[:, 1, :], ALU.subtract))
            JT = TOP * TILES
            dve.tensor_tensor(ohoff[:, :, :], offs[:, :].unsqueeze(2).broadcast_to([P, JT, P]),
                              offb[:, :].unsqueeze(1).broadcast_to([P, JT, P]), ALU.is_equal)
            link(dve.tensor_tensor(ohblk[:, :, :], slots[:, 2, :].unsqueeze(2).broadcast_to([P, JT, BCOLS]),
                                   cst[:, C_BLK128:C_BLK128 + BCOLS].unsqueeze(1).broadcast_to([P, JT, BCOLS]),
                                   ALU.is_equal))
            dve.tensor_scalar(tabr[:, :, 0, :], ohblk[:, :, :], cst[:, C_PART:C_PART + 1], None, ALU.mult)
            dve.tensor_tensor(tabr[:, :, 1, :], ohblk[:, :, :],
                              cst[:, C_TILE:C_TILE + JT].unsqueeze(2).broadcast_to([P, JT, BCOLS]),
                              ALU.mult).then_inc(S["v_tabr"], 1)
            link(dve.tensor_tensor(emt[:, :, :], cst[0:1, C_BLK:C_BLK + BCOLS].unsqueeze(2).broadcast_to([1, BCOLS, E]),
                                   blk[0:1, 1, :].unsqueeze(1).broadcast_to([1, BCOLS, E]), ALU.is_ge))
            dve.tensor_reduce(emtf[:, :], emt[:, :, :], AX.X, ALU.add)
            dve.tensor_scalar(nblk[:, 1:2], blk[0:1, 1, E - 1:E], -2.0, None, ALU.add)
            link(dve.tensor_copy(nblk[:, 0:1], blk[0:1, 1, E - 1:E]))
            dve.tensor_copy(emap[:, :], emtf[:, :]).then_inc(S["v_emap"], 1)
            dve.wait_ge(S["pe_tab"], 1)
            link(dve.tensor_copy(tab[:, 0:2, :].rearrange("p a b -> p (a b)"), b2k[:, 0:2 * BCOLS]))
            dve.tensor_scalar(tab[:, 3, :], tab[:, 0, :], 0.0, float(FAR), ALU.is_equal, ALU.mult)
            link(dve.scalar_tensor_tensor(tab[:, 2, :], tab[:, 1, :], float(P), tab[:, 0, :], ALU.mult, ALU.add))
            dve.scalar_tensor_tensor(sid[:, :], tab[:, 2, :], -1.0, tab[:, 3, :], ALU.add, ALU.add)
            link(dve.tensor_scalar(gidr[:, :], tab[:, 2, :], -1.0, 0.0, ALU.add, ALU.max))
            dve.tensor_scalar(gid[:, :], gidr[:, :], TOKENS - 1, None, ALU.bitwise_and).then_inc(S["v_tab"], 1)
            for j in range(TOP):
                ins = dve.tensor_tensor(combt[:, j], oh[:, j], cw[:, j, :].unsqueeze(2).broadcast_to([P, TILES, E]),
                                        ALU.mult)
            link(ins)
            dve.tensor_tensor(comb[:, :, :], combt[:, 0], combt[:, 1], ALU.add).then_inc(S["v_comb"], 1)
            dve.wait_ge(S["d_v"], 32)
            link(dve.tensor_scalar(v2r[0:IMAGES, :], v2[0:IMAGES, :], -2.0, None, ALU.add))
            link(dve.tensor_scalar(v2r[IMAGES:P, :], v2[IMAGES:P, ::-1], -2.0, None, ALU.add))
            v4 = v2r[:, :].rearrange("p (a b) -> p a b", b=2)
            a4 = add[:, :, :].rearrange("p (a b) c -> p a b c", b=2)
            dve.tensor_copy(a4[:, :, 0, 0], v4[:, :, 0])
            dve.tensor_scalar(a4[:, :, 1, 0], v4[:, :, 1], -1.0, None, ALU.mult)
            link(dve.memset(add[:, :, 1], -1.0))
            link(dve.tensor_copy(ch[:, 0, :], add[:, 0, :]))
            for n in range(1, PLACES):
                link(dve.tensor_tensor_reduce(chj[:, n, :], ch[:, n - 1, :], ch[:, n - 1, :], 1.0, 0.0, ALU.mult,
                                              ALU.add, chd[:, 0, n:n + 1]))
                link(dve.reciprocal(chd[:, 1, n:n + 1], chd[:, 0, n:n + 1]))
                link(dve.scalar_tensor_tensor(ch[:, n, :], ch[:, n - 1, :], chd[:, 1, n:n + 1], add[:, n, :],
                                              ALU.mult, ALU.add))
            c4 = ch[:, :, :].rearrange("p (a b) c -> p a b c", b=2)
            link(dve.tensor_scalar(c4[:, :, 1, 0], c4[:, :, 1, 0], -1.0, None, ALU.mult))
            link(dve.tensor_copy(back[:, :, :], ch[IMAGES:P, ::-1, :]))
            link(dve.tensor_tensor(zz[:, 0:2, :].rearrange("p c n -> p n c"), ch[0:IMAGES, :, :], back[:, :, :],
                                   ALU.add))
            dve.tensor_tensor(zz[:, 0, :], zz[:, 0, :], v2r[0:IMAGES, :], ALU.subtract)
            link(dve.tensor_scalar(zz[:, 1, :], zz[:, 1, :], 1.0, None, ALU.add))
            link(dve.tensor_tensor(z[:, :, :], zz[:, 0:2, :], zz[:, 0:2, :], ALU.mult))
            link(dve.tensor_tensor(zz[:, 2, :], z[:, 0, :], z[:, 1, :], ALU.add))
            link(dve.reciprocal(zz[:, 3, :], zz[:, 2, :]))
            dve.tensor_tensor(z[:, 0, :], zz[:, 0, :], zz[:, 3, :], ALU.mult)
            link(dve.scalar_tensor_tensor(z[:, 1, :], zz[:, 1, :], -1.0, zz[:, 3, :], ALU.mult, ALU.mult))
            link(dve.tensor_scalar(z[:, :, :], z[:, :, :], -10.0, 10.0, ALU.max, ALU.min))
            dve.sem_inc(S["v_feat"], 1)
            n = dve.value_load(nblk[0:1, 0:1], min_val=TOP * TOKENS // P, max_val=BLOCKS)

            def take(b):
                for part in range(2):
                    dve.wait_ge(S["pe_hgT"], b * 2 + part + 1)
                    dve.tensor_copy(hT[:, 3 * part:3 * part + 3, :].rearrange("p c n -> p (c n)"),
                                    (b2k, b3)[part][:, 0:FH]).then_inc(S["v_hgT"], 1)
                dve.wait_ge(S["pe_y"], b + 1)

            take(0)
            dve.tensor_copy(ysb[:, :], b4[:, 0:D]).then_inc(S["v_y"], 1)
            with dve.Fori(1, n) as i:
                take(i)
                dve.wait_ge(S["d_scatter"], i * 16)
                dve.tensor_copy(ysb[:, :], b4[:, 0:D]).then_inc(S["v_y"], 1)
            for t in range(TILES):
                q = t // 2
                if t % 2 == 0:
                    dve.wait_ge(S["pe_base"], q + 1)
                    pb = (b0, b1, b5, b6)[q].rearrange("p (b n) -> p b n", b=2)[:, :, 0:D]
                    dve.tensor_tensor(hb[:, t:t + 2, :], pb, hb[:, t:t + 2, :], ALU.add).then_inc(S["v_base"], 1)
            for t in range(TILES):
                q = t // 2
                dve.wait_ge(S["v_base"], q + 1)
                if t % 2 == 0:
                    dve.wait_ge(S[f"d_yb{q}"], 32)
                link(dve.scalar_tensor_tensor(hb[:, t, :], yb[:, 0, t, :], cw[:, 0, t:t + 1], hb[:, t, :],
                                              ALU.mult, ALU.add))
                dve.scalar_tensor_tensor(hb[:, t, :], yb[:, 1, t, :], cw[:, 1, t:t + 1], hb[:, t, :],
                                         ALU.mult, ALU.add).then_inc(S["v_out"], 1)

        @block.tensor
        def _(pe):
            tview = psT[:, :, :].rearrange("p a (b n) -> p a b n", b=2)

            def tok(t):
                return slice(t * P, (t + 1) * P)

            pe.wait_ge(S["s_cst"], 16)
            for c in range(CHUNKS):
                k = CROWS[c]
                pe.wait_ge(d_x[c], 16)
                pe.wait_ge(S["v_weff"], c + 1)
                for t in range(TILES):
                    pe.matmul(tview[:, t // 2, t % 2, 0:D + 1], X[0:k, c, tok(t)], weff[0:k, c, :],
                              start=(c == 0 and t % 2 == 0), stop=(c == CHUNKS - 1), skip_group_check=True)
                pe.matmul(b5[:, 0:D], ones[0:k, :], weff[0:k, c, 0:D], start=(c == 0), stop=(c == CHUNKS - 1))
                pe.wait_ge(S["a_sq"], c + 1)
                for t in range(TILES):
                    mm = pe.matmul(b4[:, t:t + 1], Xsq[0:k, c % 2, tok(t)], cst[0:k, C_MULT + c:C_MULT + c + 1],
                                   start=(c == 0 and t == 0), stop=(c == CHUNKS - 1), skip_group_check=True)
                mm.then_inc(S["pe_w"], 1)
            pe.wait_ge(S["pe_w"], CHUNKS)
            pe.sem_inc(S["t_sum"], 1)
            pe.wait_ge(S["p_acc"], CHUNKS)
            for s in range(SHIFTS):
                mm = pe.matmul(b6[:, 0:D], ones, bacc[:, s, :], start=(s == 0), stop=(s == SHIFTS - 1))
            mm.then_inc(S["t_bias"], 1)
            pe.wait_ge(S["s_qkv"], 32)
            V = 2 * D
            pe.transpose(b7[:, 0:LO], wqa[:, V:V + LO], ident)
            pe.transpose(b7[:, LO:D + 1], wqb[:, V:V + LO], ident[0:HI + 1, 0:HI + 1])
            pe.transpose(b7[0:HI, 256:256 + LO], wqa[:, V + LO:V + D], ident)
            pe.transpose(b7[0:HI, 256 + LO:256 + D + 1], wqb[:, V + LO:V + D],
                         ident[0:HI + 1, 0:HI + 1]).then_inc(S["pe_wvT"], 1)
            pe.wait_ge(S["a_wvT"], 2)
            pe.wait_ge(S["s_wp"], 32)
            pe.matmul(b7[:, 0:VG], wvTa[:, 0:LO], wpa[:, :], start=True, stop=False)
            pe.matmul(b7[:, 0:VG], wvTb[:, 0:LO], wpb[:, :], start=False, stop=True)
            pe.matmul(b7[0:HI + 1, 256:256 + VG], wvTa[:, LO:D + 1], wpa[:, :], start=True, stop=False,
                      skip_group_check=True)
            pe.matmul(b7[0:HI + 1, 256:256 + VG], wvTb[:, LO:D + 1], wpb[:, :], start=False, stop=True,
                      skip_group_check=True).then_inc(S["pe_wg"], 1)
            pe.wait_ge(S["a_wg"], 2)
            pe.wait_ge(S["p_ones"], 3)
            for f in range(2):
                pe.wait_ge(S["v_hn"], f + 1)
                if f > 0:
                    pe.wait_ge(S["a_hT"], 2 * f)
                for t in range(HALF):
                    pe.transpose(b7[:, tok(t)], hn[:, f * HALF + t, 0:LO], ident)
                for t in range(HALF):
                    mm = pe.transpose(b6[0:HI, tok(t)], hn[:, f * HALF + t, LO:D], ident)
                mm.then_inc(S["pe_hT"], 1)
                pe.wait_ge(S["a_hT"], 2 * f + 2)
                for r, (dst, a, b) in enumerate(((b0, 0, LO), (b1, LO, 2 * LO))):
                    if f > 0:
                        pe.wait_ge(S["a_q"], r + 1)
                    pe.matmul(dst, wqa[:, a:b], hnTa[:, cols[f]], start=True, stop=False)
                    pe.matmul(dst, wqb[:, a:b], hnTb[:, cols[f]], start=False, stop=True).then_inc(S["pe_qk"], 1)
                if f > 0:
                    pe.wait_ge(S["v_qk"], f)
                pe.matmul(b5, wqa[:, 2 * LO:2 * D], hnTa[:, cols[f]], start=True, stop=False)
                pe.matmul(b5, wqb[:, 2 * LO:2 * D], hnTb[:, cols[f]], start=False, stop=True).then_inc(S["pe_qk"], 1)
                if f > 0:
                    pe.wait_ge(S["a_vp"], f)
                for t in range(HALF):
                    dst = vg[:, t // 2, t % 2, 0:VG]
                    T = f * HALF + t
                    pe.matmul(dst, hnTa[:, tok(T)], wga[:, :], start=True, stop=False)
                    mm = pe.matmul(dst, hnTb[:, tok(T)], wgb[:, :], start=False, stop=True)
                mm.then_inc(S["pe_vg"], 1)
            for f in range(2):
                pe.wait_ge(S["a_q"], 2 * f + 2)
                pe.wait_ge(S["v_qk"], f + 1)
                if f == 0:
                    pe.wait_ge(S["a_hT"], 4)
                else:
                    pe.wait_ge(S["v_csub"], f)
                for t in range(HALF):
                    T = f * HALF + t
                    pe.matmul(b7[:, tok(t)], q0[:, tok(T)], k0[:, tok(T)], start=True, stop=False)
                    pe.matmul(b7[:, tok(t)], q1[:, tok(T)], k1[:, tok(T)], start=False, stop=True)
                pe.wait_ge(S["v_gw"], f + 1)
                if f == 0:
                    pe.wait_ge(S["v_qk"], 2)
                for t in range(HALF):
                    mm = pe.transpose(b5[0:GROUPS, tok(t)], gw[:, f * HALF + t, :], ident)
                mm.then_inc(S["pe_gwT"], 1)
                pe.wait_ge(S["a_gwT"], f + 1)
                for t in range(HALF):
                    T = f * HALF + t
                    mm = pe.matmul(b6[:, tok(t)], gwT[:, tok(T)], gwT[:, tok(T)], start=True, stop=True)
                mm.then_inc(S["pe_gw"], 1)
                pe.wait_ge(S["v_A"], f + 1)
                if f == 0:
                    pe.wait_ge(S["a_q"], 4)
                for t in range(HALF):
                    mm = pe.transpose(b0[:, tok(t)], Aw[:, f * HALF + t, :], ident)
                mm.then_inc(S["pe_AT"], 1)
                pe.wait_ge(S["a_AT"], f + 1)
                pe.wait_ge(S["a_vp"], 2)
                if f > 0:
                    pe.wait_ge(S["v_h1"], f)
                for t in range(HALF):
                    T = f * HALF + t
                    mm = pe.matmul(psT[:, 1:3, :].rearrange("p a (b n) -> p a b n", b=2)[:, t // 2, t % 2, 0:D],
                                   AT[:, T, :], vp[:, T, :], start=True, stop=True)
                mm.then_inc(S["pe_o"], 1)
            pe.wait_ge(S["s_gate"], 32)
            for f in range(2):
                pe.wait_ge(S["v_hn2"], f + 1)
                if f > 0:
                    pe.wait_ge(S["a_h2T"], 2 * f)
                for t in range(HALF):
                    pe.transpose(b7[:, tok(t)], hn[:, f * HALF + t, 0:LO], ident)
                for t in range(HALF):
                    mm = pe.transpose(b6[0:HI, tok(t)], hn[:, f * HALF + t, LO:D], ident)
                mm.then_inc(S["pe_h2T"], 1)
                pe.wait_ge(S["a_h2T"], 2 * f + 2)
                for t in range(HALF):
                    T = f * HALF + t
                    pe.matmul(b5[:, T * 16:T * 16 + E + 1], hnTa[:, tok(T)], wgate[:, :], start=True, stop=False)
                    mm = pe.matmul(b5[:, T * 16:T * 16 + E + 1], hnTb[:, tok(T)], wgateb[:, :], start=False,
                                   stop=True)
                mm.then_inc(S["pe_gate"], 1)
            pe.wait_ge(S["v_v"], 1)
            pe.transpose(b4[0:TILES, 0:P], vcl[:, :], ident).then_inc(S["pe_vT"], 1)
            pe.wait_ge(S["v_M"], 1)
            mo = M[:, :, :].rearrange("p t e -> p e t")
            pe.matmul(b3[:, 0:E * TILES], ones, mo, start=True, stop=True)
            pe.matmul(b3[:, 256:256 + E * TILES], cst[:, C_TRI:C_TRI + P], mo, start=True,
                      stop=True).then_inc(S["pe_rank"], 1)
            pe.wait_ge(S["v_tabr"], 1)
            JT = TOP * TILES
            for r in range(JT):
                mm = pe.matmul(b2k[:, 0:2 * BCOLS], ohoff[:, r, :], tabr[:, r, :, :].rearrange("p a b -> p (a b)"),
                               start=(r == 0), stop=(r == JT - 1))
            mm.then_inc(S["pe_tab"], 1)
            pe.wait_ge(S["v_comb"], 1)
            for f in range(2):
                for t in range(HALF):
                    mm = pe.transpose((b5, b6)[f][0:E, tok(t)], comb[:, f * HALF + t, :], ident)
                mm.then_inc(S["pe_combT"], 1)
            pe.wait_ge(S["s_w1a"], 16)
            pe.wait_ge(S["s_w1b"], 16)
            pe.wait_ge(S["s_w2"], 16)
            pe.wait_ge(S["v_emap"], 1)
            n = pe.value_load(nblk[0:1, 0:1], min_val=TOP * TOKENS // P, max_val=BLOCKS)

            def expert(b):
                return pe.value_load(emap[0:1, bass.ds(b, 1)], min_val=0, max_val=E - 1)

            def turn_x():
                pe.transpose(b7[:, 0:P], xg[:, 0:LO], ident)
                pe.transpose(b7[0:HI, P:2 * P], xg[:, LO:D], ident).then_inc(S["pe_xT"], 1)

            def up(part, e):
                dst = (b0, b1)[part][:, 0:FH]
                fs = slice(part * FH, (part + 1) * FH)
                pe.matmul(dst, xgTa[:, :], w1a[:, bass.ds(e, 1), fs], start=True, stop=False)
                pe.matmul(dst, xgTb[:, :], w1b[:, bass.ds(e, 1), fs], start=False,
                          stop=True).then_inc(S[f"pe_up{part}"], 1)

            def turn_h():
                for c in range(FC):
                    part = c // 3
                    mm = pe.transpose((b2k, b3)[part][:, (c % 3) * P:(c % 3 + 1) * P], hg[:, c * P:(c + 1) * P],
                                      ident)
                    if c % 3 == 2:
                        mm.then_inc(S["pe_hgT"], 1)

            def down(e):
                for c in range(FC):
                    mm = pe.matmul(b4[:, 0:D], hT[:, c, :], w2s[:, bass.ds(e * FC + c, 1), :], start=(c == 0),
                                   stop=(c == FC - 1))
                mm.then_inc(S["pe_y"], 1)

            pe.wait_ge(S["d_gather"], 16)
            pe.wait_ge(S["a_vT"], 1)
            turn_x()
            pe.wait_ge(S["a_xgT"], 2)
            first = expert(0)
            up(0, first)
            up(1, first)
            pe.wait_ge(S["d_gather"], 32)
            turn_x()
            with pe.Fori(1, n) as i:
                e_up = expert(i)
                e_down = expert(i - 1)
                pe.wait_ge(S["a_xgT"], i * 2 + 2)
                pe.wait_ge(S["a_ge"], i * 2)
                up(0, e_up)
                pe.wait_ge(S["v_tab"], 1)
                turn_h()
                up(1, e_up)
                pe.wait_ge(S["d_gather"], i * 16 + 32)
                turn_x()
                pe.wait_ge(S["v_hgT"], i * 2)
                down(e_down)
            pe.wait_ge(S["a_ge"], n * 2)
            turn_h()
            pe.wait_ge(S["v_hgT"], n * 2)
            down(expert(n - 1))
            pe.wait_ge(S["a_combT"], 2)
            pe.wait_ge(S["s_b2"], 16)
            pe.wait_ge(S["v_sw"], 1)
            pe.wait_ge(S["d_feat"], 32)
            for t in range(TILES):
                dst = (b0, b1, b5, b6)[t // 2].rearrange("p (b n) -> p b n", b=2)[:, t % 2, 0:D]
                pe.matmul(dst, combT[:, tok(t)], b2s[:, :], start=True, stop=False)
                mm = pe.matmul(dst, feat[:, tok(t)], sw[:, :], start=False, stop=True)
                if t % 2:
                    mm.then_inc(S["pe_base"], 1)


def constants():
    import numpy as np
    c = np.zeros((P, C_ALL), np.float32)
    p = np.arange(P)
    c[:, C_ID:C_ID + P] = np.eye(P)
    c[:, C_DIAG:C_DIAG + P] = p[:, None] // PLACES == p[None, :] // PLACES
    c[:, C_TRI:C_TRI + P] = p[:, None] < p[None, :]
    c[:, C_ONE:C_ONE + P] = 1
    u = np.arange(16)
    side = (u < 15).astype(np.float32) + (u > 0)
    mult = np.broadcast_to((1 + side[:, None] + side[None, :])[:, :, None], (16, 16, 3)).reshape(INNER, P)
    c[:, C_MULT:C_MULT + INNER] = mult.T
    c[:EDGE, C_MULT + INNER:C_MULT + CHUNKS] = 1
    c[:, C_EXP:C_EXP + E] = np.arange(E)
    c[:, C_THR:C_THR + E] = np.arange(E) * P
    c[:, C_RESET:C_RESET + E * TILES] = np.arange(E * TILES) % TILES != 0
    c[:, C_BLK:C_BLK + BCOLS] = np.arange(BCOLS)
    c[:, C_BLK128:C_BLK128 + BCOLS] = np.arange(BCOLS) * P
    c[:, C_TILE:C_TILE + TOP * TILES] = np.arange(TOP * TILES)
    c[:, C_PART] = p + 1
    c[:, C_OFF:C_OFF + P] = p
    return c


def lay_pixels(x):
    import numpy as np
    x = np.asarray(x)
    padded = np.pad(x, ((0, 0), (0, 0), (1, 1), (1, 1)))
    a = np.zeros((CHUNKS, P, TOKENS), x.dtype)
    a[:INNER] = x.reshape(64, 3, 4, 16, 4, 16).transpose(3, 5, 1, 0, 2, 4).reshape(INNER, P, TOKENS)
    inner = padded[:, :, 1:65, 1:65]
    rows = lambda z: z.reshape(64, 3, 4, 16, 4).transpose(3, 1, 0, 2, 4).reshape(48, TOKENS)
    colm = lambda z: z.reshape(64, 3, 4, 4, 16).transpose(4, 1, 0, 2, 3).reshape(48, TOKENS)
    left = rows(padded[:, :, 1:65, 0:64:16])
    right = rows(padded[:, :, 1:65, 17:66:16])
    above = colm(padded[:, :, 0:64:16, 1:65])
    below = colm(padded[:, :, 17:66:16, 1:65])
    a[INNER, :EDGE] = np.concatenate([left, right])
    a[INNER + 1, :EDGE] = np.concatenate([above, below])
    return a


def lay_rows(w):
    import numpy as np
    w = np.asarray(w)
    w = w.reshape(16, 16, SHIFTS, 3, -1)
    n = w.shape[-1]
    a = np.zeros((16, 16, 3, SHIFTS, n), w.dtype)
    a[:, :, :, 0] = w[:, :, 0]
    a[:, :15, :, 1] = w[:, 1:, 1]
    a[:, 1:, :, 2] = w[:, :15, 2]
    a[:15, :, :, 3] = w[1:, :, 3]
    a[1:, :, :, 4] = w[:15, :, 4]
    edge = np.stack([w[:, 0, 1], w[:, 15, 2], w[0, :, 3], w[15, :, 4]]).reshape(2, EDGE, n)
    return a.reshape(INNER, P, SHIFTS, n), edge


def kernel(**inputs):
    import numpy as _np
    import concourse.bacc as _bacc
    from concourse import mybir as _mybir
    from concourse.bass_utils import run_bass_kernel_spmd as _run

    g = {k: _np.asarray(v) for k, v in inputs.items()}
    w_in, w_edge = lay_rows(g["L0_tok_W"])

    def vec(v):
        a, b = lay_rows(v)
        full = _np.zeros((CHUNKS, P, SHIFTS), v.dtype)
        full[:INNER] = a[..., 0]
        full[INNER:, :EDGE, 0] = b[..., 0]
        return full.transpose(1, 0, 2)

    qkv = _np.concatenate([g["L0_attn_W_qkv"], g["L0_attn_b_qkv"][None]])
    qkv = _np.concatenate([qkv[:, 0:LO], qkv[:, D:D + LO], qkv[:, LO:D], qkv[:, D + LO:]], 1)
    wpg = _np.concatenate([g["L0_attn_W_proj"], g["L0_attn_W_gp"]], 1)
    gate = _np.concatenate([_np.concatenate([g["L0_ffn_gate_w"], g["L0_ffn_v_w"][:, None]], 1),
                            _np.concatenate([g["L0_ffn_gate_b"], g["L0_ffn_v_b"].reshape(1)])[None]])
    w1 = _np.concatenate([g["L0_ffn_w1"], g["L0_ffn_b1"][:, None]], 1)
    spec = _np.concatenate([g["L0_ffn_out_w"], g["L0_ffn_out_b"][None]])
    laid = {
        "pixels": lay_pixels(g["x"]), "mult_w": w_in, "edge_w": w_edge, 
        "gammas_betas": _np.stack([vec(g["L0_tok_gamma"]), vec(g["L0_tok_beta"])], 1), "tok_b": g["L0_tok_b"], "wqkv": qkv, "wpg": wpg,
        "b_proj": g["L0_attn_b_proj"], "alpha": g["L0_attn_alpha"].reshape(1), "gate": gate, "w1": w1,
        "w2": g["L0_ffn_w2"], "b2": g["L0_ffn_b2"], "spec_w": spec, "bk": g["L0_ffn_bk_scale"], "consts": constants(),
    }
    nc = _bacc.Bacc("TRN2", target_bir_lowering=False, num_devices=1)
    arrays, args = {}, []
    for name, a in laid.items():
        a = _np.ascontiguousarray(a)
        arrays[f"in_{name}_dram"] = a
        args.append(nc.dram_tensor(f"in_{name}_dram", a.shape, _mybir.dt.from_np(a.dtype), kind="ExternalInput").ap())
    args.append(nc.dram_tensor("out_0_dram", (TOKENS, D), _mybir.dt.float32, kind="ExternalOutput").ap())
    tower(nc, *args)
    r = _run(nc, [arrays], core_ids=[0])
    return r.results[0]["out_0_dram"].reshape(IMAGES, PLACES, D)
```

```python
from contextlib import ExitStack

import concourse.bass as bass
from concourse import mybir

F32 = mybir.dt.float32
F32R = mybir.dt.float32r
BF16 = mybir.dt.bfloat16
I32 = mybir.dt.int32
U32 = mybir.dt.uint32
ACT = mybir.ActivationFunctionType
ALU = mybir.AluOpType
AX = mybir.AxisListType

P = 128
IMAGES, PLACES, D = 64, 16, 192
TOKENS = IMAGES * PLACES
TILES = TOKENS // P
HALF = TILES // 2
RING = 4
SPLIT = 2
POOL_PAIR = 1
HT = HALF * P
LO = 128
HI = D - LO
SHIFTS = 5
FEATURES = 3840
CHUNKS = 8
INNER = 6
EDGE = 96
CROWS = [P] * INNER + [EDGE] * 2
GROUPS = 49
VG = D + GROUPS
E, F = 8, 768
FC = F // P
FH = F // 2
TOP = 2
BLOCKS = (TOP * TOKENS - E) // P + E
BCOLS = BLOCKS + 1
FAR = 2 * TOP * TOKENS
RAW = 3
BR = 96
EPS = 1e-5
SCALE = float(D) ** -0.5

C_ID, C_DIAG, C_TRI, C_ONE = 0, 128, 256, 384
C_EXP = 512
C_THR = C_EXP + E
C_RESET = C_THR + E
C_BLK = C_RESET + E * TILES
C_BLK128 = C_BLK + BCOLS
C_TILE = C_BLK128 + BCOLS
C_PART = C_TILE + TOP * TILES
C_OFF = C_PART + 1
C_ALL = C_OFF + P


def tower(nc, pixels, mult_w, edge_w, gammas_betas, tok_b, wqkv, wpg, b_proj, alpha, gate, w1, bias1, w2, b2, spec_w, bk,
          consts, out):
    hn2_rows = nc.dram_tensor("hn2_rows", (TOKENS, D), F32, kind="Internal").ap()
    y_rows = nc.dram_tensor("y_rows", (TOP * TOKENS, D), F32, kind="Internal").ap()

    with ExitStack() as ctx:
        def sb(name, shape, dt=F32):
            return ctx.enter_context(nc.sbuf_tensor(name, shape, dt))

        def sem(name):
            return ctx.enter_context(nc.semaphore(name))

        bank = [ctx.enter_context(nc.psum_tensor(f"bank{i}", [P, 512], F32)) for i in range(5, 8)]
        psT = ctx.enter_context(nc.psum_tensor("psT", [P, 4, 512], F32))
        psE = ctx.enter_context(nc.psum_tensor("psE", [P, 512], F32))
        b0, b1, b2k, b3 = (psT[:, i, :] for i in range(4))
        b4 = psE[:, :]
        b5, b6, b7 = (t[:, :] for t in bank)

        cst = sb("cst", [P, C_ALL])
        sizes = [2 * TOKENS, TOKENS, 2 * D, CHUNKS * (D + 1), SHIFTS * D, SHIFTS * D, TILES * D]
        with nc.sbuf_tensor("X", [P, CHUNKS, TOKENS], F32) as X, nc.sbuf_tensor("early", [P, sum(sizes)], F32) as early:
            pass
        w1bl = sb("w1bl", [HI + 2, E, F], F32R)
        shared = sb("shared", [P, max(RAW * F, TOP * TILES * (P // 2 + BCOLS + BCOLS))])
        raw = shared[:, 0:RAW * F].rearrange("p (a f) -> p a f", a=RAW)
        w1bh = sb("w1bh", [P, E, F], F32R)
        w1ah = sb("w1ah", [P, E, F], F32R)
        w1al = sb("w1al", [P, E, F], F32R)
        b1r = sb("b1r", [BR, E * F // BR])
        b1h = sb("b1h", [BR, E * F // BR], F32R)
        b1l = sb("b1l", [BR, E * F // BR], F32R)
        starts = [sum(sizes[:i]) for i in range(len(sizes) + 1)]
        part = [early[:, starts[i]:starts[i + 1]] for i in range(len(sizes))]
        Xsq = part[0].rearrange("p (a n) -> p a n", a=2)
        sqsum = part[1]
        We = part[2].rearrange("p (a n) -> p a n", a=2)[0:EDGE]
        weff = part[3].rearrange("p (a n) -> p a n", a=CHUNKS)
        bprod = part[4].rearrange("p (a n) -> p a n", a=SHIFTS)
        bacc = part[5].rearrange("p (a n) -> p a n", a=SHIFTS)
        ttmp = part[6].rearrange("p (a n) -> p a n", a=TILES)
        gb = sb("gb", [P, (2 * SHIFTS + 1) * CHUNKS])
        gam, bet = (gb[:, i * CHUNKS * SHIFTS:(i + 1) * CHUNKS * SHIFTS].rearrange("p (c s) -> p c s", c=CHUNKS)
                    for i in range(2))
        mult = gb[:, 2 * CHUNKS * SHIFTS:]
        tokb = sb("tokb", [P, D])
        g_sb = sb("g_sb", [P, D])
        bw_sb = sb("bw_sb", [P, D])
        st = sb("st", [P, 12, TILES])
        takes = [4 * TILES * P, TILES * D, TILES * D, TILES * GROUPS, TOKENS, 3 * D]
        attn = sb("attn", [P, max(sum(takes), E * FC * D)])
        spot = [attn[:, sum(takes[:i]):sum(takes[:i + 1])] for i in range(len(takes))]
        w2s = attn[:, 0:E * FC * D].rearrange("p (a n) -> p a n", n=D)
        h = spot[1].rearrange("p (t d) -> p t d", t=TILES)
        hb = sb("hb", [P, TILES, D])
        hn = sb("hn", [P, TILES, D])
        bn6 = sb("bn6", [P, TILES, 6])
        mv = sb("mv", [P, TILES, 2])
        rstd = sb("rstd", [P, TILES])
        var = sb("var", [P, TILES])
        sd = sb("sd", [P, TILES])
        nmr = sb("nmr", [P, TILES])
        hnTa = sb("hnTa", [P, TOKENS])
        hnTb = sb("hnTb", [HI + 1, TOKENS])
        wqa = spot[5]
        wqb = sb("wqb", [HI + 1, 3 * D])
        wpa = sb("wpa", [P, VG])
        wpb = sb("wpb", [HI, VG])
        wvTa = sb("wvTa", [P, D + 1])
        wvTb = sb("wvTb", [HI, D + 1])
        wga = sb("wga", [P, VG])
        wgb = sb("wgb", [HI + 1, VG])
        bpr = sb("bpr", [P, D])
        qk = sb("qk", [P, 4, TOKENS])
        q0, k0, q1, k1 = qk[:, 0], qk[:, 1], qk[0:HI, 2], qk[0:HI, 3]
        hg = qk[:, 0, 0:F]
        hT = qk[:, 1, 0:F].rearrange("p (c n) -> p c n", n=P)
        combT = qk[0:E, 2]
        vp = spot[2].rearrange("p (t d) -> p t d", t=TILES)
        vps = h
        gw = spot[3].rearrange("p (t g) -> p t g", t=TILES)
        gred = sb("gred", [P, 3, TILES])
        gwT = spot[4][0:GROUPS]
        maps = spot[0].rearrange("p (a t n) -> p a t n", a=4, t=TILES)
        gwm, tt, Aw, AT = (maps[:, i] for i in range(4))
        Wt = maps[:, :, :, :].rearrange("p a t n -> p (a t n)")[:, 0:RING * SHIFTS * D].rearrange(
            "p (a s n) -> p a s n", a=RING, s=SHIFTS)
        ct = sb("ct", [P, TILES, PLACES])
        cred = sb("cred", [P, 3, TILES])
        sig = sb("sig", [P, 5])
        wgate = sb("wgate", [P, E + 1])
        wgateb = sb("wgateb", [HI + 1, E + 1])
        vcl = sb("vcl", [P, TILES])
        vT = sb("vT", [TILES, P])
        lg = sb("lg", [P, TILES, E])
        gate_st = sb("gate_st", [P, 3, TILES])
        pr = sb("pr", [P, TILES, E])
        m8 = sb("m8", [P, TILES, 8])
        i8 = sb("i8", [P, TILES, 8], U32)
        best = sb("best", [P, TOP, TILES])
        cw = sb("cw", [P, TOP, TILES])
        oh = sb("oh", [P, TOP, TILES, E])
        ohp = sb("ohp", [P, TOP, TILES, E])
        M = sb("M", [P, TILES, E])
        incl = sb("incl", [P, E, TILES])
        before = sb("before", [P, E * TILES])
        rank = sb("rank", [P, E, TILES])
        gt = sb("gt", [P, E, E])
        blk = sb("blk", [P, 3, E])
        slot = sb("slot", [P, E, TILES])
        sloti = sb("sloti", [P, 3, TOP * TILES], I32)
        gidr = sb("gidr", [P, BCOLS], I32)
        offb = sb("offb", [P, P], BF16)
        JH, JB = TOP * TILES * P // 2, TOP * TILES * BCOLS
        ohoff = shared[:, 0:JH].bitcast(BF16).rearrange("p (r n) -> p r n", n=P)
        ohblk = shared[:, JH:JH + JB].rearrange("p (r n) -> p r n", n=BCOLS)
        tabr = shared[:, JH + JB:JH + 2 * JB].bitcast(BF16).rearrange("p (r a n) -> p r a n", a=2, n=BCOLS)
        tab = sb("tab", [P, 5, BCOLS])
        gid = sb("gid", [P, BCOLS], I32)
        sid = sb("sid", [P, BCOLS], I32)
        cur = sb("cur", [P, 2], I32)
        emt = sb("emt", [1, BCOLS, E])
        emtf = sb("emtf", [1, BCOLS])
        emap = sb("emap", [1, BCOLS], I32)
        nblk = sb("nblk", [1, 2], I32)
        comb = sb("comb", [P, TILES, E])
        combt = sb("combt", [P, TOP, TILES, E])
        b2s = sb("b2s", [E, D])
        sw = sb("sw", [3, D])
        bks = sb("bks", [3, D])
        feat = qk[0:3, 3]
        v2 = sb("v2", [P, PLACES])
        v2r = sb("v2r", [P, PLACES])
        add = sb("add", [P, PLACES, 2])
        ch = sb("ch", [P, PLACES, 2])
        chj = sb("chj", [P, PLACES, 2])
        chd = sb("chd", [P, 2, PLACES])
        back = sb("back", [IMAGES, PLACES, 2])
        z = sb("z", [IMAGES, 2, PLACES])
        zz = sb("zz", [IMAGES, 4, PLACES])
        xg_first = sb("xg_first", [P, D])
        xg = sb("xg", [P, D])
        xah = sb("xah", [P, P], F32R)
        xal = sb("xal", [P, P], F32R)
        xbb = sb("xbb", [P, P], F32R)
        xbh = sb("xbh", [P, P], F32R)
        ysb = g_sb
        yb = attn[:, 0:TOP * TILES * D].rearrange("p (j t d) -> p j t d", j=TOP, t=TILES)

        gate_ps = (b2k, b3)
        o_ps = ((b2k, b3), (b6, b5))
        vg = psT[:, 2:4, :].rearrange("p a (b n) -> p a b n", b=2)
        ident = cst[:, C_ID:C_ID + P]
        diag = cst[:, C_DIAG:C_DIAG + P]
        ones = cst[:, C_ONE:C_ONE + P]
        half = [slice(0, HALF), slice(HALF, TILES)]
        cols = [slice(0, HT), slice(HT, TOKENS)]

        names = """s_cst s_gb s_tokb s_qkv s_wp s_bpr s_alpha s_gate s_b2 s_sw d_b1 d_bias s_w2 s_bk
            v_weff a_sq v_chain p_chain p_prod p_acc pe_w t_sum t_bias v_bias v_h p_hb pe_hT a_hT pe_qk av_qk a_q v_qk pe_vg a_vp a_gelu
            v_gsub a_gexp v_gw pe_gwT a_gwT pe_wvT a_wvT pe_wg a_wg
            pe_s pe_gw v_csub a_cexp v_A pe_AT a_AT pe_o v_h1 d_hn2 pe_h2T v_hT pe_gate v_v pe_vT a_vT d_v
            v_lsub a_lexp v_M pe_rank v_tabr pe_tab v_tab v_emap p_ones a_sig v_sig v_comb pe_combT v_feat d_feat v_sw
            a_combT d_gather pe_xT a_xh pe_up0 pe_up1 a_ge pe_hgT v_hgT pe_y v_y d_scatter pe_base v_base
            d_yb0 d_yb1 d_yb2 d_yb3 v_out d_out p_gidx p_sidx p_pass p_col v_sq p_done p_hi p_lo p_b1 v_xl d_first t_col p_tabr v_gid v_gwm a_vps a_g a_yb p_out a_hi v_blk a_tabr a_top v_top v_cmul a_Aw a_hn v_nmr v_offs p_off v_hnb a_off v_var a_sd""".split()
        S = {n: sem(n) for n in dict.fromkeys(names)}
        d_x = [sem(f"d_x{c}") for c in range(CHUNKS)]
        d_raw = [sem(f"d_raw{i}") for i in range(RAW)]
        d_w = [sem(f"d_w{c}") for c in range(CHUNKS)]
        block = ctx.enter_context(nc.Block())

        @block.sync
        def _(sp):
            sp.dma_start(gb[:, :], gammas_betas).then_inc(S["s_gb"], 16)
            for c in range(CHUNKS):
                k = CROWS[c]
                if c < INNER:
                    if c >= RING:
                        sp.wait_ge(S["v_weff"], c - RING + 1)
                        sp.wait_ge(S["p_prod"], c - RING + 1)
                    sp.dma_start(Wt[:, c % RING, :, :], mult_w[c]).then_inc(d_w[c], 16)
                else:
                    sp.dma_start(We[:, c - INNER, :], edge_w[c - INNER]).then_inc(d_w[c], 16)
                sp.dma_start(X[0:k, c, :], pixels[c, 0:k, :]).then_inc(d_x[c], 16)
                if c == 1:
                    sp.dma_start(cst[:, :], consts).then_inc(S["s_cst"], 16)
            sp.dma_start(tokb[:, :], tok_b.partition_broadcast(P)).then_inc(S["s_tokb"], 16)
            sp.dma_start(wqa[:, :], wqkv[0:LO]).then_inc(S["s_qkv"], 16)
            sp.dma_start(wqb[:, :], wqkv[LO:]).then_inc(S["s_qkv"], 16)
            sp.dma_start(wpa[:, :], wpg[0:LO]).then_inc(S["s_wp"], 16)
            sp.dma_start(wpb[:, :], wpg[LO:]).then_inc(S["s_wp"], 16)
            sp.dma_start(bpr[:, :], b_proj.partition_broadcast(P)).then_inc(S["s_bpr"], 16)
            sp.dma_start(sig[:, 0:1], alpha.partition_broadcast(P)).then_inc(S["s_alpha"], 16)
            sp.dma_start(wgate[:, :], gate[0:LO]).then_inc(S["s_gate"], 16)
            sp.dma_start(wgateb[:, :], gate[LO:]).then_inc(S["s_gate"], 16)
            sp.dma_start(b2s[:, :], b2).then_inc(S["s_b2"], 16)
            sp.dma_start(sw[:, :], spec_w).then_inc(S["s_sw"], 16)
            sp.dma_start(bks[:, :], bk.partition_broadcast(3)).then_inc(S["s_bk"], 16)
            sp.dma_start(b1r[:, :], bias1).then_inc(S["d_b1"], 16)
            sp.wait_ge(S["t_sum"], 1)
            for c in range(2 * E):
                if c >= RAW:
                    sp.wait_ge(S["p_lo"], c - RAW + 1)
                for i in range(2):
                    row = LO if c >= E else i * HI
                    sp.dma_start(raw[i * HI:(i + 1) * HI, c % RAW, :],
                                 w1[c % E, row:row + HI, :]).then_inc(d_raw[c % RAW], 16)
            for f in range(2):
                sp.wait_ge(S["v_hnb"], f + 3)
                sp.wait_ge(S["a_hn"], (f + 3) * (HALF - SPLIT))
                sp.dma_start(hn2_rows[f * HT:(f + 1) * HT].rearrange("(t p) d -> p t d", p=P),
                             hn[:, half[f], :]).then_inc(S["d_hn2"], 16)
            sp.wait_ge(S["pe_o"], 2)
            sp.wait_ge(S["p_hb"], 2)

            def second_weights(e):
                sp.dma_start(w2s[:, e * FC:(e + 1) * FC, :],
                             w2[e].rearrange("(c p) d -> p c d", p=P)).then_inc(S["s_w2"], 16)

            for e in range(2):
                second_weights(e)
            sp.wait_ge(S["a_vT"], 1)
            for d in range(2):
                sp.dma_start(v2[d * IMAGES:(d + 1) * IMAGES, :],
                             vT[:, :].rearrange("t (b n) -> t b n", n=PLACES)).then_inc(S["d_v"], 16)
            for e in range(2, E):
                second_weights(e)
            sp.wait_ge(S["p_ones"], 3)
            sp.wait_ge(S["v_feat"], 1)
            for r in range(2):
                sp.dma_start(feat[r:r + 1, :].rearrange("r (b n) -> r b n", n=PLACES),
                             z[:, r, :]).then_inc(S["d_feat"], 16)
            sp.wait_ge(S["p_done"], 1)
            for q in range(4):
                sp.dma_start(yb[:, 0, 2 * q:2 * q + 2, :],
                             y_rows[2 * q * P:(2 * q + 2) * P].rearrange("(t p) d -> p t d", p=P)
                             ).then_inc(S[f"d_yb{q}"], 16)
                sp.dma_start(yb[:, 1, 2 * q:2 * q + 2, :],
                             y_rows[TOKENS + 2 * q * P:TOKENS + (2 * q + 2) * P].rearrange("(t p) d -> p t d", p=P)
                             ).then_inc(S[f"d_yb{q}"], 16)
            for q in [q for q in range(4) if q != POOL_PAIR] + [POOL_PAIR]:
                if q == POOL_PAIR:
                    sp.wait_ge(S["p_out"], 2)
                else:
                    sp.wait_ge(S["v_out"], q + 1 - (q > POOL_PAIR))
                sp.dma_start(out[2 * q * P:(2 * q + 2) * P].rearrange("(t p) d -> p t d", p=P),
                             hb[:, 2 * q:2 * q + 2, :]).then_inc(S["d_out"], 16)
            sp.wait_ge(S["d_out"], 64)

        @block.gpsimd
        def _(pool):
            pool.memset(hnTb[HI:HI + 1, :], 1.0).then_inc(S["p_ones"], 1)
            pool.wait_ge(S["p_ones"], 1)
            pool.memset(xbh[HI:P, :].bitcast(F32), 1.0).then_inc(S["p_ones"], 1)
            pool.wait_ge(S["p_ones"], 2)
            pool.wait_ge(S["s_gb"], 16)
            for c in range(CHUNKS):
                pool.wait_ge(d_w[c], 16)
                if c < INNER:
                    dst = bacc if c == 0 else bprod
                    if c >= 2:
                        pool.wait_ge(S["p_acc"], c)
                    pool.tensor_tensor(dst[:, :, :], Wt[:, c % RING, :, :],
                                       bet[:, c, :].unsqueeze(2).broadcast_to([P, SHIFTS, D]),
                                       ALU.mult).then_inc(S["p_prod"], 1)
                    pool.wait_ge(S["p_prod"], c + 1)
                    if c > 0:
                        pool.tensor_tensor(bacc[:, :, :], bacc[:, :, :], bprod[:, :, :],
                                           ALU.add).then_inc(S["p_acc"], 1)
                    else:
                        pool.sem_inc(S["p_acc"], 1)
                else:
                    pool.wait_ge(S["p_acc"], c)
                    pool.tensor_tensor(bprod[0:EDGE, 0, :], We[:, c - INNER, :],
                                       bet[0:EDGE, c, 0:1].broadcast_to([EDGE, D]),
                                       ALU.mult).then_inc(S["p_prod"], 1)
                    pool.wait_ge(S["p_prod"], c + 1)
                    pool.tensor_tensor(bacc[0:EDGE, 0, :], bacc[0:EDGE, 0, :], bprod[0:EDGE, 0, :],
                                       ALU.add).then_inc(S["p_acc"], 1)
            for i in range(1, SHIFTS):
                pool.wait_ge(S["p_acc"], CHUNKS + i - 1)
                pool.tensor_tensor(bacc[:, 0, :], bacc[:, 0, :], bacc[:, i, :], ALU.add).then_inc(S["p_acc"], 1)
            pool.wait_ge(S["s_bpr"], 16)
            for f in range(2):
                pool.wait_ge(S["v_h"], f + 1)
                pool.tensor_tensor(hb[:, half[f], :], h[:, half[f], :],
                                   bpr[:, :].unsqueeze(1).broadcast_to([P, HALF, D]),
                                   ALU.add).then_inc(S["p_hb"], 1)
            pool.wait_ge(S["p_hb"], 2)
            pool.wait_ge(S["d_b1"], 16)
            pool.tensor_copy(b1h[:, :], b1r[:, :]).then_inc(S["p_b1"], 1)
            pool.wait_ge(S["p_b1"], 1)
            pool.tensor_tensor(b1l[:, :], b1r[:, :], b1h[:, :].bitcast(F32), ALU.subtract).then_inc(S["p_b1"], 1)
            pool.wait_ge(S["p_b1"], 2)
            pool.wait_ge(S["t_bias"], 1)
            for i, b in enumerate((b1h, b1l)):
                pool.dma_start(w1bl[HI + i:HI + i + 1].rearrange("o e f -> o (e f)").rearrange(
                    "o (p n) -> o p n", p=BR), b[:, :]).then_inc(S["d_bias"], 16)
            for c in range(2 * E):
                e = c % E
                if c > 0:
                    pool.wait_ge(S["p_lo"], c)
                pool.wait_ge(d_raw[c % RAW], 32 * (c // RAW + 1))
                hi = (w1ah if c < E else w1bh)[:, e, :]
                if c % 2 == 0:
                    pool.tensor_copy(hi, raw[:, c % RAW, :]).then_inc(S["p_hi"], 1)
                    pool.wait_ge(S["p_hi"], c // 2 + 1)
                else:
                    pool.wait_ge(S["a_hi"], c // 2 + 1)
                k = P if c < E else HI
                pool.tensor_tensor((w1al if c < E else w1bl)[0:k, e, :], raw[0:k, c % RAW, :],
                                   hi[0:k].bitcast(F32), ALU.subtract).then_inc(S["p_lo"], 1)
            pool.wait_ge(S["pe_o"], 2)
            pool.wait_ge(S["p_lo"], 2 * E)
            pool.memset(feat[:, :], 1.0).then_inc(S["p_ones"], 1)
            pool.wait_ge(S["v_blk"], 1)
            pool.tensor_tensor(tabr[:, :, 1, :], ohblk[:, :, :],
                               cst[:, C_TILE:C_TILE + TOP * TILES].unsqueeze(2).broadcast_to([P, TOP * TILES, BCOLS]),
                               ALU.mult).then_inc(S["p_tabr"], 1)
            pool.wait_ge(S["v_emap"], 1)
            pool.wait_ge(S["d_hn2"], 32)
            m = pool.value_load(nblk[0:1, 1:2], min_val=TOP * TOKENS // P - 2, max_val=BLOCKS - 2)

            last_row = pool.to_reg(TOP * TOKENS - 1)

            def gather_rows(rows, index, landed):
                pool.indirect_dma_start(rows[:, :], None, hn2_rows,
                                        bass.IndirectOffsetOnAxis(index, 0)).then_inc(landed, 16)

            def gather(b):
                pool.tensor_copy(cur[:, 0:1], gid[:, bass.ds(b, 1)]).then_inc(S["p_gidx"], 1)
                pool.wait_ge(S["p_gidx"], b - 1)
                pool.sem_inc(S["p_pass"], 1)
                gather_rows(xg, cur[:, 0:1], S["d_gather"])

            def scatter(b):
                pool.wait_ge(S["v_y"], b + 1)
                pool.sem_inc(S["p_pass"], 1)
                pool.tensor_copy(cur[:, 1:2], sid[:, bass.ds(b, 1)]).then_inc(S["p_sidx"], 1)
                pool.wait_ge(S["p_sidx"], b + 1)
                pool.sem_inc(S["p_pass"], 1)
                pool.indirect_dma_start(y_rows, bass.IndirectOffsetOnAxis(cur[:, 1:2], 0), ysb[:, :], None,
                                        bounds_check=last_row, oob_is_err=False
                                        ).then_inc(S["d_scatter"], 16)

            pool.wait_ge(S["v_gid"], 1)
            gather_rows(xg_first, gid[:, 0:1], S["d_first"])
            gather_rows(xg, gid[:, 1:2], S["d_gather"])
            pool.wait_ge(S["v_tab"], 1)
            pool.wait_ge(S["pe_xT"], 2)
            gather(2)
            with pool.Fori(0, m) as i:
                pool.wait_ge(S["pe_xT"], i + 3)
                pool.sem_inc(S["p_pass"], 1)
                gather(i + 3)
                scatter(i)
            scatter(m)
            scatter(m + 1)
            pool.wait_ge(S["d_scatter"], m * 16 + 32)
            pool.sem_inc(S["p_done"], 1)
            pool.wait_ge(S["v_base"], 4)
            pair = slice(2 * POOL_PAIR, 2 * POOL_PAIR + 2)
            for j in range(TOP):
                pool.wait_ge(S["a_yb"], 2 * j + 2)
                if j > 0:
                    pool.wait_ge(S["p_out"], j)
                pool.tensor_tensor(hb[:, pair, :], hb[:, pair, :], yb[:, j, pair, :], ALU.add).then_inc(S["p_out"], 1)

        @block.scalar
        def _(act):
            for c in range(CHUNKS):
                act.wait_ge(d_x[c], 16)
                if c >= 2:
                    act.wait_ge(S["v_sq"], c - 1)
                k = CROWS[c]
                act.activation(Xsq[0:k, c % 2, :], X[0:k, c, :], ACT.Square).then_inc(S["a_sq"], 1)
            act.wait_ge(S["v_var"], 1)
            act.activation(st[:, 6, :], st[:, 5, :], ACT.Sqrt).then_inc(S["a_sd"], 1)
            act.wait_ge(S["t_col"], 1)
            act.activation(g_sb[:, :], b5[:, 0:D], ACT.Copy).then_inc(S["a_g"], 1)

            def deviation(f, turn):
                act.wait_ge(S["v_var"], turn)
                act.activation(sd[:, half[f]], var[:, half[f]], ACT.Sqrt).then_inc(S["a_sd"], 1)

            def norm_rows(src, f):
                for t in range(f * HALF + SPLIT, (f + 1) * HALF):
                    act.activation(hn[:, t, :], src[:, t, :], ACT.Identity, bias=nmr[:, t:t + 1],
                                   scale=rstd[:, t:t + 1]).then_inc(S["a_hn"], 1)

            def high_w1(c):
                act.wait_ge(d_raw[c % RAW], 32 * (c // RAW + 1))
                act.activation((w1ah if c < E else w1bh)[:, c % E, :], raw[:, c % RAW, :],
                               ACT.Copy).then_inc(S["a_hi"], 1)

            act.wait_ge(S["pe_wvT"], 1)
            act.activation(wvTa[:, :], b7[:, 0:D + 1], ACT.Copy).then_inc(S["a_wvT"], 1)
            act.activation(wvTb[:, :], b7[0:HI, 256:256 + D + 1], ACT.Copy).then_inc(S["a_wvT"], 1)
            act.wait_ge(S["pe_wg"], 1)
            act.activation(wga[:, :], b7[:, 0:VG], ACT.Copy).then_inc(S["a_wg"], 1)
            act.activation(wgb[:, :], b7[0:HI + 1, 256:256 + VG], ACT.Copy).then_inc(S["a_wg"], 1)
            for f in range(2):
                deviation(f, f + 2)
                act.wait_ge(S["v_nmr"], f + 1)
                norm_rows(h, f)
                if f == 0:
                    act.wait_ge(S["pe_hT"], 1)
                    act.activation(hnTa[:, cols[0]], b7, ACT.Copy).then_inc(S["a_hT"], 1)
            act.wait_ge(S["v_h"], 2)
            act.wait_ge(S["t_bias"], 1)
            high_w1(1)

            def take_values(f):
                act.activation(vp[:, half[f], :].rearrange("p (a b) g -> p a b g", b=2), vg[:, :, :, 0:D],
                               ACT.Copy).then_inc(S["a_vp"], 1)

            for f in range(2):
                act.wait_ge(S["pe_qk"], 3 * f + 1)
                act.activation(q0[:, cols[f]], b0, ACT.Copy).then_inc(S["a_q"], 1)
                act.wait_ge(S["pe_qk"], 3 * f + 2)
                act.activation(k0[:, cols[f]], b1, ACT.Copy).then_inc(S["a_q"], 1)
                if f == 0:
                    act.wait_ge(S["pe_hT"], 2)
                    act.activation(hnTa[:, cols[1]], b4, ACT.Copy).then_inc(S["a_hT"], 1)
                high_w1(2 * f + 3)
                act.wait_ge(S["pe_vg"], f + 1)
                act.activation(gw[:, half[f], :].rearrange("p (a b) g -> p a b g", b=2), vg[:, :, :, D:VG],
                               ACT.Gelu).then_inc(S["a_gelu"], 1)
                if f == 0:
                    take_values(0)
            act.wait_ge(S["s_alpha"], 16)
            act.activation(sig[:, 1:2], sig[:, 0:1], ACT.Exp, scale=-1.0).then_inc(S["a_sig"], 1)
            for f in range(2):
                act.wait_ge(S["v_gsub"], f + 1)
                act.activation(gw[:, half[f], :], gw[:, half[f], :], ACT.Exp).then_inc(S["a_gexp"], 1)
            high_w1(7)
            for f in range(2):
                act.wait_ge(S["pe_gwT"], f + 1)
                act.activation(gwT[:, cols[f]], (b0, b1)[f][0:GROUPS, :], ACT.Copy).then_inc(S["a_gwT"], 1)
            take_values(1)
            act.wait_ge(S["v_sig"], 1)
            for f in range(2):
                act.wait_ge(S["a_vp"], f + 1)
                act.activation(vps[:, half[f], :], vp[:, half[f], :], ACT.Copy,
                               scale=sig[:, 3:4]).then_inc(S["a_vps"], 1)
            for f in range(2):
                act.wait_ge(S["v_csub"], f + 1)
                act.activation(ct[:, half[f], :], ct[:, half[f], :], ACT.Exp).then_inc(S["a_cexp"], 1)
                if f == 0:
                    high_w1(9)
            for f in range(2):
                act.wait_ge(S["pe_AT"], f + 1)
                act.activation(AT[:, half[f], :].rearrange("p t n -> p (t n)"), (b0, b1)[f],
                               ACT.Copy).then_inc(S["a_AT"], 1)
                if f == 0:
                    high_w1(11)
            for f in range(2):
                deviation(f, f + 4)
                act.wait_ge(S["v_nmr"], f + 3)
                norm_rows(hb, f)
                act.wait_ge(S["pe_h2T"], f + 1)
                act.activation(hnTa[:, cols[f]], (b7, b4)[f], ACT.Copy).then_inc(S["a_hT"], 1)
                high_w1(13 + 2 * f)
            act.wait_ge(S["pe_vT"], 1)
            act.activation(vT[:, :], b4[0:TILES, 0:P], ACT.Copy).then_inc(S["a_vT"], 1)
            act.wait_ge(S["v_lsub"], 1)
            act.activation(pr[:, :, :], lg[:, :, :], ACT.Exp).then_inc(S["a_lexp"], 1)
            act.wait_ge(S["v_top"], 1)
            act.activation(best[:, :, :], best[:, :, :], ACT.Exp).then_inc(S["a_top"], 1)
            act.wait_ge(S["v_blk"], 1)
            act.activation(tabr[:, :, 0, :], ohblk[:, :, :], ACT.Copy,
                           scale=cst[:, C_PART:C_PART + 1]).then_inc(S["a_tabr"], 1)
            for f in range(2):
                act.wait_ge(S["pe_combT"], f + 1)
                act.activation(combT[:, cols[f]], (b5, b6)[f][0:E, :], ACT.Copy).then_inc(S["a_combT"], 1)
            act.wait_ge(S["v_emap"], 1)
            n = act.value_load(nblk[0:1, 0:1], min_val=TOP * TOKENS // P, max_val=BLOCKS)

            def high_x(b):
                act.activation(xah[:, :], b7[:, 0:P], ACT.Copy).then_inc(S["a_xh"], 1)
                act.activation(xbb[0:HI, :], b7[0:HI, P:2 * P], ACT.Copy).then_inc(S["a_xh"], 1)
                act.wait_ge(S["a_xh"], b * 3 + 2)
                act.activation(xbh[0:HI, :], xbb[0:HI, :].bitcast(F32), ACT.Copy).then_inc(S["a_xh"], 1)

            def gelu(part):
                act.activation(hg[:, part * FH:(part + 1) * FH], (b0, b1)[part][:, 0:FH],
                               ACT.Gelu_apprx_tanh).then_inc(S["a_ge"], 1)

            act.wait_ge(S["pe_xT"], 1)
            act.wait_ge(S["p_ones"], 2)
            high_x(0)
            act.wait_ge(S["pe_up0"], 1)
            gelu(0)
            act.wait_ge(S["pe_xT"], 2)
            high_x(1)
            act.wait_ge(S["pe_up1"], 1)
            gelu(1)
            with act.Fori(1, n) as i:
                act.wait_ge(S["pe_up0"], i + 1)
                act.wait_ge(S["pe_hgT"], i * 2)
                gelu(0)
                act.wait_ge(S["pe_xT"], i + 2)
                high_x(i + 1)
                act.wait_ge(S["pe_up1"], i + 1)
                gelu(1)
            act.wait_ge(S[f"d_yb{POOL_PAIR}"], 32)
            for j in range(TOP):
                for t in (2 * POOL_PAIR, 2 * POOL_PAIR + 1):
                    act.activation(yb[:, j, t, :], yb[:, j, t, :], ACT.Copy,
                                   scale=cw[:, j, t:t + 1]).then_inc(S["a_yb"], 1)

        @block.vector
        def _(dve):
            count = [0]

            def link(ins):
                count[0] += 1
                ins.then_inc(S["v_chain"], 1)
                dve.wait_ge(S["v_chain"], count[0])

            dve.wait_ge(S["s_gb"], 16)
            dve.tensor_copy(weff[:, :, D:D + 1], mult.unsqueeze(2))

            def sum_squares(c):
                k = CROWS[c]
                dve.wait_ge(S["a_sq"], c + 1)
                times = mult[0:k, c:c + 1]
                if c == 0:
                    ins = dve.tensor_scalar(sqsum[:, :], Xsq[:, 0, :], times, None, ALU.mult)
                else:
                    dve.wait_ge(S["v_sq"], c)
                    ins = dve.scalar_tensor_tensor(sqsum[0:k], Xsq[0:k, c % 2, :], times, sqsum[0:k], ALU.mult, ALU.add)
                ins.then_inc(S["v_sq"], 1)

            for c in range(CHUNKS):
                dve.wait_ge(d_w[c], 16)
                if c < INNER:
                    link(dve.tensor_scalar(weff[:, c, 0:D], Wt[:, c % RING, 0, :], gam[:, c, 0:1], None, ALU.mult))
                    for i in range(1, SHIFTS):
                        ins = dve.scalar_tensor_tensor(weff[:, c, 0:D], Wt[:, c % RING, i, :], gam[:, c, i:i + 1],
                                                       weff[:, c, 0:D], ALU.mult, ALU.add)
                        if i < SHIFTS - 1:
                            link(ins)
                    ins.then_inc(S["v_weff"], 1)
                else:
                    dve.tensor_scalar(weff[0:EDGE, c, 0:D], We[:, c - INNER, :], gam[0:EDGE, c, 0:1], None,
                                      ALU.mult).then_inc(S["v_weff"], 1)
                if c > 0:
                    sum_squares(c - 1)
            sum_squares(CHUNKS - 1)
            dve.wait_ge(S["s_cst"], 16)
            dve.tensor_copy(offb[:, :], cst[:, C_OFF:C_OFF + P])
            dve.wait_ge(S["s_sw"], 16)
            dve.wait_ge(S["s_bk"], 16)
            dve.tensor_tensor(sw[:, :], sw[:, :], bks[:, :], ALU.mult).then_inc(S["v_sw"], 1)
            dve.wait_ge(S["t_sum"], 1)
            tview = psT[:, :, :].rearrange("p a (b n) -> p a b n", b=2)
            tv = [tview[:, t // 2, t % 2, :] for t in range(TILES)]
            link(dve.tensor_scalar(st[:, 0, :].rearrange("p (a b) -> p a b", b=2), tview[:, :, :, D], -1.0 / FEATURES,
                                   None, ALU.mult))
            link(dve.tensor_tensor(st[:, 1, :], st[:, 0, :], st[:, 0, :], ALU.mult))
            link(dve.scalar_tensor_tensor(st[:, 2, :], b4[:, 0:TILES], 1.0 / FEATURES, st[:, 1, :],
                                          ALU.mult, ALU.subtract))
            dve.tensor_scalar(st[:, 5, :], st[:, 2, :], EPS, None, ALU.add).then_inc(S["v_var"], 1)
            dve.wait_ge(S["a_sd"], 1)
            link(dve.reciprocal(st[:, 3, :], st[:, 6, :]))
            link(dve.tensor_tensor(st[:, 4, :], st[:, 0, :], st[:, 3, :], ALU.mult))
            dve.wait_ge(S["t_bias"], 1)
            dve.wait_ge(S["s_tokb"], 16)
            dve.wait_ge(S["a_g"], 1)
            link(dve.tensor_tensor(bw_sb[:, :], b6[:, 0:D], tokb[:, :], ALU.add))
            def make_h(f):
                for t in range(f * HALF, (f + 1) * HALF):
                    ins = dve.scalar_tensor_tensor(ttmp[:, t, :], g_sb[:, :], st[:, 4, t:t + 1], bw_sb[:, :],
                                                   ALU.mult, ALU.add)
                link(ins)
                for t in range(f * HALF, (f + 1) * HALF):
                    ins = dve.scalar_tensor_tensor(h[:, t, :], tv[t][:, 0:D], st[:, 3, t:t + 1], ttmp[:, t, :],
                                                   ALU.mult, ALU.add)
                ins.then_inc(S["v_h"], 1)
                dve.wait_ge(S["v_h"], f + 1)

            def take_low_rows(f, turn, src):
                dve.wait_ge(src[0], turn)
                dve.tensor_copy(hnTb[0:HI, cols[f]], src[1][0:HI, :]).then_inc(S["v_hT"], 1)

            def norm(src, f, turn, between=None):
                for t in range(f * HALF, (f + 1) * HALF):
                    ins = dve.bn_stats(bn6[:, t, :], src[:, t, :])
                link(ins)
                for t in range(f * HALF, (f + 1) * HALF):
                    ins = dve.bn_aggr(mv[:, t, :], bn6[:, t, :])
                link(ins)
                dve.tensor_scalar(var[:, half[f]], mv[:, half[f], 1], EPS, None, ALU.add).then_inc(S["v_var"], 1)
                if between:
                    between()
                dve.wait_ge(S["a_sd"], turn)
                link(dve.reciprocal(rstd[:, half[f]], sd[:, half[f]]))
                link(dve.scalar_tensor_tensor(nmr[:, half[f]], mv[:, half[f], 0], -1.0, rstd[:, half[f]],
                                              ALU.mult, ALU.mult))
                dve.sem_inc(S["v_nmr"], 1)
                for t in range(f * HALF, f * HALF + SPLIT):
                    ins = dve.tensor_scalar(hn[:, t, :], src[:, t, :], mv[:, t, 0:1], rstd[:, t:t + 1],
                                            ALU.subtract, ALU.mult)
                ins.then_inc(S["v_hnb"], 1)

            make_h(0)
            norm(h, 0, 2)
            make_h(1)
            take_low_rows(0, 1, (S["pe_hT"], b6))
            norm(h, 1, 3)
            for f in range(2):
                dve.wait_ge(S["pe_qk"], 3 * f + 3)
                dve.tensor_copy(q1[:, cols[f]], b5[0:HI, :])
                dve.tensor_copy(k1[:, cols[f]], b5[HI:P, :]).then_inc(S["v_qk"], 1)
                if f == 0:
                    take_low_rows(1, 2, (S["pe_hT"], b6))
                dve.wait_ge(S["a_gelu"], f + 1)
                g = gw[:, half[f], :]
                link(dve.tensor_reduce(gred[:, 0, half[f]], g, AX.X, ALU.max))
                dve.tensor_tensor(g, g, gred[:, 0, half[f]].unsqueeze(2).broadcast_to([P, HALF, GROUPS]),
                                  ALU.subtract).then_inc(S["v_gsub"], 1)
            for f in range(2):
                g = gw[:, half[f], :]
                dve.wait_ge(S["a_gexp"], f + 1)
                link(dve.tensor_reduce(gred[:, 1, half[f]], g, AX.X, ALU.add))
                link(dve.reciprocal(gred[:, 2, half[f]], gred[:, 1, half[f]]))
                dve.tensor_tensor(g, g, gred[:, 2, half[f]].unsqueeze(2).broadcast_to([P, HALF, GROUPS]),
                                  ALU.mult).then_inc(S["v_gw"], 1)
            dve.wait_ge(S["a_sig"], 1)
            link(dve.tensor_scalar(sig[:, 2:3], sig[:, 1:2], 1.0, None, ALU.add))
            link(dve.reciprocal(sig[:, 3:4], sig[:, 2:3]))
            link(dve.tensor_tensor(sig[:, 4:5], sig[:, 1:2], sig[:, 3:4], ALU.mult))
            dve.sem_inc(S["v_sig"], 1)
            dg = diag.unsqueeze(1).broadcast_to([P, HALF, P])

            def masked_scores(f):
                dve.wait_ge(S["pe_gw"], f + 1)
                link(dve.tensor_tensor(gwm[:, half[f], :], (b6, b5)[f].rearrange("p (t n) -> p t n", n=P), dg,
                                       ALU.mult))
                dve.sem_inc(S["v_gwm"], 1)
                link(dve.scalar_tensor_tensor(tt[:, half[f], :], (b7, b4)[f].rearrange("p (t n) -> p t n", n=P), SCALE,
                                              gwm[:, half[f], :], ALU.mult, ALU.mult))

            def less_max(f):
                c = ct[:, half[f], :]
                link(dve.tensor_reduce(c, tt[:, half[f], :].rearrange("p t (b n) -> p t n b", n=PLACES), AX.X,
                                       ALU.add))
                link(dve.tensor_reduce(cred[:, 0, half[f]], c, AX.X, ALU.max))
                dve.tensor_tensor(c, c, cred[:, 0, half[f]].unsqueeze(2).broadcast_to([P, HALF, PLACES]),
                                  ALU.subtract).then_inc(S["v_csub"], 1)

            def weights(f):
                c = ct[:, half[f], :]
                dve.wait_ge(S["a_cexp"], f + 1)
                link(dve.tensor_reduce(cred[:, 1, half[f]], c, AX.X, ALU.add))
                link(dve.reciprocal(cred[:, 2, half[f]], cred[:, 1, half[f]]))
                link(dve.tensor_scalar(cred[:, 2, half[f]], cred[:, 2, half[f]], sig[:, 4:5], None, ALU.mult))
                link(dve.tensor_tensor(c, c, cred[:, 2, half[f]].unsqueeze(2).broadcast_to([P, HALF, PLACES]),
                                       ALU.mult))
                for t in range(f * HALF, (f + 1) * HALF):
                    ins = dve.tensor_tensor(Aw[:, t, :].rearrange("p (b n) -> p b n", n=PLACES),
                                            ct[:, t, :].unsqueeze(1).broadcast_to([P, P // PLACES, PLACES]),
                                            diag.rearrange("p (b n) -> p b n", n=PLACES), ALU.mult)
                ins.then_inc(S["v_A"], 1)

            masked_scores(0)
            less_max(0)
            masked_scores(1)
            weights(0)
            less_max(1)
            weights(1)
            for f in range(2):
                dve.wait_ge(S["pe_o"], f + 1)
                dve.wait_ge(S["p_hb"], f + 1)
                for i in range(2):
                    hv = hb[:, f * HALF + 2 * i:f * HALF + 2 * i + 2, :]
                    ins = dve.tensor_tensor(hv, o_ps[f][i].rearrange("p (b n) -> p b n", b=2)[:, :, 0:D], hv, ALU.add)
                link(ins)
                norm(hb, f, f + 4, (lambda: take_low_rows(0, 1, (S["pe_h2T"], b0))) if f else None)
            take_low_rows(1, 2, (S["pe_h2T"], b1))
            dve.wait_ge(S["pe_gate"], 2)
            gv = psT[:, 2:4, 0:HALF * 16].rearrange("p f (t n) -> p f t n", n=16)
            by = lambda a: a.rearrange("p (f t) -> p f t", f=2)
            dve.tensor_scalar(by(vcl[:, :]), gv[:, :, :, E], -3.0, 3.0, ALU.max, ALU.min).then_inc(S["v_v"], 1)
            for t in range(TILES):
                ins = dve.max(m8[:, t, :], gv[:, t // HALF, t % HALF, 0:E])
            link(ins)
            for t in range(TILES):
                ins = dve.max_index(i8[:, t, :], m8[:, t, :], gv[:, t // HALF, t % HALF, 0:E])
            link(ins)
            for j in range(TOP):
                ins = dve.tensor_tensor(oh[:, j], i8[:, :, j].unsqueeze(2).broadcast_to([P, TILES, E]),
                                        cst[:, C_EXP:C_EXP + E].unsqueeze(1).broadcast_to([P, TILES, E]),
                                        ALU.is_equal)
            link(ins)
            dve.tensor_tensor(M[:, :, :], oh[:, 0], oh[:, 1], ALU.add).then_inc(S["v_M"], 1)
            dve.tensor_tensor(lg[:, :, :].rearrange("p (f t) e -> p f t e", f=2), gv[:, :, :, 0:E],
                              by(m8[:, :, 0]).unsqueeze(3).broadcast_to([P, 2, HALF, E]),
                              ALU.subtract).then_inc(S["v_lsub"], 1)
            dve.tensor_tensor(best[:, :, :], m8[:, :, 0:TOP].rearrange("p t j -> p j t"),
                              m8[:, :, 0].unsqueeze(1).broadcast_to([P, TOP, TILES]),
                              ALU.subtract).then_inc(S["v_top"], 1)
            dve.wait_ge(S["pe_rank"], 1)
            tot = b5[:, 0:E * TILES]
            pre = b5[:, 256:256 + E * TILES]
            fl = lambda a: a.rearrange("p e t -> p (e t)")
            dve.tensor_copy(before[:, :], pre)
            link(dve.tensor_tensor_scan(fl(incl[:, :, :]), cst[:, C_RESET:C_RESET + E * TILES], tot, 0.0,
                                        ALU.mult, ALU.add))
            dve.tensor_tensor(fl(rank[:, :, :]), fl(incl[:, :, :]), tot, ALU.subtract)
            link(dve.tensor_tensor(gt[:, :, :], incl[:, :, TILES - 1:TILES].broadcast_to([P, E, E]),
                                   cst[:, C_THR:C_THR + E].unsqueeze(1).broadcast_to([P, E, E]), ALU.is_gt))
            dve.tensor_tensor(fl(rank[:, :, :]), fl(rank[:, :, :]), before[:, :], ALU.add)
            link(dve.tensor_reduce(blk[:, 0, :], gt[:, :, :], AX.X, ALU.add))
            link(dve.tensor_tensor_scan(blk[:, 1, :], ones[:, 0:E], blk[:, 0, :], 0.0, ALU.mult, ALU.add))
            link(dve.tensor_tensor(blk[:, 2, :], blk[:, 1, :], blk[:, 0, :], ALU.subtract))
            link(dve.scalar_tensor_tensor(slot[:, :, :], blk[:, 2, :].unsqueeze(2).broadcast_to([P, E, TILES]),
                                          float(P), rank[:, :, :], ALU.mult, ALU.add))
            for j in range(TOP):
                ins = dve.tensor_tensor(ohp[:, j], oh[:, j], slot[:, :, :].rearrange("p e t -> p t e"), ALU.mult)
            link(ins)
            with nc.allow_low_precision("whole numbers below 4096"):
                link(dve.tensor_reduce(sloti[:, 0, :], ohp[:, :, :, :].rearrange("p j t e -> p (j t) e"), AX.X,
                                       ALU.add))
            dve.tensor_scalar(sloti[:, 2, :], sloti[:, 0, :], -P, None, ALU.bitwise_and)
            link(dve.tensor_scalar(sloti[:, 1, :], sloti[:, 0, :], P - 1, None, ALU.bitwise_and))
            dve.wait_ge(S["p_lo"], 2 * E)
            JT = TOP * TILES
            link(dve.tensor_tensor(ohblk[:, :, :], sloti[:, 2, :].unsqueeze(2).broadcast_to([P, JT, BCOLS]),
                                   cst[:, C_BLK128:C_BLK128 + BCOLS].unsqueeze(1).broadcast_to([P, JT, BCOLS]),
                                   ALU.is_equal))
            dve.sem_inc(S["v_blk"], 1)
            dve.tensor_tensor(ohoff[:, :, :], sloti[:, 1, :].unsqueeze(2).broadcast_to([P, JT, P]),
                              offb[:, :].unsqueeze(1).broadcast_to([P, JT, P]),
                              ALU.is_equal).then_inc(S["v_tabr"], 1)
            link(dve.tensor_tensor(emt[:, :, :], cst[0:1, C_BLK:C_BLK + BCOLS].unsqueeze(2).broadcast_to([1, BCOLS, E]),
                                   blk[0:1, 1, :].unsqueeze(1).broadcast_to([1, BCOLS, E]), ALU.is_ge))
            dve.tensor_reduce(emtf[:, :], emt[:, :, :], AX.X, ALU.add)
            dve.tensor_scalar(nblk[:, 1:2], blk[0:1, 1, E - 1:E], -2.0, None, ALU.add)
            link(dve.tensor_copy(nblk[:, 0:1], blk[0:1, 1, E - 1:E]))
            dve.tensor_copy(emap[:, :], emtf[:, :]).then_inc(S["v_emap"], 1)
            dve.wait_ge(S["pe_tab"], 1)
            link(dve.tensor_copy(tab[:, 0:2, :].rearrange("p a b -> p (a b)"), b2k[:, 0:2 * BCOLS]))
            link(dve.scalar_tensor_tensor(tab[:, 2, :], tab[:, 1, :], float(P), tab[:, 0, :], ALU.mult, ALU.add))
            link(dve.tensor_scalar(gidr[:, :], tab[:, 2, :], -1.0, 0.0, ALU.add, ALU.max))
            dve.tensor_scalar(gid[:, :], gidr[:, :], TOKENS - 1, None, ALU.bitwise_and).then_inc(S["v_gid"], 1)
            link(dve.tensor_scalar(tab[:, 3, :], tab[:, 0, :], 0.0, float(FAR), ALU.is_equal, ALU.mult))
            dve.scalar_tensor_tensor(sid[:, :], tab[:, 2, :], -1.0, tab[:, 3, :], ALU.add,
                                     ALU.add).then_inc(S["v_tab"], 1)
            dve.wait_ge(S["a_lexp"], 1)
            dve.wait_ge(S["a_top"], 1)
            link(dve.tensor_reduce(gate_st[:, 1, :], pr[:, :, :], AX.X, ALU.add))
            link(dve.reciprocal(gate_st[:, 2, :], gate_st[:, 1, :]))
            link(dve.tensor_tensor(best[:, :, :], best[:, :, :],
                                   gate_st[:, 2, :].unsqueeze(1).broadcast_to([P, TOP, TILES]), ALU.mult))
            link(dve.tensor_tensor(gate_st[:, 0, :], best[:, 0, :], best[:, 1, :], ALU.add))
            link(dve.reciprocal(gate_st[:, 1, :], gate_st[:, 0, :]))
            link(dve.tensor_tensor(cw[:, :, :], best[:, :, :],
                                   gate_st[:, 1, :].unsqueeze(1).broadcast_to([P, TOP, TILES]), ALU.mult))
            for j in range(TOP):
                ins = dve.tensor_tensor(combt[:, j], oh[:, j], cw[:, j, :].unsqueeze(2).broadcast_to([P, TILES, E]),
                                        ALU.mult)
            link(ins)
            dve.tensor_tensor(comb[:, :, :], combt[:, 0], combt[:, 1], ALU.add).then_inc(S["v_comb"], 1)
            dve.wait_ge(S["d_v"], 32)
            link(dve.tensor_scalar(v2r[0:IMAGES, :], v2[0:IMAGES, :], -2.0, None, ALU.add))
            link(dve.tensor_scalar(v2r[IMAGES:P, :], v2[IMAGES:P, ::-1], -2.0, None, ALU.add))
            v4 = v2r[:, :].rearrange("p (a b) -> p a b", b=2)
            a4 = add[:, :, :].rearrange("p (a b) c -> p a b c", b=2)
            dve.tensor_copy(a4[:, :, 0, 0], v4[:, :, 0])
            dve.tensor_scalar(a4[:, :, 1, 0], v4[:, :, 1], -1.0, None, ALU.mult)
            link(dve.memset(add[:, :, 1], -1.0))
            link(dve.tensor_copy(ch[:, 0, :], add[:, 0, :]))

            def fraction(start, stop):
                for n in range(start, stop):
                    link(dve.tensor_tensor_reduce(chj[:, n, :], ch[:, n - 1, :], ch[:, n - 1, :], 1.0, 0.0, ALU.mult,
                                                  ALU.add, chd[:, 0, n:n + 1]))
                    link(dve.reciprocal(chd[:, 1, n:n + 1], chd[:, 0, n:n + 1]))
                    link(dve.scalar_tensor_tensor(ch[:, n, :], ch[:, n - 1, :], chd[:, 1, n:n + 1], add[:, n, :],
                                                  ALU.mult, ALU.add))

            m = dve.value_load(nblk[0:1, 1:2], min_val=TOP * TOKENS // P - 2, max_val=BLOCKS - 2)

            def low_x(b):
                dve.wait_ge(S["a_xh"], b * 3 + 2)
                dve.tensor_tensor(xal[:, :], b7[:, 0:P], xah[:, :].bitcast(F32), ALU.subtract)
                dve.tensor_tensor(xbb[HI:P, :], b7[0:HI, P:2 * P], xbb[0:HI, :].bitcast(F32),
                                  ALU.subtract).then_inc(S["v_xl"], 1)

            def take_h(b):
                for part in range(2):
                    dve.wait_ge(S["pe_hgT"], b * 2 + part + 1)
                    dve.tensor_copy(hT[:, 3 * part:3 * part + 3, :].rearrange("p c n -> p (c n)"),
                                    (b2k, b3)[part][:, 0:FH]).then_inc(S["v_hgT"], 1)

            def take_y(b):
                dve.wait_ge(S["pe_y"], b + 1)
                dve.tensor_copy(ysb[:, :], b4[:, 0:D]).then_inc(S["v_y"], 1)
            fraction(1, 5)
            low_x(0)
            fraction(5, 11)
            low_x(1)
            fraction(11, 13)
            take_h(0)
            low_x(2)
            fraction(13, 14)
            take_y(0)
            take_h(1)
            low_x(3)
            fraction(14, PLACES)
            dve.wait_ge(S["d_scatter"], 16)
            take_y(1)
            take_h(2)
            low_x(4)
            c4 = ch[:, :, :].rearrange("p (a b) c -> p a b c", b=2)
            link(dve.tensor_scalar(c4[:, :, 1, 0], c4[:, :, 1, 0], -1.0, None, ALU.mult))
            link(dve.tensor_copy(back[:, :, :], ch[IMAGES:P, ::-1, :]))
            link(dve.tensor_tensor(zz[:, 0:2, :].rearrange("p c n -> p n c"), ch[0:IMAGES, :, :], back[:, :, :],
                                   ALU.add))
            dve.tensor_tensor(zz[:, 0, :], zz[:, 0, :], v2r[0:IMAGES, :], ALU.subtract)
            link(dve.tensor_scalar(zz[:, 1, :], zz[:, 1, :], 1.0, None, ALU.add))
            link(dve.tensor_tensor(z[:, :, :], zz[:, 0:2, :], zz[:, 0:2, :], ALU.mult))
            link(dve.tensor_tensor(zz[:, 2, :], z[:, 0, :], z[:, 1, :], ALU.add))
            link(dve.reciprocal(zz[:, 3, :], zz[:, 2, :]))
            dve.tensor_tensor(z[:, 0, :], zz[:, 0, :], zz[:, 3, :], ALU.mult)
            link(dve.scalar_tensor_tensor(z[:, 1, :], zz[:, 1, :], -1.0, zz[:, 3, :], ALU.mult, ALU.mult))
            link(dve.tensor_scalar(z[:, :, :], z[:, :, :], -10.0, 10.0, ALU.max, ALU.min))
            dve.sem_inc(S["v_feat"], 1)
            dve.wait_ge(S["d_scatter"], 32)
            take_y(2)
            with dve.Fori(2, m) as i:
                take_h(i + 1)
                low_x(i + 3)
                dve.wait_ge(S["d_scatter"], i * 16 + 16)
                take_y(i + 1)
            take_h(m + 1)
            dve.wait_ge(S["d_scatter"], m * 16 + 16)
            take_y(m + 1)
            for t in range(TILES):
                q = t // 2
                if t % 2 == 0:
                    dve.wait_ge(S["pe_base"], q + 1)
                    pb = (b0, b1, b5, b6)[q].rearrange("p (b n) -> p b n", b=2)[:, :, 0:D]
                    dve.tensor_tensor(hb[:, t:t + 2, :], pb, hb[:, t:t + 2, :], ALU.add).then_inc(S["v_base"], 1)
            for q in range(4):
                if q == POOL_PAIR:
                    continue
                dve.wait_ge(S["v_base"], 4)
                dve.wait_ge(S[f"d_yb{q}"], 32)
                for j in range(TOP):
                    for t in (2 * q, 2 * q + 1):
                        ins = dve.scalar_tensor_tensor(hb[:, t, :], yb[:, j, t, :], cw[:, j, t:t + 1], hb[:, t, :],
                                                       ALU.mult, ALU.add)
                    if j == 0:
                        link(ins)
                ins.then_inc(S["v_out"], 1)

        @block.tensor
        def _(pe):
            tview = psT[:, :, :].rearrange("p a (b n) -> p a b n", b=2)

            def tok(t):
                return slice(t * P, (t + 1) * P)

            for c in range(CHUNKS):
                k = CROWS[c]
                pe.wait_ge(d_x[c], 16)
                pe.wait_ge(S["v_weff"], c + 1)
                for t in range(TILES):
                    pe.matmul(tview[:, t // 2, t % 2, 0:D + 1], X[0:k, c, tok(t)], weff[0:k, c, :],
                              start=(c == 0 and t % 2 == 0), stop=(c == CHUNKS - 1), skip_group_check=True)
            pe.wait_ge(S["s_cst"], 16)
            pe.wait_ge(S["v_sq"], CHUNKS)
            for t in range(TILES):
                mm = pe.matmul(b4[:, t:t + 1], sqsum[:, tok(t)], ones[:, 0:1], start=True, stop=True)
            mm.then_inc(S["t_sum"], 1)
            for c in range(CHUNKS):
                k = CROWS[c]
                mm = pe.matmul(b5[:, 0:D], ones[0:k], weff[0:k, c, 0:D], start=(c == 0), stop=(c == CHUNKS - 1))
            mm.then_inc(S["t_col"], 1)
            pe.wait_ge(S["p_acc"], CHUNKS + SHIFTS - 1)
            pe.matmul(b6[:, 0:D], ones, bacc[:, 0, :], start=True, stop=True).then_inc(S["t_bias"], 1)
            pe.wait_ge(S["s_qkv"], 32)
            V = 2 * D
            pe.transpose(b7[:, 0:LO], wqa[:, V:V + LO], ident)
            pe.transpose(b7[:, LO:D + 1], wqb[:, V:V + LO], ident[0:HI + 1, 0:HI + 1])
            pe.transpose(b7[0:HI, 256:256 + LO], wqa[:, V + LO:V + D], ident)
            pe.transpose(b7[0:HI, 256 + LO:256 + D + 1], wqb[:, V + LO:V + D],
                         ident[0:HI + 1, 0:HI + 1]).then_inc(S["pe_wvT"], 1)
            pe.wait_ge(S["a_wvT"], 2)
            pe.wait_ge(S["s_wp"], 32)
            pe.matmul(b7[:, 0:VG], wvTa[:, 0:LO], wpa[:, :], start=True, stop=False)
            pe.matmul(b7[:, 0:VG], wvTb[:, 0:LO], wpb[:, :], start=False, stop=True)
            pe.matmul(b7[0:HI + 1, 256:256 + VG], wvTa[:, LO:D + 1], wpa[:, :], start=True, stop=False,
                      skip_group_check=True)
            pe.matmul(b7[0:HI + 1, 256:256 + VG], wvTb[:, LO:D + 1], wpb[:, :], start=False, stop=True,
                      skip_group_check=True).then_inc(S["pe_wg"], 1)
            pe.wait_ge(S["a_wg"], 2)
            pe.wait_ge(S["p_ones"], 2)
            def turn_rows(f, n, low):
                pe.wait_ge(S["v_hnb"], n)
                pe.wait_ge(S["a_hn"], n * (HALF - SPLIT))
                for t in range(HALF):
                    pe.transpose((b7, b4)[f][:, tok(t)], hn[:, f * HALF + t, 0:LO], ident)
                for t in range(HALF):
                    mm = pe.transpose(low[0:HI, tok(t)], hn[:, f * HALF + t, LO:D], ident)
                return mm

            turn_rows(0, 1, b6).then_inc(S["pe_hT"], 1)
            for f in range(2):
                pe.wait_ge(S["a_hT"], f + 1)
                pe.wait_ge(S["v_hT"], f + 1)
                for i, (dst, a, b) in enumerate(((b0, 0, LO), (b1, LO, 2 * LO))):
                    if f > 0:
                        pe.wait_ge(S["a_q"], i + 1)
                    pe.matmul(dst, wqa[:, a:b], hnTa[:, cols[f]], start=True, stop=False)
                    pe.matmul(dst, wqb[:, a:b], hnTb[:, cols[f]], start=False, stop=True).then_inc(S["pe_qk"], 1)
                if f > 0:
                    pe.wait_ge(S["v_qk"], f)
                pe.matmul(b5, wqa[:, 2 * LO:2 * D], hnTa[:, cols[f]], start=True, stop=False)
                pe.matmul(b5, wqb[:, 2 * LO:2 * D], hnTb[:, cols[f]], start=False, stop=True).then_inc(S["pe_qk"], 1)
                if f == 0:
                    turn_rows(1, 2, b6).then_inc(S["pe_hT"], 1)
                pe.wait_ge(S["v_h"], 2)
                if f > 0:
                    pe.wait_ge(S["a_vp"], f)
                for t in range(HALF):
                    dst = vg[:, t // 2, t % 2, 0:VG]
                    T = f * HALF + t
                    pe.matmul(dst, hnTa[:, tok(T)], wga[:, :], start=True, stop=False)
                    mm = pe.matmul(dst, hnTb[:, tok(T)], wgb[:, :], start=False, stop=True)
                mm.then_inc(S["pe_vg"], 1)
            for f in range(2):
                pe.wait_ge(S["a_q"], 2 * f + 2)
                pe.wait_ge(S["v_qk"], f + 1)
                for t in range(HALF):
                    T = f * HALF + t
                    dst = (b7, b4)[f][:, tok(t)]
                    pe.matmul(dst, q0[:, tok(T)], k0[:, tok(T)], start=True, stop=False)
                    pe.matmul(dst, q1[:, tok(T)], k1[:, tok(T)], start=False, stop=True)
            for f in range(2):
                pe.wait_ge(S["v_gw"], f + 1)
                if f == 0:
                    pe.wait_ge(S["a_q"], 4)
                for t in range(HALF):
                    mm = pe.transpose((b0, b1)[f][0:GROUPS, tok(t)], gw[:, f * HALF + t, :], ident)
                mm.then_inc(S["pe_gwT"], 1)
            for f in range(2):
                pe.wait_ge(S["a_gwT"], f + 1)
                for t in range(HALF):
                    T = f * HALF + t
                    mm = pe.matmul((b6, b5)[f][:, tok(t)], gwT[:, tok(T)], gwT[:, tok(T)], start=True, stop=True)
                mm.then_inc(S["pe_gw"], 1)

            def attended(T):
                return o_ps[T // HALF][T % HALF // 2][:, (T % 2) * 256:(T % 2) * 256 + D]

            for f in range(2):
                pe.wait_ge(S["v_gwm"], f + 1)
                pe.wait_ge(S["a_vp"], 2)
                pe.wait_ge(S["a_vps"], f + 1)
                for T in range(f * HALF, (f + 1) * HALF):
                    pe.matmul(attended(T), gwm[:, T, :], vps[:, T, :], start=(T % 2 == 0), stop=False,
                              skip_group_check=True)
            for f in range(2):
                pe.wait_ge(S["v_A"], f + 1)
                for t in range(HALF):
                    mm = pe.transpose((b0, b1)[f][:, tok(t)], Aw[:, f * HALF + t, :], ident)
                mm.then_inc(S["pe_AT"], 1)
                pe.wait_ge(S["a_AT"], f + 1)
                pe.wait_ge(S["a_vp"], 2)
                for t in range(HALF):
                    T = f * HALF + t
                    mm = pe.matmul(attended(T), AT[:, T, :], vp[:, T, :], start=False, stop=True,
                                   skip_group_check=True)
                mm.then_inc(S["pe_o"], 1)
            pe.wait_ge(S["s_gate"], 32)

            def gate_logits(tiles):
                for T in tiles:
                    t, dst = T % HALF, gate_ps[T // HALF]
                    pe.matmul(dst[:, t * 16:t * 16 + E + 1], hnTa[:, tok(T)], wgate[:, :], start=True, stop=False)
                    mm = pe.matmul(dst[:, t * 16:t * 16 + E + 1], hnTb[:, tok(T)], wgateb[:, :], start=False,
                                   stop=True)
                return mm

            turn_rows(0, 3, b0).then_inc(S["pe_h2T"], 1)
            pe.wait_ge(S["a_hT"], 3)
            pe.wait_ge(S["v_hT"], 3)
            gate_logits(range(2))
            turn_rows(1, 4, b1).then_inc(S["pe_h2T"], 1)
            gate_logits(range(2, HALF)).then_inc(S["pe_gate"], 1)
            pe.wait_ge(S["a_hT"], 4)
            pe.wait_ge(S["v_hT"], 4)
            gate_logits(range(HALF, TILES)).then_inc(S["pe_gate"], 1)
            pe.wait_ge(S["v_v"], 1)
            pe.transpose(b4[0:TILES, 0:P], vcl[:, :], ident).then_inc(S["pe_vT"], 1)
            pe.wait_ge(S["v_M"], 1)
            mo = M[:, :, :].rearrange("p t e -> p e t")
            pe.matmul(b5[:, 0:E * TILES], ones, mo, start=True, stop=True)
            pe.matmul(b5[:, 256:256 + E * TILES], cst[:, C_TRI:C_TRI + P], mo, start=True,
                      stop=True).then_inc(S["pe_rank"], 1)
            pe.wait_ge(S["v_tabr"], 1)
            pe.wait_ge(S["a_tabr"], 1)
            pe.wait_ge(S["p_tabr"], 1)
            JT = TOP * TILES
            for r in range(JT):
                mm = pe.matmul(b2k[:, 0:2 * BCOLS], ohoff[:, r, :], tabr[:, r, :, :].rearrange("p a b -> p (a b)"),
                               start=(r == 0), stop=(r == JT - 1))
            mm.then_inc(S["pe_tab"], 1)
            pe.wait_ge(S["v_comb"], 1)
            for f in range(2):
                for t in range(HALF):
                    mm = pe.transpose((b5, b6)[f][0:E, tok(t)], comb[:, f * HALF + t, :], ident)
                mm.then_inc(S["pe_combT"], 1)
            pe.wait_ge(S["p_lo"], 2 * E)
            pe.wait_ge(S["d_bias"], 32)
            pe.wait_ge(S["s_w2"], 16 * E)
            pe.wait_ge(S["v_emap"], 1)
            n = pe.value_load(nblk[0:1, 0:1], min_val=TOP * TOKENS // P, max_val=BLOCKS)

            def expert(b):
                return pe.value_load(emap[0:1, bass.ds(b, 1)], min_val=0, max_val=E - 1)

            first = expert(0)
            last_expert = pe.alloc_register("last_expert")
            pe.reg_mov(last_expert, first)

            def turn_x(rows):
                pe.transpose(b7[:, 0:P], rows[:, 0:LO], ident)
                pe.transpose(b7[0:HI, P:2 * P], rows[:, LO:D], ident).then_inc(S["pe_xT"], 1)

            def up(part, e, b):
                dst = (b0, b1)[part][:, 0:FH]
                fs = slice(part * FH, (part + 1) * FH)
                pe.matmul(dst, xah[:, :], w1ah[:, bass.ds(e, 1), fs], start=True, stop=False)
                pe.matmul(dst, xah[:, :], w1al[:, bass.ds(e, 1), fs], start=False, stop=False)
                pe.matmul(dst, xbh[0:HI + 2, :], w1bl[:, bass.ds(e, 1), fs], start=False, stop=False)
                if part == 0:
                    pe.wait_ge(S["v_xl"], b + 1)
                pe.matmul(dst, xal[:, :], w1ah[:, bass.ds(e, 1), fs], start=False, stop=False)
                pe.matmul(dst, xbb[:, :], w1bh[:, bass.ds(e, 1), fs], start=False,
                          stop=True).then_inc(S[f"pe_up{part}"], 1)

            def turn_h():
                for c in range(FC):
                    part = c // 3
                    mm = pe.transpose((b2k, b3)[part][:, (c % 3) * P:(c % 3 + 1) * P], hg[:, c * P:(c + 1) * P],
                                      ident)
                    if c % 3 == 2:
                        mm.then_inc(S["pe_hgT"], 1)

            def down(e):
                for c in range(FC):
                    mm = pe.matmul(b4[:, 0:D], hT[:, c, :], w2s[:, bass.ds(e * FC + c, 1), :], start=(c == 0),
                                   stop=(c == FC - 1))
                mm.then_inc(S["pe_y"], 1)

            pe.wait_ge(S["d_first"], 16)
            pe.wait_ge(S["a_vT"], 1)
            turn_x(xg_first)
            pe.wait_ge(S["a_xh"], 3)
            up(0, first, 0)
            up(1, first, 0)
            pe.wait_ge(S["d_gather"], 16)
            turn_x(xg)
            with pe.Fori(1, n) as i:
                e_down = pe.snap(last_expert, min_val=0, max_val=E - 1)
                e_up = expert(i)
                pe.reg_mov(last_expert, e_up)
                pe.wait_ge(S["a_xh"], i * 3 + 3)
                up(0, e_up, i)
                pe.wait_ge(S["a_ge"], i * 2)
                pe.wait_ge(S["v_tab"], 1)
                turn_h()
                up(1, e_up, i)
                pe.wait_ge(S["d_gather"], i * 16 + 16)
                turn_x(xg)
                pe.wait_ge(S["v_hgT"], i * 2)
                down(e_down)
            pe.wait_ge(S["a_ge"], n * 2)
            turn_h()
            pe.wait_ge(S["v_hgT"], n * 2)
            down(pe.snap(last_expert, min_val=0, max_val=E - 1))
            pe.wait_ge(S["a_combT"], 2)
            pe.wait_ge(S["s_b2"], 16)
            pe.wait_ge(S["v_sw"], 1)
            pe.wait_ge(S["d_feat"], 32)
            for t in range(TILES):
                dst = (b0, b1, b5, b6)[t // 2].rearrange("p (b n) -> p b n", b=2)[:, t % 2, 0:D]
                pe.matmul(dst, combT[:, tok(t)], b2s[:, :], start=True, stop=False)
                mm = pe.matmul(dst, feat[:, tok(t)], sw[:, :], start=False, stop=True)
                if t % 2:
                    mm.then_inc(S["pe_base"], 1)


def constants():
    import numpy as np
    c = np.zeros((P, C_ALL), np.float32)
    p = np.arange(P)
    c[:, C_ID:C_ID + P] = np.eye(P)
    c[:, C_DIAG:C_DIAG + P] = p[:, None] // PLACES == p[None, :] // PLACES
    c[:, C_TRI:C_TRI + P] = p[:, None] < p[None, :]
    c[:, C_ONE:C_ONE + P] = 1
    c[:, C_EXP:C_EXP + E] = np.arange(E)
    c[:, C_THR:C_THR + E] = np.arange(E) * P
    c[:, C_RESET:C_RESET + E * TILES] = np.arange(E * TILES) % TILES != 0
    c[:, C_BLK:C_BLK + BCOLS] = np.arange(BCOLS)
    c[:, C_BLK128:C_BLK128 + BCOLS] = np.arange(BCOLS) * P
    c[:, C_TILE:C_TILE + TOP * TILES] = np.arange(TOP * TILES)
    c[:, C_PART] = p + 1
    c[:, C_OFF:C_OFF + P] = p
    return c


def times_read():
    import numpy as np
    c = np.zeros((P, CHUNKS), np.float32)
    u = np.arange(16)
    side = (u < 15).astype(np.float32) + (u > 0)
    times = np.broadcast_to((1 + side[:, None] + side[None, :])[:, :, None], (16, 16, 3)).reshape(INNER, P)
    c[:, :INNER] = times.T
    c[:EDGE, INNER:] = 1
    return c


def lay_pixels(x):
    import numpy as np
    x = np.asarray(x)
    padded = np.pad(x, ((0, 0), (0, 0), (1, 1), (1, 1)))
    a = np.zeros((CHUNKS, P, TOKENS), x.dtype)
    a[:INNER] = x.reshape(64, 3, 4, 16, 4, 16).transpose(3, 5, 1, 0, 2, 4).reshape(INNER, P, TOKENS)
    inner = padded[:, :, 1:65, 1:65]
    rows = lambda z: z.reshape(64, 3, 4, 16, 4).transpose(3, 1, 0, 2, 4).reshape(48, TOKENS)
    colm = lambda z: z.reshape(64, 3, 4, 4, 16).transpose(4, 1, 0, 2, 3).reshape(48, TOKENS)
    left = rows(padded[:, :, 1:65, 0:64:16])
    right = rows(padded[:, :, 1:65, 17:66:16])
    above = colm(padded[:, :, 0:64:16, 1:65])
    below = colm(padded[:, :, 17:66:16, 1:65])
    a[INNER, :EDGE] = np.concatenate([left, right])
    a[INNER + 1, :EDGE] = np.concatenate([above, below])
    return a


def lay_rows(w):
    import numpy as np
    w = np.asarray(w)
    w = w.reshape(16, 16, SHIFTS, 3, -1)
    n = w.shape[-1]
    a = np.zeros((16, 16, 3, SHIFTS, n), w.dtype)
    a[:, :, :, 0] = w[:, :, 0]
    a[:, :15, :, 1] = w[:, 1:, 1]
    a[:, 1:, :, 2] = w[:, :15, 2]
    a[:15, :, :, 3] = w[1:, :, 3]
    a[1:, :, :, 4] = w[:15, :, 4]
    edge = np.stack([w[:, 0, 1], w[:, 15, 2], w[0, :, 3], w[15, :, 4]]).reshape(2, EDGE, n)
    return a.reshape(INNER, P, SHIFTS, n), edge


def kernel(**inputs):
    import numpy as _np
    import concourse.bacc as _bacc
    from concourse import mybir as _mybir
    from concourse.bass_utils import run_bass_kernel_spmd as _run

    g = {k: _np.asarray(v) for k, v in inputs.items()}
    w_in, w_edge = lay_rows(g["L0_tok_W"])

    def vec(v):
        a, b = lay_rows(v)
        full = _np.zeros((CHUNKS, P, SHIFTS), v.dtype)
        full[:INNER] = a[..., 0]
        full[INNER:, :EDGE, 0] = b[..., 0]
        return full.transpose(1, 0, 2)

    qkv = _np.concatenate([g["L0_attn_W_qkv"], g["L0_attn_b_qkv"][None]])
    qkv = _np.concatenate([qkv[:, 0:LO], qkv[:, D:D + LO], qkv[:, LO:D], qkv[:, D + LO:]], 1)
    wpg = _np.concatenate([g["L0_attn_W_proj"], g["L0_attn_W_gp"]], 1)
    gate = _np.concatenate([_np.concatenate([g["L0_ffn_gate_w"], g["L0_ffn_v_w"][:, None]], 1),
                            _np.concatenate([g["L0_ffn_gate_b"], g["L0_ffn_v_b"].reshape(1)])[None]])
    spec = _np.concatenate([g["L0_ffn_out_w"], g["L0_ffn_out_b"][None]])
    laid = {
        "pixels": lay_pixels(g["x"]), "mult_w": w_in, "edge_w": w_edge,
        "gammas_betas": _np.concatenate([vec(g["L0_tok_gamma"]).reshape(P, -1), vec(g["L0_tok_beta"]).reshape(P, -1),
                                         times_read()], 1),
        "tok_b": g["L0_tok_b"], "wqkv": qkv, "wpg": wpg,
        "b_proj": g["L0_attn_b_proj"], "alpha": g["L0_attn_alpha"].reshape(1), "gate": gate, "w1": g["L0_ffn_w1"],
        "bias1": g["L0_ffn_b1"].reshape(BR, E * F // BR),
        "w2": g["L0_ffn_w2"], "b2": g["L0_ffn_b2"], "spec_w": spec, "bk": g["L0_ffn_bk_scale"], "consts": constants(),
    }
    nc = _bacc.Bacc("TRN2", target_bir_lowering=False, num_devices=1)
    arrays, args = {}, []
    for name, a in laid.items():
        a = _np.ascontiguousarray(a)
        arrays[f"in_{name}_dram"] = a
        args.append(nc.dram_tensor(f"in_{name}_dram", a.shape, _mybir.dt.from_np(a.dtype), kind="ExternalInput").ap())
    args.append(nc.dram_tensor("out_0_dram", (TOKENS, D), _mybir.dt.float32, kind="ExternalOutput").ap())
    tower(nc, *args)
    r = _run(nc, [arrays], core_ids=[0])
    return r.results[0]["out_0_dram"].reshape(IMAGES, PLACES, D)
```

```python
from contextlib import ExitStack

import concourse.bass as bass
from concourse import mybir

F32 = mybir.dt.float32
F32R = mybir.dt.float32r
BF16 = mybir.dt.bfloat16
I32 = mybir.dt.int32
U32 = mybir.dt.uint32
ACT = mybir.ActivationFunctionType
ALU = mybir.AluOpType
AX = mybir.AxisListType

P = 128
IMAGES, PLACES, D = 64, 16, 192
TOKENS = IMAGES * PLACES
TILES = TOKENS // P
HALF = TILES // 2
RING = 4
SPLIT = 2
HT = HALF * P
LO = 128
HI = D - LO
SHIFTS = 5
FEATURES = 3840
CHUNKS = 8
INNER = 6
EDGE = 96
CROWS = [P] * INNER + [EDGE] * 2
GROUPS = 49
VG = D + GROUPS
VGE = VG + VG % 2
E, F = 8, 768
FC = F // P
FH = F // 2
TOP = 2
BLOCKS = (TOP * TOKENS - E) // P + E
BCOLS = BLOCKS + 1
FAR = 2 * TOP * TOKENS
RAW = 3
BY_DVE = (4, 8)
BR = 96
EPS = 1e-5
SCALE = float(D) ** -0.5

C_ID, C_DIAG, C_TRI, C_ONE = 0, 128, 256, 384
C_EXP = 512
C_THR = C_EXP + E
C_RESET = C_THR + E
C_BLK = C_RESET + E * TILES
C_BLK128 = C_BLK + BCOLS
C_TILE = C_BLK128 + BCOLS
C_PART = C_TILE + TOP * TILES
C_OFF = C_PART + 1
C_ALL = C_OFF + P


def tower(nc, pixels, mult_w, edge_w, gammas_betas, tok_b, wqkv, wpg, b_proj, alpha, gate, w1, bias1, w2, b2, spec_w, bk,
          consts, out):
    hn2_rows = nc.dram_tensor("hn2_rows", (TOKENS, D), F32, kind="Internal").ap()
    sums = nc.dram_tensor("sums", (TOKENS, D), F32, kind="Internal").ap()

    with ExitStack() as ctx:
        def sb(name, shape, dt=F32):
            return ctx.enter_context(nc.sbuf_tensor(name, shape, dt))

        def sem(name):
            return ctx.enter_context(nc.semaphore(name))

        bank = [ctx.enter_context(nc.psum_tensor(f"bank{i}", [P, 512], F32)) for i in range(5, 8)]
        psT = ctx.enter_context(nc.psum_tensor("psT", [P, 4, 512], F32))
        psE = ctx.enter_context(nc.psum_tensor("psE", [P, 512], F32))
        b0, b1, b2k, b3 = (psT[:, i, :] for i in range(4))
        b4 = psE[:, :]
        b5, b6, b7 = (t[:, :] for t in bank)

        cst = sb("cst", [P, C_ALL])
        sizes = [2 * TOKENS, TOKENS, 2 * D, CHUNKS * (D + 1), SHIFTS * D, SHIFTS * D, TILES * D]
        with ExitStack() as lent:
            X = lent.enter_context(nc.sbuf_tensor("X", [P, CHUNKS, TOKENS], F32))
            early = lent.enter_context(nc.sbuf_tensor("early", [P, sum(sizes)], F32))
            tah, tal, tbb, tbh = (lent.enter_context(nc.sbuf_tensor(n, [P, TOKENS], F32R))
                                  for n in ("tah", "tal", "tbb", "tbh"))
            qah, qal, qbb, qbl = (lent.enter_context(nc.sbuf_tensor(n, [P, 2 * D], F32R))
                                  for n in ("qah", "qal", "qbb", "qbl"))
            gah, gal, gbb, gbl = (lent.enter_context(nc.sbuf_tensor(n, [P, VGE], F32R))
                                  for n in ("gah", "gal", "gbb", "gbl"))
        shared = sb("shared", [P, max(RAW * F, TOP * TILES * (P // 2 + BCOLS + BCOLS))])
        raw = shared[:, 0:RAW * F].rearrange("p (a f) -> p a f", a=RAW)
        w1ah = sb("w1ah", [P, E, F], F32R)
        w1al = sb("w1al", [P, E, F], F32R)
        w1bh = sb("w1bh", [P, E, F], F32R)
        w1bl = sb("w1bl", [HI + 2, E, F], F32R)
        b1r = sb("b1r", [BR, E * F // BR])
        b1h = sb("b1h", [BR, E * F // BR], F32R)
        b1l = sb("b1l", [BR, E * F // BR], F32R)
        starts = [sum(sizes[:i]) for i in range(len(sizes) + 1)]
        part = [early[:, starts[i]:starts[i + 1]] for i in range(len(sizes))]
        Xsq = part[0].rearrange("p (a n) -> p a n", a=2)
        sqsum = part[1]
        We = part[2].rearrange("p (a n) -> p a n", a=2)[0:EDGE]
        weff = part[3].rearrange("p (a n) -> p a n", a=CHUNKS)
        bprod = part[4].rearrange("p (a n) -> p a n", a=SHIFTS)
        bacc = part[5].rearrange("p (a n) -> p a n", a=SHIFTS)
        ttmp = part[6].rearrange("p (a n) -> p a n", a=TILES)
        gb = sb("gb", [P, (2 * SHIFTS + 1) * CHUNKS])
        gam, bet = (gb[:, i * CHUNKS * SHIFTS:(i + 1) * CHUNKS * SHIFTS].rearrange("p (c s) -> p c s", c=CHUNKS)
                    for i in range(2))
        mult = gb[:, 2 * CHUNKS * SHIFTS:]
        tokb = sb("tokb", [P, D])
        g_sb = sb("g_sb", [P, D])
        bw_sb = sb("bw_sb", [P, D])
        st = sb("st", [P, 12, TILES])
        takes = [4 * TILES * P, TILES * D, TILES * D, TILES * GROUPS, TOKENS, 3 * D]
        attn = sb("attn", [P, max(sum(takes), E * FC * D)])
        spot = [attn[:, sum(takes[:i]):sum(takes[:i + 1])] for i in range(len(takes))]
        w2s = attn[:, 0:E * FC * D].rearrange("p (a n) -> p a n", n=D)
        h = spot[1].rearrange("p (t d) -> p t d", t=TILES)
        hb = sb("hb", [P, TILES, D])
        hn = sb("hn", [P, TILES, D])
        bn6 = sb("bn6", [P, TILES, 6])
        mv = sb("mv", [P, TILES, 2])
        rstd = sb("rstd", [P, TILES])
        var = sb("var", [P, TILES])
        sd = sb("sd", [P, TILES])
        nmr = sb("nmr", [P, TILES])
        hnTa = sb("hnTa", [P, TOKENS])
        hnTb = sb("hnTb", [HI + 1, TOKENS])
        wqa = spot[5]
        wqb = sb("wqb", [HI + 1, 3 * D])
        wpa = sb("wpa", [P, VG])
        wpb = sb("wpb", [HI, VG])
        wvTa = sb("wvTa", [P, D + 1])
        wvTb = sb("wvTb", [HI, D + 1])
        wga = sb("wga", [P, VG])
        wgb = sb("wgb", [HI + 1, VG])
        bpr = sb("bpr", [P, D])
        qk = sb("qk", [P, 4, TOKENS])
        q0, k0, q1, k1 = qk[:, 0], qk[:, 1], qk[0:HI, 2], qk[0:HI, 3]
        hg = qk[:, 0, 0:F]
        hT = qk[:, 1, 0:F].rearrange("p (c n) -> p c n", n=P)
        rows_last = qk[0:E + 3, 2]
        vp = spot[2].rearrange("p (t d) -> p t d", t=TILES)
        vps = h
        gw = spot[3].rearrange("p (t g) -> p t g", t=TILES)
        gred = sb("gred", [P, 3, TILES])
        gwT = spot[4][0:GROUPS]
        maps = spot[0].rearrange("p (a t n) -> p a t n", a=4, t=TILES)
        gwm, tt, Aw, AT = (maps[:, i] for i in range(4))
        Wt = maps[:, :, :, :].rearrange("p a t n -> p (a t n)")[:, 0:RING * SHIFTS * D].rearrange(
            "p (a s n) -> p a s n", a=RING, s=SHIFTS)
        ct = sb("ct", [P, TILES, PLACES])
        cred = sb("cred", [P, 3, TILES])
        sig = sb("sig", [P, 5])
        wgate = sb("wgate", [P, E + 1])
        wgateb = sb("wgateb", [HI + 1, E + 1])
        vcl = sb("vcl", [P, TILES])
        vT = sb("vT", [TILES, P])
        lg = sb("lg", [P, TILES, E])
        gate_st = sb("gate_st", [P, 3, TILES])
        pr = sb("pr", [P, TILES, E])
        m8 = sb("m8", [P, TILES, 8])
        i8 = sb("i8", [P, TILES, 8], U32)
        best = sb("best", [P, TOP, TILES])
        cw = sb("cw", [P, TOP, TILES])
        oh = sb("oh", [P, TOP, TILES, E])
        ohp = sb("ohp", [P, TOP, TILES, E])
        M = sb("M", [P, TILES, E])
        incl = sb("incl", [P, E, TILES])
        before = sb("before", [P, E * TILES])
        rank = sb("rank", [P, E, TILES])
        gt = sb("gt", [P, E, E])
        blk = sb("blk", [P, 3, E])
        slot = sb("slot", [P, E, TILES])
        sloti = sb("sloti", [P, 3, TOP * TILES], I32)
        gidr = sb("gidr", [P, BCOLS], I32)
        offb = sb("offb", [P, P], BF16)
        JH, JB = TOP * TILES * P // 2, TOP * TILES * BCOLS
        ohoff = shared[:, 0:JH].bitcast(BF16).rearrange("p (r n) -> p r n", n=P)
        ohblk = shared[:, JH:JH + JB].rearrange("p (r n) -> p r n", n=BCOLS)
        tabr = shared[:, JH + JB:JH + 2 * JB].bitcast(BF16).rearrange("p (r a n) -> p r a n", a=2, n=BCOLS)
        cwb = sb("cwb", [P, 3, TOP * TILES], BF16)
        cwr = sb("cwr", [P, 2, TOP * TILES])
        wtab = shared[:, JH + JB:JH + JB + 3 * JB // 2].bitcast(BF16).rearrange("p (r a n) -> p r a n", a=3, n=BCOLS)
        wparts = sb("wparts", [P, 3, BCOLS])
        wslot = sb("wslot", [P, 2, BCOLS])
        tab = sb("tab", [P, 5, BCOLS])
        gid = sb("gid", [P, BCOLS], I32)
        sid = sb("sid", [P, BCOLS], I32)
        cur = sb("cur", [P, 2], I32)
        emt = sb("emt", [1, BCOLS, E])
        emtf = sb("emtf", [1, BCOLS])
        emap = sb("emap", [1, BCOLS], I32)
        nblk = sb("nblk", [1, 2], I32)
        comb = sb("comb", [P, TILES, E])
        combt = sb("combt", [P, TOP, TILES, E])
        last_w = sb("last_w", [E + 3, D])
        scales = sb("scales", [E + 3, D])
        v2 = sb("v2", [P, PLACES])
        v2r = sb("v2r", [P, PLACES])
        add = sb("add", [P, PLACES, 2])
        ch = sb("ch", [P, PLACES, 2])
        chj = sb("chj", [P, PLACES, 2])
        chd = sb("chd", [P, 2, PLACES])
        back = sb("back", [IMAGES, PLACES, 2])
        z = sb("z", [IMAGES, 2, PLACES])
        zz = sb("zz", [IMAGES, 4, PLACES])
        xg_first = sb("xg_first", [P, D])
        xg = sb("xg", [P, D])
        xah = sb("xah", [P, P], F32R)
        xal = sb("xal", [P, P], F32R)
        xbb = sb("xbb", [P, P], F32R)
        xbh = sb("xbh", [P, P], F32R)
        ysb = g_sb
        yb = attn[:, 0:TILES * D].rearrange("p (t d) -> p t d", t=TILES)

        gate_ps = (b2k, b3)
        o_ps = ((b2k, b3), (b6, b5))
        vg = psT[:, 2:4, :].rearrange("p a (b n) -> p a b n", b=2)
        ident = cst[:, C_ID:C_ID + P]
        diag = cst[:, C_DIAG:C_DIAG + P]
        ones = cst[:, C_ONE:C_ONE + P]
        half = [slice(0, HALF), slice(HALF, TILES)]
        cols = [slice(0, HT), slice(HT, TOKENS)]

        names = """s_cst s_gb s_tokb s_qkv s_wp s_bpr s_alpha s_gate s_sw d_b1 d_bias s_w2 s_bk v_weff a_sq
            v_chain p_prod p_acc t_sum t_bias v_h p_hb pe_hT a_hT pe_qk a_q v_qk pe_vg a_vp a_gelu v_gsub
            a_gexp v_gw pe_gwT a_gwT pe_wvT a_wvT pe_wg a_wg pe_gw v_csub a_cexp v_A pe_AT a_AT pe_o d_hn2
            pe_h2T v_hT pe_gate v_v pe_vT a_vT d_v v_lsub a_lexp v_M pe_rank v_tabr pe_tab v_tab v_emap
            p_ones a_sig v_sig v_comb pe_combT v_feat d_feat v_sw a_combT d_gather pe_xT a_xh pe_up0 pe_up1
            a_ge pe_hgT v_hgT pe_y v_y d_scatter pe_base d_yb0 d_yb1 d_yb2 d_yb3 v_out d_out p_gidx p_sidx
            p_pass v_sq p_done p_hi p_lo p_b1 v_xl d_first t_col p_clear v_lo a_q1 p_q1 a_g1 p_g1 a_t v_t v_cw
            p_cw pe_wtab v_wslot d_base p_tabr v_gid v_gwm a_vps a_g a_hi v_blk a_tabr a_top v_top a_hn
            v_nmr v_hnb v_var a_sd""".split()
        S = {n: sem(n) for n in names}
        d_x = [sem(f"d_x{c}") for c in range(CHUNKS)]
        d_raw = [sem(f"d_raw{i}") for i in range(RAW)]
        d_w = [sem(f"d_w{c}") for c in range(CHUNKS)]
        block = ctx.enter_context(nc.Block())

        @block.sync
        def _(sp):
            sp.dma_start(gb[:, :], gammas_betas).then_inc(S["s_gb"], 16)
            for c in range(CHUNKS):
                k = CROWS[c]
                if c < INNER:
                    if c >= RING:
                        sp.wait_ge(S["v_weff"], c - RING + 1)
                        sp.wait_ge(S["p_prod"], c - RING + 1)
                    sp.dma_start(Wt[:, c % RING, :, :], mult_w[c]).then_inc(d_w[c], 16)
                else:
                    sp.dma_start(We[:, c - INNER, :], edge_w[c - INNER]).then_inc(d_w[c], 16)
                sp.dma_start(X[0:k, c, :], pixels[c, 0:k, :]).then_inc(d_x[c], 16)
                if c == 1:
                    sp.dma_start(cst[:, :], consts).then_inc(S["s_cst"], 16)
            sp.dma_start(tokb[:, :], tok_b.partition_broadcast(P)).then_inc(S["s_tokb"], 16)
            sp.dma_start(wqa[:, :], wqkv[0:LO]).then_inc(S["s_qkv"], 16)
            sp.dma_start(wqb[:, :], wqkv[LO:]).then_inc(S["s_qkv"], 16)
            sp.dma_start(wpa[:, :], wpg[0:LO]).then_inc(S["s_wp"], 16)
            sp.dma_start(wpb[:, :], wpg[LO:]).then_inc(S["s_wp"], 16)
            sp.dma_start(bpr[:, :], b_proj.partition_broadcast(P)).then_inc(S["s_bpr"], 16)
            sp.dma_start(sig[:, 0:1], alpha.partition_broadcast(P)).then_inc(S["s_alpha"], 16)
            sp.dma_start(wgate[:, :], gate[0:LO]).then_inc(S["s_gate"], 16)
            sp.dma_start(wgateb[:, :], gate[LO:]).then_inc(S["s_gate"], 16)
            sp.dma_start(last_w[0:E, :], b2).then_inc(S["s_sw"], 16)
            sp.dma_start(last_w[E:E + 3, :], spec_w).then_inc(S["s_sw"], 16)
            sp.wait_ge(S["p_ones"], 3)
            sp.dma_start(scales[E:E + 3, :], bk.partition_broadcast(3)).then_inc(S["s_bk"], 16)
            sp.dma_start(b1r[:, :], bias1).then_inc(S["d_b1"], 16)
            sp.wait_ge(S["t_sum"], 1)
            for c in range(2 * E):
                if c >= RAW:
                    sp.wait_ge(S["p_lo"], c - RAW + 1)
                for i in range(2):
                    row = LO if c >= E else i * HI
                    sp.dma_start(raw[i * HI:(i + 1) * HI, c % RAW, :],
                                 w1[c % E, row:row + HI, :]).then_inc(d_raw[c % RAW], 16)
            for f in range(2):
                sp.wait_ge(S["v_hnb"], f + 3)
                sp.wait_ge(S["a_hn"], (f + 3) * (HALF - SPLIT))
                sp.dma_start(hn2_rows[f * HT:(f + 1) * HT].rearrange("(t p) d -> p t d", p=P),
                             hn[:, half[f], :]).then_inc(S["d_hn2"], 16)
            for f in range(2):
                sp.dma_start(sums[f * HT:(f + 1) * HT].rearrange("(t p) d -> p t d", p=P),
                             hb[:, half[f], :]).then_inc(S["d_base"], 16)
            sp.wait_ge(S["pe_o"], 2)
            sp.wait_ge(S["p_hb"], 2)

            def second_weights(e):
                sp.dma_start(w2s[:, e * FC:(e + 1) * FC, :],
                             w2[e].rearrange("(c p) d -> p c d", p=P)).then_inc(S["s_w2"], 16)

            for e in range(2):
                second_weights(e)
            sp.wait_ge(S["a_vT"], 1)
            for d in range(2):
                sp.dma_start(v2[d * IMAGES:(d + 1) * IMAGES, :],
                             vT[:, :].rearrange("t (b n) -> t b n", n=PLACES)).then_inc(S["d_v"], 16)
            for e in range(2, E):
                second_weights(e)
            sp.wait_ge(S["p_ones"], 4)
            sp.wait_ge(S["v_feat"], 1)
            for r in range(2):
                sp.dma_start(rows_last[E + r:E + r + 1, :].rearrange("r (b n) -> r b n", n=PLACES),
                             z[:, r, :]).then_inc(S["d_feat"], 16)
            sp.wait_ge(S["p_done"], 1)
            for q in range(4):
                sp.dma_start(yb[:, 2 * q:2 * q + 2, :],
                             sums[2 * q * P:(2 * q + 2) * P].rearrange("(t p) d -> p t d", p=P)
                             ).then_inc(S[f"d_yb{q}"], 16)
            for q in range(4):
                sp.wait_ge(S["v_out"], q + 1)
                sp.dma_start(out[2 * q * P:(2 * q + 2) * P].rearrange("(t p) d -> p t d", p=P),
                             hb[:, 2 * q:2 * q + 2, :]).then_inc(S["d_out"], 16)
            sp.wait_ge(S["d_out"], 64)

        @block.gpsimd
        def _(pool):
            pool.memset(hnTb[HI:HI + 1, :], 1.0).then_inc(S["p_ones"], 1)
            pool.wait_ge(S["p_ones"], 1)
            pool.memset(xbh[HI:P, :].bitcast(F32), 1.0).then_inc(S["p_ones"], 1)
            pool.wait_ge(S["p_ones"], 2)
            pool.memset(scales[:, :], 1.0).then_inc(S["p_ones"], 1)
            pool.wait_ge(S["p_ones"], 3)
            pool.memset(tbh[HI:P, :].bitcast(F32), 1.0).then_inc(S["p_clear"], 1)
            pool.wait_ge(S["p_clear"], 1)
            pool.memset(qbl[HI:P, :].bitcast(F32), 0.0).then_inc(S["p_clear"], 1)
            pool.wait_ge(S["p_clear"], 2)
            pool.memset(gbl[HI:P, :].bitcast(F32), 0.0).then_inc(S["p_clear"], 1)
            pool.wait_ge(S["p_clear"], 3)
            for i, g in enumerate((gah, gal, gbb, gbl)):
                pool.memset(g[:, VG:VGE].bitcast(F32), 0.0).then_inc(S["p_clear"], 1)
                pool.wait_ge(S["p_clear"], 4 + i)
            pool.wait_ge(S["p_ones"], 3)
            pool.wait_ge(S["s_gb"], 16)
            for c in range(CHUNKS):
                pool.wait_ge(d_w[c], 16)
                if c < INNER:
                    dst = bacc if c == 0 else bprod
                    if c >= 2:
                        pool.wait_ge(S["p_acc"], c)
                    pool.tensor_tensor(dst[:, :, :], Wt[:, c % RING, :, :],
                                       bet[:, c, :].unsqueeze(2).broadcast_to([P, SHIFTS, D]),
                                       ALU.mult).then_inc(S["p_prod"], 1)
                    pool.wait_ge(S["p_prod"], c + 1)
                    if c > 0:
                        pool.tensor_tensor(bacc[:, :, :], bacc[:, :, :], bprod[:, :, :],
                                           ALU.add).then_inc(S["p_acc"], 1)
                    else:
                        pool.sem_inc(S["p_acc"], 1)
                else:
                    pool.wait_ge(S["p_acc"], c)
                    pool.tensor_tensor(bprod[0:EDGE, 0, :], We[:, c - INNER, :],
                                       bet[0:EDGE, c, 0:1].broadcast_to([EDGE, D]),
                                       ALU.mult).then_inc(S["p_prod"], 1)
                    pool.wait_ge(S["p_prod"], c + 1)
                    pool.tensor_tensor(bacc[0:EDGE, 0, :], bacc[0:EDGE, 0, :], bprod[0:EDGE, 0, :],
                                       ALU.add).then_inc(S["p_acc"], 1)
            for i in range(1, SHIFTS):
                pool.wait_ge(S["p_acc"], CHUNKS + i - 1)
                pool.tensor_tensor(bacc[:, 0, :], bacc[:, 0, :], bacc[:, i, :], ALU.add).then_inc(S["p_acc"], 1)

            def low_parts(src_a, src_b, ah, al, bb, bl, high, done):
                pool.wait_ge(S[high], 4)
                pool.tensor_tensor(al, src_a, ah.bitcast(F32), ALU.subtract).then_inc(S[done], 1)
                pool.wait_ge(S[done], 1)
                pool.tensor_tensor(bl[0:HI], src_b[0:HI], bb[0:HI].bitcast(F32), ALU.subtract).then_inc(S[done], 1)
                pool.wait_ge(S[done], 2)
                pool.tensor_tensor(bl[96:97], src_b[HI:HI + 1], bl[HI:HI + 1].bitcast(F32),
                                   ALU.subtract).then_inc(S[done], 1)
                pool.wait_ge(S[done], 3)

            pool.wait_ge(S["p_acc"], CHUNKS + SHIFTS - 1)
            low_parts(wqa[:, 0:2 * D], wqb[:, 0:2 * D], qah[:, :], qal[:, :], qbb[:, :], qbl[:, :], "a_q1", "p_q1")
            pool.wait_ge(S["d_b1"], 16)
            pool.tensor_copy(b1h[:, :], b1r[:, :]).then_inc(S["p_b1"], 1)
            pool.wait_ge(S["p_b1"], 1)
            pool.tensor_tensor(b1l[:, :], b1r[:, :], b1h[:, :].bitcast(F32), ALU.subtract).then_inc(S["p_b1"], 1)
            pool.wait_ge(S["p_b1"], 2)
            low_parts(wga[:, :], wgb[:, :], gah[:, 0:VG], gal[:, 0:VG], gbb[:, 0:VG], gbl[:, 0:VG], "a_g1", "p_g1")
            pool.wait_ge(S["s_bpr"], 16)
            for f in range(2):
                pool.wait_ge(S["v_h"], f + 1)
                pool.tensor_tensor(hb[:, half[f], :], h[:, half[f], :],
                                   bpr[:, :].unsqueeze(1).broadcast_to([P, HALF, D]),
                                   ALU.add).then_inc(S["p_hb"], 1)
            pool.wait_ge(S["p_hb"], 2)
            pool.wait_ge(S["t_bias"], 1)
            for c in range(2 * E):
                e = c % E
                if c > 0:
                    pool.wait_ge(S["p_lo"], c)
                if c == E:
                    pool.wait_ge(S["pe_vg"], 2)
                    for i, b in enumerate((b1h, b1l)):
                        pool.dma_start(w1bl[HI + i:HI + i + 1].rearrange("o e f -> o (e f)").rearrange(
                            "o (p n) -> o p n", p=BR), b[:, :]).then_inc(S["d_bias"], 16)
                if c in BY_DVE:
                    pool.wait_ge(S["v_lo"], BY_DVE.index(c) + 1)
                    pool.sem_inc(S["p_lo"], 1)
                    continue
                pool.wait_ge(d_raw[c % RAW], 32 * (c // RAW + 1))
                hi = (w1ah if c < E else w1bh)[:, e, :]
                if c % 2 == 0:
                    pool.tensor_copy(hi, raw[:, c % RAW, :]).then_inc(S["p_hi"], 1)
                    pool.wait_ge(S["p_hi"], c // 2 + 1 - sum(i < c for i in BY_DVE))
                else:
                    pool.wait_ge(S["a_hi"], c // 2 + 1)
                k = P if c < E else HI
                pool.tensor_tensor((w1al if c < E else w1bl)[0:k, e, :], raw[0:k, c % RAW, :],
                                   hi[0:k].bitcast(F32), ALU.subtract).then_inc(S["p_lo"], 1)
            pool.wait_ge(S["pe_o"], 2)
            pool.wait_ge(S["p_lo"], 2 * E)
            pool.memset(rows_last, 1.0).then_inc(S["p_ones"], 1)
            pool.wait_ge(S["v_blk"], 1)
            pool.tensor_tensor(tabr[:, :, 1, :], ohblk[:, :, :],
                               cst[:, C_TILE:C_TILE + TOP * TILES].unsqueeze(2).broadcast_to([P, TOP * TILES, BCOLS]),
                               ALU.mult).then_inc(S["p_tabr"], 1)
            pool.wait_ge(S["v_emap"], 1)
            pool.wait_ge(S["d_hn2"], 32)
            m = pool.value_load(nblk[0:1, 1:2], min_val=TOP * TOKENS // P - 2, max_val=BLOCKS - 2)

            last_row = pool.to_reg(TOKENS - 1)

            def gather_rows(rows, index, landed):
                pool.indirect_dma_start(rows[:, :], None, hn2_rows,
                                        bass.IndirectOffsetOnAxis(index, 0)).then_inc(landed, 16)

            def gather(b):
                pool.tensor_copy(cur[:, 0:1], gid[:, bass.ds(b, 1)]).then_inc(S["p_gidx"], 1)
                pool.wait_ge(S["p_gidx"], b - 1)
                pool.sem_inc(S["p_pass"], 1)
                gather_rows(xg, cur[:, 0:1], S["d_gather"])

            def scatter(b):
                pool.wait_ge(S["v_y"], b + 1)
                pool.sem_inc(S["p_pass"], 1)
                pool.tensor_copy(cur[:, 1:2], sid[:, bass.ds(b, 1)]).then_inc(S["p_sidx"], 1)
                pool.wait_ge(S["p_sidx"], b + 1)
                pool.sem_inc(S["p_pass"], 1)
                pool.indirect_dma_start(sums, bass.IndirectOffsetOnAxis(cur[:, 1:2], 0), ysb[:, :], None,
                                        bounds_check=last_row, oob_is_err=False, compute_op=ALU.add
                                        ).then_inc(S["d_scatter"], 16)

            pool.wait_ge(S["v_gid"], 1)
            gather_rows(xg_first, gid[:, 0:1], S["d_first"])
            gather_rows(xg, gid[:, 1:2], S["d_gather"])
            pool.wait_ge(S["v_cw"], 1)
            weight = cw[:, :, :].rearrange("p j t -> p (j t)")
            pool.tensor_copy(cwb[:, 0, :], weight).then_inc(S["p_cw"], 1)
            pool.wait_ge(S["p_cw"], 1)
            pool.tensor_tensor(cwr[:, 0, :], weight, cwb[:, 0, :], ALU.subtract).then_inc(S["p_cw"], 1)
            pool.wait_ge(S["p_cw"], 2)
            pool.tensor_copy(cwb[:, 1, :], cwr[:, 0, :]).then_inc(S["p_cw"], 1)
            pool.wait_ge(S["p_cw"], 3)
            pool.tensor_tensor(cwr[:, 1, :], cwr[:, 0, :], cwb[:, 1, :], ALU.subtract).then_inc(S["p_cw"], 1)
            pool.wait_ge(S["p_cw"], 4)
            pool.tensor_copy(cwb[:, 2, :], cwr[:, 1, :]).then_inc(S["p_cw"], 1)
            pool.wait_ge(S["p_cw"], 5)
            pool.wait_ge(S["pe_tab"], 1)
            for i in range(3):
                pool.tensor_tensor(wtab[:, :, i, :], ohblk[:, :, :],
                                   cwb[:, i, :].unsqueeze(2).broadcast_to([P, TOP * TILES, BCOLS]),
                                   ALU.mult).then_inc(S["p_cw"], 1)
                pool.wait_ge(S["p_cw"], 6 + i)
            pool.wait_ge(S["v_tab"], 1)
            pool.wait_ge(S["d_base"], 32)
            pool.wait_ge(S["pe_xT"], 2)
            gather(2)
            with pool.Fori(0, m) as i:
                pool.wait_ge(S["pe_xT"], i + 3)
                pool.sem_inc(S["p_pass"], 1)
                gather(i + 3)
                scatter(i)
            scatter(m)
            scatter(m + 1)
            pool.wait_ge(S["d_scatter"], m * 16 + 32)
            pool.sem_inc(S["p_done"], 1)

        @block.scalar
        def _(act):
            for c in range(CHUNKS):
                act.wait_ge(d_x[c], 16)
                if c >= 2:
                    act.wait_ge(S["v_sq"], c - 1)
                k = CROWS[c]
                act.activation(Xsq[0:k, c % 2, :], X[0:k, c, :], ACT.Square).then_inc(S["a_sq"], 1)

            def high_parts(src_a, src_b, ah, bb, bl, done):
                act.activation(ah, src_a, ACT.Copy).then_inc(S[done], 1)
                act.activation(bb[0:HI], src_b[0:HI], ACT.Copy).then_inc(S[done], 1)
                act.activation(bb[HI:P], src_b[0:HI], ACT.Copy).then_inc(S[done], 1)
                act.activation(bl[HI:HI + 1], src_b[HI:HI + 1], ACT.Copy).then_inc(S[done], 1)

            act.wait_ge(S["s_qkv"], 32)
            act.wait_ge(S["p_clear"], 3)
            high_parts(wqa[:, 0:2 * D], wqb[:, 0:2 * D], qah[:, :], qbb[:, :], qbl[:, :], "a_q1")
            act.wait_ge(S["v_var"], 1)
            act.activation(st[:, 6, :], st[:, 5, :], ACT.Sqrt).then_inc(S["a_sd"], 1)
            act.wait_ge(S["t_col"], 1)
            act.activation(g_sb[:, :], b5[:, 0:D], ACT.Copy).then_inc(S["a_g"], 1)

            def deviation(f, turn):
                act.wait_ge(S["v_var"], turn)
                act.activation(sd[:, half[f]], var[:, half[f]], ACT.Sqrt).then_inc(S["a_sd"], 1)

            def norm_rows(src, f):
                for t in range(f * HALF + SPLIT, (f + 1) * HALF):
                    act.activation(hn[:, t, :], src[:, t, :], ACT.Identity, bias=nmr[:, t:t + 1],
                                   scale=rstd[:, t:t + 1]).then_inc(S["a_hn"], 1)

            def high_w1(c):
                act.wait_ge(d_raw[c % RAW], 32 * (c // RAW + 1))
                act.activation((w1ah if c < E else w1bh)[:, c % E, :], raw[:, c % RAW, :],
                               ACT.Copy).then_inc(S["a_hi"], 1)

            act.wait_ge(S["pe_wvT"], 1)
            act.activation(wvTa[:, :], b7[:, 0:D + 1], ACT.Copy).then_inc(S["a_wvT"], 1)
            act.activation(wvTb[:, :], b7[0:HI, 256:256 + D + 1], ACT.Copy).then_inc(S["a_wvT"], 1)
            act.wait_ge(S["pe_wg"], 1)
            act.activation(wga[:, :], b7[:, 0:VG], ACT.Copy).then_inc(S["a_wg"], 1)
            act.activation(wgb[:, :], b7[0:HI + 1, 256:256 + VG], ACT.Copy).then_inc(S["a_wg"], 1)
            act.wait_ge(S["a_wg"], 2)
            high_parts(wga[:, :], wgb[:, :], gah[:, 0:VG], gbb[:, 0:VG], gbl[:, 0:VG], "a_g1")

            def high_rows(f, bank_a):
                act.wait_ge(S["pe_hT"], f + 1)
                act.activation(tah[:, cols[f]], bank_a, ACT.Copy).then_inc(S["a_t"], 1)
                act.activation(tbb[0:HI, cols[f]], b6[0:HI, :], ACT.Copy).then_inc(S["a_t"], 1)
                act.wait_ge(S["a_t"], 3 * f + 2)
                act.activation(tbh[0:HI, cols[f]], tbb[0:HI, cols[f]].bitcast(F32), ACT.Copy).then_inc(S["a_t"], 1)

            for f in range(2):
                deviation(f, f + 2)
                act.wait_ge(S["v_nmr"], f + 1)
                norm_rows(h, f)
                if f == 0:
                    high_rows(0, b7)
            act.wait_ge(S["v_h"], 2)
            act.wait_ge(S["t_bias"], 1)

            def take_values(f):
                act.activation(vp[:, half[f], :].rearrange("p (a b) g -> p a b g", b=2), vg[:, :, :, 0:D],
                               ACT.Copy).then_inc(S["a_vp"], 1)

            for f in range(2):
                act.wait_ge(S["pe_qk"], 3 * f + 1)
                act.activation(q0[:, cols[f]], b0, ACT.Copy).then_inc(S["a_q"], 1)
                act.wait_ge(S["pe_qk"], 3 * f + 2)
                act.activation(k0[:, cols[f]], b1, ACT.Copy).then_inc(S["a_q"], 1)
                if f == 0:
                    high_w1(1)
                    high_rows(1, b4)
                act.wait_ge(S["pe_vg"], f + 1)
                act.activation(gw[:, half[f], :].rearrange("p (a b) g -> p a b g", b=2), vg[:, :, :, D:VG],
                               ACT.Gelu).then_inc(S["a_gelu"], 1)
                if f == 0:
                    take_values(0)
                    high_w1(3)
            act.wait_ge(S["s_alpha"], 16)
            act.activation(sig[:, 1:2], sig[:, 0:1], ACT.Exp, scale=-1.0).then_inc(S["a_sig"], 1)
            for f in range(2):
                act.wait_ge(S["v_gsub"], f + 1)
                act.activation(gw[:, half[f], :], gw[:, half[f], :], ACT.Exp).then_inc(S["a_gexp"], 1)
            high_w1(5)
            for f in range(2):
                act.wait_ge(S["pe_gwT"], f + 1)
                act.activation(gwT[:, cols[f]], (b0, b1)[f][0:GROUPS, :], ACT.Copy).then_inc(S["a_gwT"], 1)
            take_values(1)
            act.wait_ge(S["v_sig"], 1)
            for f in range(2):
                act.wait_ge(S["a_vp"], f + 1)
                act.activation(vps[:, half[f], :], vp[:, half[f], :], ACT.Copy,
                               scale=sig[:, 3:4]).then_inc(S["a_vps"], 1)
            high_w1(7)
            for f in range(2):
                act.wait_ge(S["v_csub"], f + 1)
                act.activation(ct[:, half[f], :], ct[:, half[f], :], ACT.Exp).then_inc(S["a_cexp"], 1)
                if f == 0:
                    high_w1(9)
            for f in range(2):
                act.wait_ge(S["pe_AT"], f + 1)
                act.activation(AT[:, half[f], :].rearrange("p t n -> p (t n)"), (b0, b1)[f],
                               ACT.Copy).then_inc(S["a_AT"], 1)
                if f == 0:
                    high_w1(11)
            for f in range(2):
                deviation(f, f + 4)
                act.wait_ge(S["v_nmr"], f + 3)
                norm_rows(hb, f)
                act.wait_ge(S["pe_h2T"], f + 1)
                act.activation(hnTa[:, cols[f]], (b7, b4)[f], ACT.Copy).then_inc(S["a_hT"], 1)
                high_w1(13 + 2 * f)
            act.wait_ge(S["pe_vT"], 1)
            act.activation(vT[:, :], b4[0:TILES, 0:P], ACT.Copy).then_inc(S["a_vT"], 1)
            act.wait_ge(S["v_lsub"], 1)
            act.activation(pr[:, :, :], lg[:, :, :], ACT.Exp).then_inc(S["a_lexp"], 1)
            act.wait_ge(S["v_top"], 1)
            act.activation(best[:, :, :], best[:, :, :], ACT.Exp).then_inc(S["a_top"], 1)
            act.wait_ge(S["v_blk"], 1)
            act.activation(tabr[:, :, 0, :], ohblk[:, :, :], ACT.Copy,
                           scale=cst[:, C_PART:C_PART + 1]).then_inc(S["a_tabr"], 1)
            act.wait_ge(S["p_ones"], 4)
            for f in range(2):
                act.wait_ge(S["pe_combT"], f + 1)
                act.activation(rows_last[0:E, cols[f]], (b5, b6)[f][0:E, :], ACT.Copy).then_inc(S["a_combT"], 1)
            act.wait_ge(S["v_emap"], 1)
            n = act.value_load(nblk[0:1, 0:1], min_val=TOP * TOKENS // P, max_val=BLOCKS)

            def high_x(b):
                act.activation(xah[:, :], b7[:, 0:P], ACT.Copy).then_inc(S["a_xh"], 1)
                act.activation(xbb[0:HI, :], b7[0:HI, P:2 * P], ACT.Copy).then_inc(S["a_xh"], 1)
                act.wait_ge(S["a_xh"], b * 3 + 2)
                act.activation(xbh[0:HI, :], xbb[0:HI, :].bitcast(F32), ACT.Copy).then_inc(S["a_xh"], 1)

            def gelu(part):
                act.activation(hg[:, part * FH:(part + 1) * FH], (b0, b1)[part][:, 0:FH],
                               ACT.Gelu_apprx_tanh).then_inc(S["a_ge"], 1)

            act.wait_ge(S["pe_xT"], 1)
            act.wait_ge(S["p_ones"], 2)
            high_x(0)
            act.wait_ge(S["pe_up0"], 1)
            gelu(0)
            act.wait_ge(S["pe_xT"], 2)
            high_x(1)
            act.wait_ge(S["pe_up1"], 1)
            gelu(1)
            with act.Fori(1, n) as i:
                act.wait_ge(S["pe_up0"], i + 1)
                act.wait_ge(S["pe_hgT"], i * 2)
                gelu(0)
                act.wait_ge(S["pe_xT"], i + 2)
                high_x(i + 1)
                act.wait_ge(S["pe_up1"], i + 1)
                gelu(1)

        @block.vector
        def _(dve):
            count = [0]

            def link(ins):
                count[0] += 1
                ins.then_inc(S["v_chain"], 1)
                dve.wait_ge(S["v_chain"], count[0])

            dve.wait_ge(S["s_gb"], 16)
            dve.tensor_copy(weff[:, :, D:D + 1], mult.unsqueeze(2))

            def sum_squares(c):
                k = CROWS[c]
                dve.wait_ge(S["a_sq"], c + 1)
                times = mult[0:k, c:c + 1]
                if c == 0:
                    ins = dve.tensor_scalar(sqsum[:, :], Xsq[:, 0, :], times, None, ALU.mult)
                else:
                    dve.wait_ge(S["v_sq"], c)
                    ins = dve.scalar_tensor_tensor(sqsum[0:k], Xsq[0:k, c % 2, :], times, sqsum[0:k], ALU.mult, ALU.add)
                ins.then_inc(S["v_sq"], 1)

            for c in range(CHUNKS):
                dve.wait_ge(d_w[c], 16)
                if c < INNER:
                    link(dve.tensor_scalar(weff[:, c, 0:D], Wt[:, c % RING, 0, :], gam[:, c, 0:1], None, ALU.mult))
                    for i in range(1, SHIFTS):
                        ins = dve.scalar_tensor_tensor(weff[:, c, 0:D], Wt[:, c % RING, i, :], gam[:, c, i:i + 1],
                                                       weff[:, c, 0:D], ALU.mult, ALU.add)
                        if i < SHIFTS - 1:
                            link(ins)
                    ins.then_inc(S["v_weff"], 1)
                else:
                    dve.tensor_scalar(weff[0:EDGE, c, 0:D], We[:, c - INNER, :], gam[0:EDGE, c, 0:1], None,
                                      ALU.mult).then_inc(S["v_weff"], 1)
                if c > 0:
                    sum_squares(c - 1)
            sum_squares(CHUNKS - 1)
            dve.wait_ge(S["s_cst"], 16)
            dve.tensor_copy(offb[:, :], cst[:, C_OFF:C_OFF + P])
            dve.wait_ge(S["s_sw"], 32)
            dve.wait_ge(S["s_bk"], 16)
            dve.tensor_tensor(last_w[:, :], last_w[:, :], scales[:, :], ALU.mult).then_inc(S["v_sw"], 1)
            dve.wait_ge(S["t_sum"], 1)
            tview = psT[:, :, :].rearrange("p a (b n) -> p a b n", b=2)
            tv = [tview[:, t // 2, t % 2, :] for t in range(TILES)]
            link(dve.tensor_scalar(st[:, 0, :].rearrange("p (a b) -> p a b", b=2), tview[:, :, :, D], -1.0 / FEATURES,
                                   None, ALU.mult))
            link(dve.tensor_tensor(st[:, 1, :], st[:, 0, :], st[:, 0, :], ALU.mult))
            link(dve.scalar_tensor_tensor(st[:, 2, :], b4[:, 0:TILES], 1.0 / FEATURES, st[:, 1, :],
                                          ALU.mult, ALU.subtract))
            dve.tensor_scalar(st[:, 5, :], st[:, 2, :], EPS, None, ALU.add).then_inc(S["v_var"], 1)
            dve.wait_ge(S["a_sd"], 1)
            link(dve.reciprocal(st[:, 3, :], st[:, 6, :]))
            link(dve.tensor_tensor(st[:, 4, :], st[:, 0, :], st[:, 3, :], ALU.mult))
            dve.wait_ge(S["t_bias"], 1)
            dve.wait_ge(S["s_tokb"], 16)
            dve.wait_ge(S["a_g"], 1)
            link(dve.tensor_tensor(bw_sb[:, :], b6[:, 0:D], tokb[:, :], ALU.add))
            def make_h(f):
                for t in range(f * HALF, (f + 1) * HALF):
                    ins = dve.scalar_tensor_tensor(ttmp[:, t, :], g_sb[:, :], st[:, 4, t:t + 1], bw_sb[:, :],
                                                   ALU.mult, ALU.add)
                link(ins)
                for t in range(f * HALF, (f + 1) * HALF):
                    ins = dve.scalar_tensor_tensor(h[:, t, :], tv[t][:, 0:D], st[:, 3, t:t + 1], ttmp[:, t, :],
                                                   ALU.mult, ALU.add)
                ins.then_inc(S["v_h"], 1)
                dve.wait_ge(S["v_h"], f + 1)

            def take_low_rows(f, bank):
                dve.wait_ge(S["pe_h2T"], f + 1)
                dve.tensor_copy(hnTb[0:HI, cols[f]], bank[0:HI, :]).then_inc(S["v_hT"], 1)

            def norm(src, f, turn, between=None):
                for t in range(f * HALF, (f + 1) * HALF):
                    ins = dve.bn_stats(bn6[:, t, :], src[:, t, :])
                link(ins)
                for t in range(f * HALF, (f + 1) * HALF):
                    ins = dve.bn_aggr(mv[:, t, :], bn6[:, t, :])
                link(ins)
                dve.tensor_scalar(var[:, half[f]], mv[:, half[f], 1], EPS, None, ALU.add).then_inc(S["v_var"], 1)
                if between:
                    between()
                dve.wait_ge(S["a_sd"], turn)
                link(dve.reciprocal(rstd[:, half[f]], sd[:, half[f]]))
                link(dve.scalar_tensor_tensor(nmr[:, half[f]], mv[:, half[f], 0], -1.0, rstd[:, half[f]],
                                              ALU.mult, ALU.mult))
                dve.sem_inc(S["v_nmr"], 1)
                for t in range(f * HALF, f * HALF + SPLIT):
                    ins = dve.tensor_scalar(hn[:, t, :], src[:, t, :], mv[:, t, 0:1], rstd[:, t:t + 1],
                                            ALU.subtract, ALU.mult)
                ins.then_inc(S["v_hnb"], 1)

            def low_rows(f, bank_a):
                dve.wait_ge(S["a_t"], 3 * f + 2)
                dve.tensor_tensor(tal[:, cols[f]], bank_a, tah[:, cols[f]].bitcast(F32), ALU.subtract)
                dve.tensor_tensor(tbb[HI:P, cols[f]], b6[0:HI, :], tbb[0:HI, cols[f]].bitcast(F32),
                                  ALU.subtract).then_inc(S["v_t"], 1)

            def split_w1(c):
                dve.wait_ge(d_raw[c % RAW], 32 * (c // RAW + 1))
                hi = (w1ah if c < E else w1bh)[:, c % E, :]
                link(dve.tensor_copy(hi, raw[:, c % RAW, :]))
                k = P if c < E else HI
                dve.tensor_tensor((w1al if c < E else w1bl)[0:k, c % E, :], raw[0:k, c % RAW, :],
                                  hi[0:k].bitcast(F32), ALU.subtract).then_inc(S["v_lo"], 1)

            make_h(0)
            norm(h, 0, 2)
            make_h(1)
            low_rows(0, b7)
            norm(h, 1, 3)
            for f in range(2):
                dve.wait_ge(S["pe_qk"], 3 * f + 3)
                dve.tensor_copy(q1[:, cols[f]], b5[0:HI, :])
                dve.tensor_copy(k1[:, cols[f]], b5[HI:P, :]).then_inc(S["v_qk"], 1)
                if f == 0:
                    low_rows(1, b4)
                else:
                    split_w1(4)
                dve.wait_ge(S["a_gelu"], f + 1)
                g = gw[:, half[f], :]
                link(dve.tensor_reduce(gred[:, 0, half[f]], g, AX.X, ALU.max))
                dve.tensor_tensor(g, g, gred[:, 0, half[f]].unsqueeze(2).broadcast_to([P, HALF, GROUPS]),
                                  ALU.subtract).then_inc(S["v_gsub"], 1)
            for f in range(2):
                g = gw[:, half[f], :]
                dve.wait_ge(S["a_gexp"], f + 1)
                link(dve.tensor_reduce(gred[:, 1, half[f]], g, AX.X, ALU.add))
                link(dve.reciprocal(gred[:, 2, half[f]], gred[:, 1, half[f]]))
                dve.tensor_tensor(g, g, gred[:, 2, half[f]].unsqueeze(2).broadcast_to([P, HALF, GROUPS]),
                                  ALU.mult).then_inc(S["v_gw"], 1)
            dve.wait_ge(S["a_sig"], 1)
            link(dve.tensor_scalar(sig[:, 2:3], sig[:, 1:2], 1.0, None, ALU.add))
            link(dve.reciprocal(sig[:, 3:4], sig[:, 2:3]))
            link(dve.tensor_tensor(sig[:, 4:5], sig[:, 1:2], sig[:, 3:4], ALU.mult))
            dve.sem_inc(S["v_sig"], 1)
            dve.wait_ge(S["pe_vg"], 2)
            split_w1(8)
            dg = diag.unsqueeze(1).broadcast_to([P, HALF, P])

            def masked_scores(f):
                dve.wait_ge(S["pe_gw"], f + 1)
                link(dve.tensor_tensor(gwm[:, half[f], :], (b6, b5)[f].rearrange("p (t n) -> p t n", n=P), dg,
                                       ALU.mult))
                dve.sem_inc(S["v_gwm"], 1)
                link(dve.scalar_tensor_tensor(tt[:, half[f], :], (b7, b4)[f].rearrange("p (t n) -> p t n", n=P), SCALE,
                                              gwm[:, half[f], :], ALU.mult, ALU.mult))

            def less_max(f):
                c = ct[:, half[f], :]
                link(dve.tensor_reduce(c, tt[:, half[f], :].rearrange("p t (b n) -> p t n b", n=PLACES), AX.X,
                                       ALU.add))
                link(dve.tensor_reduce(cred[:, 0, half[f]], c, AX.X, ALU.max))
                dve.tensor_tensor(c, c, cred[:, 0, half[f]].unsqueeze(2).broadcast_to([P, HALF, PLACES]),
                                  ALU.subtract).then_inc(S["v_csub"], 1)

            def weights(f):
                c = ct[:, half[f], :]
                dve.wait_ge(S["a_cexp"], f + 1)
                link(dve.tensor_reduce(cred[:, 1, half[f]], c, AX.X, ALU.add))
                link(dve.reciprocal(cred[:, 2, half[f]], cred[:, 1, half[f]]))
                link(dve.tensor_scalar(cred[:, 2, half[f]], cred[:, 2, half[f]], sig[:, 4:5], None, ALU.mult))
                link(dve.tensor_tensor(c, c, cred[:, 2, half[f]].unsqueeze(2).broadcast_to([P, HALF, PLACES]),
                                       ALU.mult))
                for t in range(f * HALF, (f + 1) * HALF):
                    ins = dve.tensor_tensor(Aw[:, t, :].rearrange("p (b n) -> p b n", n=PLACES),
                                            ct[:, t, :].unsqueeze(1).broadcast_to([P, P // PLACES, PLACES]),
                                            diag.rearrange("p (b n) -> p b n", n=PLACES), ALU.mult)
                ins.then_inc(S["v_A"], 1)

            masked_scores(0)
            less_max(0)
            masked_scores(1)
            weights(0)
            less_max(1)
            weights(1)
            for f in range(2):
                dve.wait_ge(S["pe_o"], f + 1)
                dve.wait_ge(S["p_hb"], f + 1)
                for i in range(2):
                    hv = hb[:, f * HALF + 2 * i:f * HALF + 2 * i + 2, :]
                    ins = dve.tensor_tensor(hv, o_ps[f][i].rearrange("p (b n) -> p b n", b=2)[:, :, 0:D], hv, ALU.add)
                link(ins)
                norm(hb, f, f + 4, (lambda: take_low_rows(0, b0)) if f else None)
            take_low_rows(1, b1)
            dve.wait_ge(S["pe_gate"], 2)
            gv = psT[:, 2:4, 0:HALF * 16].rearrange("p f (t n) -> p f t n", n=16)
            by = lambda a: a.rearrange("p (f t) -> p f t", f=2)
            dve.tensor_scalar(by(vcl[:, :]), gv[:, :, :, E], -3.0, 3.0, ALU.max, ALU.min).then_inc(S["v_v"], 1)
            for t in range(TILES):
                ins = dve.max(m8[:, t, :], gv[:, t // HALF, t % HALF, 0:E])
            link(ins)
            for t in range(TILES):
                ins = dve.max_index(i8[:, t, :], m8[:, t, :], gv[:, t // HALF, t % HALF, 0:E])
            link(ins)
            for j in range(TOP):
                ins = dve.tensor_tensor(oh[:, j], i8[:, :, j].unsqueeze(2).broadcast_to([P, TILES, E]),
                                        cst[:, C_EXP:C_EXP + E].unsqueeze(1).broadcast_to([P, TILES, E]),
                                        ALU.is_equal)
            link(ins)
            dve.tensor_tensor(M[:, :, :], oh[:, 0], oh[:, 1], ALU.add).then_inc(S["v_M"], 1)
            dve.tensor_tensor(lg[:, :, :].rearrange("p (f t) e -> p f t e", f=2), gv[:, :, :, 0:E],
                              by(m8[:, :, 0]).unsqueeze(3).broadcast_to([P, 2, HALF, E]),
                              ALU.subtract).then_inc(S["v_lsub"], 1)
            dve.tensor_tensor(best[:, :, :], m8[:, :, 0:TOP].rearrange("p t j -> p j t"),
                              m8[:, :, 0].unsqueeze(1).broadcast_to([P, TOP, TILES]),
                              ALU.subtract).then_inc(S["v_top"], 1)
            dve.wait_ge(S["pe_rank"], 1)
            tot = b5[:, 0:E * TILES]
            pre = b5[:, 256:256 + E * TILES]
            fl = lambda a: a.rearrange("p e t -> p (e t)")
            dve.tensor_copy(before[:, :], pre)
            link(dve.tensor_tensor_scan(fl(incl[:, :, :]), cst[:, C_RESET:C_RESET + E * TILES], tot, 0.0,
                                        ALU.mult, ALU.add))
            dve.tensor_tensor(fl(rank[:, :, :]), fl(incl[:, :, :]), tot, ALU.subtract)
            link(dve.tensor_tensor(gt[:, :, :], incl[:, :, TILES - 1:TILES].broadcast_to([P, E, E]),
                                   cst[:, C_THR:C_THR + E].unsqueeze(1).broadcast_to([P, E, E]), ALU.is_gt))
            dve.tensor_tensor(fl(rank[:, :, :]), fl(rank[:, :, :]), before[:, :], ALU.add)
            link(dve.tensor_reduce(blk[:, 0, :], gt[:, :, :], AX.X, ALU.add))
            link(dve.tensor_tensor_scan(blk[:, 1, :], ones[:, 0:E], blk[:, 0, :], 0.0, ALU.mult, ALU.add))
            link(dve.tensor_tensor(blk[:, 2, :], blk[:, 1, :], blk[:, 0, :], ALU.subtract))
            link(dve.scalar_tensor_tensor(slot[:, :, :], blk[:, 2, :].unsqueeze(2).broadcast_to([P, E, TILES]),
                                          float(P), rank[:, :, :], ALU.mult, ALU.add))
            for j in range(TOP):
                ins = dve.tensor_tensor(ohp[:, j], oh[:, j], slot[:, :, :].rearrange("p e t -> p t e"), ALU.mult)
            link(ins)
            with nc.allow_low_precision("whole numbers below 4096"):
                link(dve.tensor_reduce(sloti[:, 0, :], ohp[:, :, :, :].rearrange("p j t e -> p (j t) e"), AX.X,
                                       ALU.add))
            dve.tensor_scalar(sloti[:, 2, :], sloti[:, 0, :], -P, None, ALU.bitwise_and)
            link(dve.tensor_scalar(sloti[:, 1, :], sloti[:, 0, :], P - 1, None, ALU.bitwise_and))
            dve.wait_ge(S["p_lo"], 2 * E)
            JT = TOP * TILES
            link(dve.tensor_tensor(ohblk[:, :, :], sloti[:, 2, :].unsqueeze(2).broadcast_to([P, JT, BCOLS]),
                                   cst[:, C_BLK128:C_BLK128 + BCOLS].unsqueeze(1).broadcast_to([P, JT, BCOLS]),
                                   ALU.is_equal))
            dve.sem_inc(S["v_blk"], 1)
            dve.tensor_tensor(ohoff[:, :, :], sloti[:, 1, :].unsqueeze(2).broadcast_to([P, JT, P]),
                              offb[:, :].unsqueeze(1).broadcast_to([P, JT, P]),
                              ALU.is_equal).then_inc(S["v_tabr"], 1)
            link(dve.tensor_tensor(emt[:, :, :], cst[0:1, C_BLK:C_BLK + BCOLS].unsqueeze(2).broadcast_to([1, BCOLS, E]),
                                   blk[0:1, 1, :].unsqueeze(1).broadcast_to([1, BCOLS, E]), ALU.is_ge))
            dve.tensor_reduce(emtf[:, :], emt[:, :, :], AX.X, ALU.add)
            dve.tensor_scalar(nblk[:, 1:2], blk[0:1, 1, E - 1:E], -2.0, None, ALU.add)
            link(dve.tensor_copy(nblk[:, 0:1], blk[0:1, 1, E - 1:E]))
            dve.tensor_copy(emap[:, :], emtf[:, :]).then_inc(S["v_emap"], 1)
            dve.wait_ge(S["pe_tab"], 1)
            link(dve.tensor_copy(tab[:, 0:2, :].rearrange("p a b -> p (a b)"), b2k[:, 0:2 * BCOLS]))
            link(dve.scalar_tensor_tensor(tab[:, 2, :], tab[:, 1, :], float(P), tab[:, 0, :], ALU.mult, ALU.add))
            link(dve.tensor_scalar(gidr[:, :], tab[:, 2, :], -1.0, 0.0, ALU.add, ALU.max))
            dve.tensor_scalar(gid[:, :], gidr[:, :], TOKENS - 1, None, ALU.bitwise_and).then_inc(S["v_gid"], 1)
            link(dve.tensor_scalar(tab[:, 3, :], tab[:, 0, :], 0.0, float(FAR), ALU.is_equal, ALU.mult))
            dve.tensor_tensor(sid[:, :], gid[:, :], tab[:, 3, :], ALU.add).then_inc(S["v_tab"], 1)
            dve.wait_ge(S["a_lexp"], 1)
            dve.wait_ge(S["a_top"], 1)
            link(dve.tensor_reduce(gate_st[:, 1, :], pr[:, :, :], AX.X, ALU.add))
            link(dve.reciprocal(gate_st[:, 2, :], gate_st[:, 1, :]))
            link(dve.tensor_tensor(best[:, :, :], best[:, :, :],
                                   gate_st[:, 2, :].unsqueeze(1).broadcast_to([P, TOP, TILES]), ALU.mult))
            link(dve.tensor_tensor(gate_st[:, 0, :], best[:, 0, :], best[:, 1, :], ALU.add))
            link(dve.reciprocal(gate_st[:, 1, :], gate_st[:, 0, :]))
            link(dve.tensor_tensor(cw[:, :, :], best[:, :, :],
                                   gate_st[:, 1, :].unsqueeze(1).broadcast_to([P, TOP, TILES]), ALU.mult))
            dve.sem_inc(S["v_cw"], 1)
            for j in range(TOP):
                ins = dve.tensor_tensor(combt[:, j], oh[:, j], cw[:, j, :].unsqueeze(2).broadcast_to([P, TILES, E]),
                                        ALU.mult)
            link(ins)
            dve.tensor_tensor(comb[:, :, :], combt[:, 0], combt[:, 1], ALU.add).then_inc(S["v_comb"], 1)
            dve.wait_ge(S["d_v"], 32)
            link(dve.tensor_scalar(v2r[0:IMAGES, :], v2[0:IMAGES, :], -2.0, None, ALU.add))
            link(dve.tensor_scalar(v2r[IMAGES:P, :], v2[IMAGES:P, ::-1], -2.0, None, ALU.add))
            v4 = v2r[:, :].rearrange("p (a b) -> p a b", b=2)
            a4 = add[:, :, :].rearrange("p (a b) c -> p a b c", b=2)
            dve.tensor_copy(a4[:, :, 0, 0], v4[:, :, 0])
            dve.tensor_scalar(a4[:, :, 1, 0], v4[:, :, 1], -1.0, None, ALU.mult)
            link(dve.memset(add[:, :, 1], -1.0))
            link(dve.tensor_copy(ch[:, 0, :], add[:, 0, :]))

            def fraction(start, stop):
                for n in range(start, stop):
                    link(dve.tensor_tensor_reduce(chj[:, n, :], ch[:, n - 1, :], ch[:, n - 1, :], 1.0, 0.0, ALU.mult,
                                                  ALU.add, chd[:, 0, n:n + 1]))
                    link(dve.reciprocal(chd[:, 1, n:n + 1], chd[:, 0, n:n + 1]))
                    link(dve.scalar_tensor_tensor(ch[:, n, :], ch[:, n - 1, :], chd[:, 1, n:n + 1], add[:, n, :],
                                                  ALU.mult, ALU.add))

            m = dve.value_load(nblk[0:1, 1:2], min_val=TOP * TOKENS // P - 2, max_val=BLOCKS - 2)

            def low_x(b):
                dve.wait_ge(S["a_xh"], b * 3 + 2)
                dve.tensor_tensor(xal[:, :], b7[:, 0:P], xah[:, :].bitcast(F32), ALU.subtract)
                dve.tensor_tensor(xbb[HI:P, :], b7[0:HI, P:2 * P], xbb[0:HI, :].bitcast(F32),
                                  ALU.subtract).then_inc(S["v_xl"], 1)

            def take_h(b):
                for part in range(2):
                    dve.wait_ge(S["pe_hgT"], b * 2 + part + 1)
                    dve.tensor_copy(hT[:, 3 * part:3 * part + 3, :].rearrange("p c n -> p (c n)"),
                                    (b2k, b3)[part][:, 0:FH]).then_inc(S["v_hgT"], 1)

            def take_y(b):
                dve.wait_ge(S["pe_y"], b + 1)
                dve.tensor_scalar(ysb[:, :], b4[:, 0:D], wslot[:, 1, bass.ds(b, 1)], None,
                                  ALU.mult).then_inc(S["v_y"], 1)
            fraction(1, 5)
            low_x(0)
            fraction(5, 11)
            low_x(1)
            dve.wait_ge(S["pe_wtab"], 1)
            link(dve.tensor_copy(wparts[:, :, :].rearrange("p a b -> p (a b)"), b4[:, 0:3 * BCOLS]))
            dve.sem_inc(S["v_wslot"], 1)
            link(dve.tensor_tensor(wslot[:, 0, :], wparts[:, 1, :], wparts[:, 2, :], ALU.add))
            link(dve.tensor_tensor(wslot[:, 1, :], wparts[:, 0, :], wslot[:, 0, :], ALU.add))
            fraction(11, 12)
            take_h(0)
            low_x(2)
            fraction(12, 14)
            take_y(0)
            take_h(1)
            low_x(3)
            fraction(14, PLACES)
            dve.wait_ge(S["d_scatter"], 16)
            take_y(1)
            take_h(2)
            low_x(4)
            c4 = ch[:, :, :].rearrange("p (a b) c -> p a b c", b=2)
            link(dve.tensor_scalar(c4[:, :, 1, 0], c4[:, :, 1, 0], -1.0, None, ALU.mult))
            link(dve.tensor_copy(back[:, :, :], ch[IMAGES:P, ::-1, :]))
            link(dve.tensor_tensor(zz[:, 0:2, :].rearrange("p c n -> p n c"), ch[0:IMAGES, :, :], back[:, :, :],
                                   ALU.add))
            dve.tensor_tensor(zz[:, 0, :], zz[:, 0, :], v2r[0:IMAGES, :], ALU.subtract)
            link(dve.tensor_scalar(zz[:, 1, :], zz[:, 1, :], 1.0, None, ALU.add))
            link(dve.tensor_tensor(z[:, :, :], zz[:, 0:2, :], zz[:, 0:2, :], ALU.mult))
            link(dve.tensor_tensor(zz[:, 2, :], z[:, 0, :], z[:, 1, :], ALU.add))
            link(dve.reciprocal(zz[:, 3, :], zz[:, 2, :]))
            dve.tensor_tensor(z[:, 0, :], zz[:, 0, :], zz[:, 3, :], ALU.mult)
            link(dve.scalar_tensor_tensor(z[:, 1, :], zz[:, 1, :], -1.0, zz[:, 3, :], ALU.mult, ALU.mult))
            link(dve.tensor_scalar(z[:, :, :], z[:, :, :], -10.0, 10.0, ALU.max, ALU.min))
            dve.sem_inc(S["v_feat"], 1)
            dve.wait_ge(S["d_scatter"], 32)
            take_y(2)
            with dve.Fori(2, m) as i:
                take_h(i + 1)
                low_x(i + 3)
                dve.wait_ge(S["d_scatter"], i * 16 + 16)
                take_y(i + 1)
            take_h(m + 1)
            dve.wait_ge(S["d_scatter"], m * 16 + 16)
            take_y(m + 1)
            for q in range(4):
                dve.wait_ge(S["pe_base"], q + 1)
                dve.wait_ge(S[f"d_yb{q}"], 16)
                dve.tensor_tensor(hb[:, 2 * q:2 * q + 2, :],
                                  (b0, b1, b5, b6)[q].rearrange("p (b n) -> p b n", b=2)[:, :, 0:D],
                                  yb[:, 2 * q:2 * q + 2, :], ALU.add).then_inc(S["v_out"], 1)

        @block.tensor
        def _(pe):
            tview = psT[:, :, :].rearrange("p a (b n) -> p a b n", b=2)

            def tok(t):
                return slice(t * P, (t + 1) * P)

            for c in range(CHUNKS):
                k = CROWS[c]
                pe.wait_ge(d_x[c], 16)
                pe.wait_ge(S["v_weff"], c + 1)
                for t in range(TILES):
                    pe.matmul(tview[:, t // 2, t % 2, 0:D + 1], X[0:k, c, tok(t)], weff[0:k, c, :],
                              start=(c == 0 and t % 2 == 0), stop=(c == CHUNKS - 1), skip_group_check=True)
            pe.wait_ge(S["s_cst"], 16)
            pe.wait_ge(S["v_sq"], CHUNKS)
            for t in range(TILES):
                mm = pe.matmul(b4[:, t:t + 1], sqsum[:, tok(t)], ones[:, 0:1], start=True, stop=True)
            mm.then_inc(S["t_sum"], 1)
            for c in range(CHUNKS):
                k = CROWS[c]
                mm = pe.matmul(b5[:, 0:D], ones[0:k], weff[0:k, c, 0:D], start=(c == 0), stop=(c == CHUNKS - 1))
            mm.then_inc(S["t_col"], 1)
            pe.wait_ge(S["p_acc"], CHUNKS + SHIFTS - 1)
            pe.matmul(b6[:, 0:D], ones, bacc[:, 0, :], start=True, stop=True).then_inc(S["t_bias"], 1)
            pe.wait_ge(S["s_qkv"], 32)
            V = 2 * D
            pe.transpose(b7[:, 0:LO], wqa[:, V:V + LO], ident)
            pe.transpose(b7[:, LO:D + 1], wqb[:, V:V + LO], ident[0:HI + 1, 0:HI + 1])
            pe.transpose(b7[0:HI, 256:256 + LO], wqa[:, V + LO:V + D], ident)
            pe.transpose(b7[0:HI, 256 + LO:256 + D + 1], wqb[:, V + LO:V + D],
                         ident[0:HI + 1, 0:HI + 1]).then_inc(S["pe_wvT"], 1)
            pe.wait_ge(S["a_wvT"], 2)
            pe.wait_ge(S["s_wp"], 32)
            pe.matmul(b7[:, 0:VG], wvTa[:, 0:LO], wpa[:, :], start=True, stop=False)
            pe.matmul(b7[:, 0:VG], wvTb[:, 0:LO], wpb[:, :], start=False, stop=True)
            pe.matmul(b7[0:HI + 1, 256:256 + VG], wvTa[:, LO:D + 1], wpa[:, :], start=True, stop=False,
                      skip_group_check=True)
            pe.matmul(b7[0:HI + 1, 256:256 + VG], wvTb[:, LO:D + 1], wpb[:, :], start=False, stop=True,
                      skip_group_check=True).then_inc(S["pe_wg"], 1)
            pe.wait_ge(S["a_wg"], 2)
            pe.wait_ge(S["p_ones"], 2)

            def turn_rows(f, n, low):
                pe.wait_ge(S["v_hnb"], n)
                pe.wait_ge(S["a_hn"], n * (HALF - SPLIT))
                for t in range(HALF):
                    pe.transpose((b7, b4)[f][:, tok(t)], hn[:, f * HALF + t, 0:LO], ident)
                for t in range(HALF):
                    mm = pe.transpose(low[0:HI, tok(t)], hn[:, f * HALF + t, LO:D], ident)
                return mm

            turn_rows(0, 1, b6).then_inc(S["pe_hT"], 1)
            for f in range(2):
                for i, dst in enumerate((b0, b1, b5)):
                    part = slice(i * LO, (i + 1) * LO)
                    if f > 0:
                        if i < 2:
                            pe.wait_ge(S["a_q"], i + 1)
                        else:
                            pe.wait_ge(S["v_qk"], f)
                    pe.wait_ge(S["p_q1"], 3)
                    pe.wait_ge(S["a_t"], 3 * f + 1)
                    pe.matmul(dst, qah[:, part], tah[:, cols[f]], start=True, stop=False)
                    pe.matmul(dst, qal[:, part], tah[:, cols[f]], start=False, stop=False)
                    pe.wait_ge(S["a_t"], 3 * f + 3)
                    pe.matmul(dst, qbl[0:97, part], tbh[0:97, cols[f]], start=False, stop=False)
                    pe.wait_ge(S["v_t"], f + 1)
                    pe.matmul(dst, qah[:, part], tal[:, cols[f]], start=False, stop=False)
                    pe.matmul(dst, qbb[:, part], tbb[:, cols[f]], start=False, stop=True).then_inc(S["pe_qk"], 1)
                if f == 0:
                    turn_rows(1, 2, b6).then_inc(S["pe_hT"], 1)
                pe.wait_ge(S["v_h"], 2)
                if f > 0:
                    pe.wait_ge(S["a_vp"], f)
                pe.wait_ge(S["p_g1"], 3)
                for t in range(HALF):
                    dst = vg[:, t // 2, t % 2, 0:VGE]
                    T = f * HALF + t
                    pe.matmul(dst, tah[:, tok(T)], gah[:, :], start=True, stop=False)
                    pe.matmul(dst, tah[:, tok(T)], gal[:, :], start=False, stop=False)
                    pe.matmul(dst, tal[:, tok(T)], gah[:, :], start=False, stop=False)
                    pe.matmul(dst, tbb[:, tok(T)], gbb[:, :], start=False, stop=False)
                    mm = pe.matmul(dst, tbh[0:97, tok(T)], gbl[0:97, :], start=False, stop=True)
                mm.then_inc(S["pe_vg"], 1)
            for f in range(2):
                pe.wait_ge(S["a_q"], 2 * f + 2)
                pe.wait_ge(S["v_qk"], f + 1)
                for t in range(HALF):
                    T = f * HALF + t
                    dst = (b7, b4)[f][:, tok(t)]
                    pe.matmul(dst, q0[:, tok(T)], k0[:, tok(T)], start=True, stop=False)
                    pe.matmul(dst, q1[:, tok(T)], k1[:, tok(T)], start=False, stop=True)
            for f in range(2):
                pe.wait_ge(S["v_gw"], f + 1)
                if f == 0:
                    pe.wait_ge(S["a_q"], 4)
                for t in range(HALF):
                    mm = pe.transpose((b0, b1)[f][0:GROUPS, tok(t)], gw[:, f * HALF + t, :], ident)
                mm.then_inc(S["pe_gwT"], 1)
            for f in range(2):
                pe.wait_ge(S["a_gwT"], f + 1)
                for t in range(HALF):
                    T = f * HALF + t
                    mm = pe.matmul((b6, b5)[f][:, tok(t)], gwT[:, tok(T)], gwT[:, tok(T)], start=True, stop=True)
                mm.then_inc(S["pe_gw"], 1)

            def attended(T):
                return o_ps[T // HALF][T % HALF // 2][:, (T % 2) * 256:(T % 2) * 256 + D]

            for f in range(2):
                pe.wait_ge(S["v_gwm"], f + 1)
                pe.wait_ge(S["a_vp"], 2)
                pe.wait_ge(S["a_vps"], f + 1)
                for T in range(f * HALF, (f + 1) * HALF):
                    pe.matmul(attended(T), gwm[:, T, :], vps[:, T, :], start=(T % 2 == 0), stop=False,
                              skip_group_check=True)
            for f in range(2):
                pe.wait_ge(S["v_A"], f + 1)
                for t in range(HALF):
                    mm = pe.transpose((b0, b1)[f][:, tok(t)], Aw[:, f * HALF + t, :], ident)
                mm.then_inc(S["pe_AT"], 1)
                pe.wait_ge(S["a_AT"], f + 1)
                pe.wait_ge(S["a_vp"], 2)
                for t in range(HALF):
                    T = f * HALF + t
                    mm = pe.matmul(attended(T), AT[:, T, :], vp[:, T, :], start=False, stop=True,
                                   skip_group_check=True)
                mm.then_inc(S["pe_o"], 1)
            pe.wait_ge(S["s_gate"], 32)

            def gate_logits(tiles):
                for T in tiles:
                    t, dst = T % HALF, gate_ps[T // HALF]
                    pe.matmul(dst[:, t * 16:t * 16 + E + 1], hnTa[:, tok(T)], wgate[:, :], start=True, stop=False)
                    mm = pe.matmul(dst[:, t * 16:t * 16 + E + 1], hnTb[:, tok(T)], wgateb[:, :], start=False,
                                   stop=True)
                return mm

            turn_rows(0, 3, b0).then_inc(S["pe_h2T"], 1)
            pe.wait_ge(S["a_hT"], 1)
            pe.wait_ge(S["v_hT"], 1)
            gate_logits(range(2))
            turn_rows(1, 4, b1).then_inc(S["pe_h2T"], 1)
            gate_logits(range(2, HALF)).then_inc(S["pe_gate"], 1)
            pe.wait_ge(S["a_hT"], 2)
            pe.wait_ge(S["v_hT"], 2)
            gate_logits(range(HALF, TILES)).then_inc(S["pe_gate"], 1)
            pe.wait_ge(S["v_v"], 1)
            pe.transpose(b4[0:TILES, 0:P], vcl[:, :], ident).then_inc(S["pe_vT"], 1)
            pe.wait_ge(S["v_M"], 1)
            mo = M[:, :, :].rearrange("p t e -> p e t")
            pe.matmul(b5[:, 0:E * TILES], ones, mo, start=True, stop=True)
            pe.matmul(b5[:, 256:256 + E * TILES], cst[:, C_TRI:C_TRI + P], mo, start=True,
                      stop=True).then_inc(S["pe_rank"], 1)
            pe.wait_ge(S["v_tabr"], 1)
            pe.wait_ge(S["a_tabr"], 1)
            pe.wait_ge(S["p_tabr"], 1)
            JT = TOP * TILES
            for r in range(JT):
                mm = pe.matmul(b2k[:, 0:2 * BCOLS], ohoff[:, r, :], tabr[:, r, :, :].rearrange("p a b -> p (a b)"),
                               start=(r == 0), stop=(r == JT - 1))
            mm.then_inc(S["pe_tab"], 1)
            pe.wait_ge(S["v_comb"], 1)
            for f in range(2):
                for t in range(HALF):
                    mm = pe.transpose((b5, b6)[f][0:E, tok(t)], comb[:, f * HALF + t, :], ident)
                mm.then_inc(S["pe_combT"], 1)
            pe.wait_ge(S["p_lo"], 2 * E)
            pe.wait_ge(S["d_bias"], 32)
            pe.wait_ge(S["s_w2"], 16 * E)
            pe.wait_ge(S["v_emap"], 1)
            n = pe.value_load(nblk[0:1, 0:1], min_val=TOP * TOKENS // P, max_val=BLOCKS)

            def expert(b):
                return pe.value_load(emap[0:1, bass.ds(b, 1)], min_val=0, max_val=E - 1)

            first = expert(0)
            last_expert = pe.alloc_register("last_expert")
            pe.reg_mov(last_expert, first)

            def turn_x(rows):
                pe.transpose(b7[:, 0:P], rows[:, 0:LO], ident)
                pe.transpose(b7[0:HI, P:2 * P], rows[:, LO:D], ident).then_inc(S["pe_xT"], 1)

            def up(part, e, b):
                dst = (b0, b1)[part][:, 0:FH]
                fs = slice(part * FH, (part + 1) * FH)
                pe.matmul(dst, xah[:, :], w1ah[:, bass.ds(e, 1), fs], start=True, stop=False)
                pe.matmul(dst, xah[:, :], w1al[:, bass.ds(e, 1), fs], start=False, stop=False)
                pe.matmul(dst, xbh[0:HI + 2, :], w1bl[:, bass.ds(e, 1), fs], start=False, stop=False)
                if part == 0:
                    pe.wait_ge(S["v_xl"], b + 1)
                pe.matmul(dst, xal[:, :], w1ah[:, bass.ds(e, 1), fs], start=False, stop=False)
                pe.matmul(dst, xbb[:, :], w1bh[:, bass.ds(e, 1), fs], start=False,
                          stop=True).then_inc(S[f"pe_up{part}"], 1)

            def turn_h():
                for c in range(FC):
                    part = c // 3
                    mm = pe.transpose((b2k, b3)[part][:, (c % 3) * P:(c % 3 + 1) * P], hg[:, c * P:(c + 1) * P],
                                      ident)
                    if c % 3 == 2:
                        mm.then_inc(S["pe_hgT"], 1)

            def down(e):
                for c in range(FC):
                    mm = pe.matmul(b4[:, 0:D], hT[:, c, :], w2s[:, bass.ds(e * FC + c, 1), :], start=(c == 0),
                                   stop=(c == FC - 1))
                mm.then_inc(S["pe_y"], 1)

            pe.wait_ge(S["d_first"], 16)
            pe.wait_ge(S["a_vT"], 1)
            turn_x(xg_first)
            pe.wait_ge(S["a_xh"], 3)
            up(0, first, 0)
            up(1, first, 0)
            pe.wait_ge(S["d_gather"], 16)
            turn_x(xg)
            pe.wait_ge(S["p_cw"], 8)
            for r in range(JT):
                mm = pe.matmul(b4[:, 0:3 * BCOLS], ohoff[:, r, :], wtab[:, r, :, :].rearrange("p a b -> p (a b)"),
                               start=(r == 0), stop=(r == JT - 1))
            mm.then_inc(S["pe_wtab"], 1)
            with pe.Fori(1, n) as i:
                e_down = pe.snap(last_expert, min_val=0, max_val=E - 1)
                e_up = expert(i)
                pe.reg_mov(last_expert, e_up)
                pe.wait_ge(S["a_xh"], i * 3 + 3)
                up(0, e_up, i)
                pe.wait_ge(S["a_ge"], i * 2)
                pe.wait_ge(S["v_tab"], 1)
                turn_h()
                up(1, e_up, i)
                pe.wait_ge(S["d_gather"], i * 16 + 16)
                turn_x(xg)
                pe.wait_ge(S["v_hgT"], i * 2)
                pe.wait_ge(S["v_wslot"], 1)
                down(e_down)
            pe.wait_ge(S["a_ge"], n * 2)
            turn_h()
            pe.wait_ge(S["v_hgT"], n * 2)
            down(pe.snap(last_expert, min_val=0, max_val=E - 1))
            pe.wait_ge(S["a_combT"], 2)
            pe.wait_ge(S["v_sw"], 1)
            pe.wait_ge(S["d_feat"], 32)
            for t in range(TILES):
                dst = (b0, b1, b5, b6)[t // 2].rearrange("p (b n) -> p b n", b=2)[:, t % 2, 0:D]
                mm = pe.matmul(dst, rows_last[:, tok(t)], last_w[:, :], start=True, stop=True)
                if t % 2:
                    mm.then_inc(S["pe_base"], 1)


def constants():
    import numpy as np
    c = np.zeros((P, C_ALL), np.float32)
    p = np.arange(P)
    c[:, C_ID:C_ID + P] = np.eye(P)
    c[:, C_DIAG:C_DIAG + P] = p[:, None] // PLACES == p[None, :] // PLACES
    c[:, C_TRI:C_TRI + P] = p[:, None] < p[None, :]
    c[:, C_ONE:C_ONE + P] = 1
    c[:, C_EXP:C_EXP + E] = np.arange(E)
    c[:, C_THR:C_THR + E] = np.arange(E) * P
    c[:, C_RESET:C_RESET + E * TILES] = np.arange(E * TILES) % TILES != 0
    c[:, C_BLK:C_BLK + BCOLS] = np.arange(BCOLS)
    c[:, C_BLK128:C_BLK128 + BCOLS] = np.arange(BCOLS) * P
    c[:, C_TILE:C_TILE + TOP * TILES] = np.arange(TOP * TILES)
    c[:, C_PART] = p + 1
    c[:, C_OFF:C_OFF + P] = p
    return c


def times_read():
    import numpy as np
    c = np.zeros((P, CHUNKS), np.float32)
    u = np.arange(16)
    side = (u < 15).astype(np.float32) + (u > 0)
    times = np.broadcast_to((1 + side[:, None] + side[None, :])[:, :, None], (16, 16, 3)).reshape(INNER, P)
    c[:, :INNER] = times.T
    c[:EDGE, INNER:] = 1
    return c


def lay_pixels(x):
    import numpy as np
    x = np.asarray(x)
    padded = np.pad(x, ((0, 0), (0, 0), (1, 1), (1, 1)))
    a = np.zeros((CHUNKS, P, TOKENS), x.dtype)
    a[:INNER] = x.reshape(64, 3, 4, 16, 4, 16).transpose(3, 5, 1, 0, 2, 4).reshape(INNER, P, TOKENS)
    inner = padded[:, :, 1:65, 1:65]
    rows = lambda z: z.reshape(64, 3, 4, 16, 4).transpose(3, 1, 0, 2, 4).reshape(48, TOKENS)
    colm = lambda z: z.reshape(64, 3, 4, 4, 16).transpose(4, 1, 0, 2, 3).reshape(48, TOKENS)
    left = rows(padded[:, :, 1:65, 0:64:16])
    right = rows(padded[:, :, 1:65, 17:66:16])
    above = colm(padded[:, :, 0:64:16, 1:65])
    below = colm(padded[:, :, 17:66:16, 1:65])
    a[INNER, :EDGE] = np.concatenate([left, right])
    a[INNER + 1, :EDGE] = np.concatenate([above, below])
    return a


def lay_rows(w):
    import numpy as np
    w = np.asarray(w)
    w = w.reshape(16, 16, SHIFTS, 3, -1)
    n = w.shape[-1]
    a = np.zeros((16, 16, 3, SHIFTS, n), w.dtype)
    a[:, :, :, 0] = w[:, :, 0]
    a[:, :15, :, 1] = w[:, 1:, 1]
    a[:, 1:, :, 2] = w[:, :15, 2]
    a[:15, :, :, 3] = w[1:, :, 3]
    a[1:, :, :, 4] = w[:15, :, 4]
    edge = np.stack([w[:, 0, 1], w[:, 15, 2], w[0, :, 3], w[15, :, 4]]).reshape(2, EDGE, n)
    return a.reshape(INNER, P, SHIFTS, n), edge


def kernel(**inputs):
    import numpy as _np
    import concourse.bacc as _bacc
    from concourse import mybir as _mybir
    from concourse.bass_utils import run_bass_kernel_spmd as _run

    g = {k: _np.asarray(v) for k, v in inputs.items()}
    w_in, w_edge = lay_rows(g["L0_tok_W"])

    def vec(v):
        a, b = lay_rows(v)
        full = _np.zeros((CHUNKS, P, SHIFTS), v.dtype)
        full[:INNER] = a[..., 0]
        full[INNER:, :EDGE, 0] = b[..., 0]
        return full.transpose(1, 0, 2)

    qkv = _np.concatenate([g["L0_attn_W_qkv"], g["L0_attn_b_qkv"][None]])
    qkv = _np.concatenate([qkv[:, 0:LO], qkv[:, D:D + LO], qkv[:, LO:D], qkv[:, D + LO:]], 1)
    wpg = _np.concatenate([g["L0_attn_W_proj"], g["L0_attn_W_gp"]], 1)
    gate = _np.concatenate([_np.concatenate([g["L0_ffn_gate_w"], g["L0_ffn_v_w"][:, None]], 1),
                            _np.concatenate([g["L0_ffn_gate_b"], g["L0_ffn_v_b"].reshape(1)])[None]])
    spec = _np.concatenate([g["L0_ffn_out_w"], g["L0_ffn_out_b"][None]])
    laid = {
        "pixels": lay_pixels(g["x"]), "mult_w": w_in, "edge_w": w_edge,
        "gammas_betas": _np.concatenate([vec(g["L0_tok_gamma"]).reshape(P, -1), vec(g["L0_tok_beta"]).reshape(P, -1),
                                         times_read()], 1),
        "tok_b": g["L0_tok_b"], "wqkv": qkv, "wpg": wpg,
        "b_proj": g["L0_attn_b_proj"], "alpha": g["L0_attn_alpha"].reshape(1), "gate": gate, "w1": g["L0_ffn_w1"],
        "bias1": g["L0_ffn_b1"].reshape(BR, E * F // BR),
        "w2": g["L0_ffn_w2"], "b2": g["L0_ffn_b2"], "spec_w": spec, "bk": g["L0_ffn_bk_scale"], "consts": constants(),
    }
    nc = _bacc.Bacc("TRN2", target_bir_lowering=False, num_devices=1)
    arrays, args = {}, []
    for name, a in laid.items():
        a = _np.ascontiguousarray(a)
        arrays[f"in_{name}_dram"] = a
        args.append(nc.dram_tensor(f"in_{name}_dram", a.shape, _mybir.dt.from_np(a.dtype), kind="ExternalInput").ap())
    args.append(nc.dram_tensor("out_0_dram", (TOKENS, D), _mybir.dt.float32, kind="ExternalOutput").ap())
    tower(nc, *args)
    r = _run(nc, [arrays], core_ids=[0])
    return r.results[0]["out_0_dram"].reshape(IMAGES, PLACES, D)
```
